# Optimizing a Trainium2 kernel written in Bass

```python
import numpy as np
import jax
import jax.numpy as jnp

def _softmax(x, axis=-1):
    return jax.nn.softmax(x, axis=axis)

def _gelu(x):
    return jax.nn.gelu(x, approximate=True)

def _silu(x):
    return jax.nn.silu(x)

def _sigmoid(x):
    return jax.nn.sigmoid(x)

def _layernorm(x, axis=-1, eps=1e-05):
    m = jnp.mean(x, axis=axis, keepdims=True)
    v = jnp.var(x, axis=axis, keepdims=True)
    return (x - m) / jnp.sqrt(v + eps)

def _scatter_add(tgt, idx, src, axis=0):
    return tgt.at[idx].add(src)

def _segment_sum(src, seg, n):
    return jax.ops.segment_sum(src, seg, n)
kernel_name = 'mk_conv_attn_hybrid_d4_conv_nchw256_r2_aa7cbd'

def setup_inputs(seed: int=0):
    np.random.seed(seed)
    _w = jnp.asarray

    def _rec_inputs():
        import jax
        import jax.numpy as jnp
        _gk = jax.random.key(seed)
        x = -0.0002928 + 1 * jax.random.normal(jax.random.fold_in(_gk, 1), (4, 128, 32, 32), jnp.float32)
        return x
    x = _rec_inputs()

    def _L0_conv_setup():
        import jax, jax.numpy as jnp
        import numpy as np
        GROUPS = 8
        EPS = 1e-05

        def _group_norm(x, gamma, beta):
            B, C, H, W = x.shape
            g = x.reshape(B, GROUPS, C // GROUPS, H, W)
            mean = g.mean(axis=(2, 3, 4), keepdims=True)
            var = g.var(axis=(2, 3, 4), keepdims=True)
            g = (g - mean) * jax.lax.rsqrt(var + EPS)
            g = g.reshape(B, C, H, W)
            return g * gamma[None, :, None, None] + beta[None, :, None, None]
        key = jax.random.key(seed)
        ks = jax.random.split(key, 7)
        B, C, H, W = (4, 128, 32, 32)
        x = jax.random.normal(ks[0], (B, C, H, W), dtype=jnp.float32)
        gn_gamma = jnp.ones((C,), dtype=jnp.float32)
        gn_beta = jnp.zeros((C,), dtype=jnp.float32)
        qkv_w = jax.random.normal(ks[1], (3 * C, C), dtype=jnp.float32) * C ** (-0.5)
        qkv_b = jax.random.normal(ks[2], (3 * C,), dtype=jnp.float32) * 0.01
        proj_w = jax.random.normal(ks[3], (C, C), dtype=jnp.float32) * C ** (-0.5)
        proj_b = jax.random.normal(ks[4], (C,), dtype=jnp.float32) * 0.01
        return {'x': x, 'gn_gamma': gn_gamma, 'gn_beta': gn_beta, 'qkv_w': qkv_w, 'qkv_b': qkv_b, 'proj_w': proj_w, 'proj_b': proj_b}
    _L0_conv_all = _L0_conv_setup()
    _L0_conv_in = {k: v for k, v in _L0_conv_all.items() if k in ('gn_gamma', 'gn_beta', 'qkv_w', 'qkv_b', 'proj_w', 'proj_b')}
    del _L0_conv_all

    def _L1_conv_setup():
        import jax, jax.numpy as jnp
        import numpy as np
        KSIZE = 5
        PAD = 2
        DILATE = 1
        STRIDE = 1
        NHEADS = 8

        def extract_patches(x, ksize=KSIZE, pad=PAD, dilate=DILATE, stride=STRIDE):
            N, D, H, W = x.shape
            xp = jnp.pad(x, ((0, 0), (0, 0), (pad, pad), (pad, pad)))
            Ho = (H + 2 * pad - dilate * (ksize - 1) - 1) // stride + 1
            Wo = (W + 2 * pad - dilate * (ksize - 1) - 1) // stride + 1
            slices = []
            for i in range(ksize):
                for j in range(ksize):
                    r0, c0 = (i * dilate, j * dilate)
                    slices.append(xp[:, :, r0:r0 + (Ho - 1) * stride + 1:stride, c0:c0 + (Wo - 1) * stride + 1:stride])
            return jnp.stack(slices, axis=2)
        key = jax.random.key(seed)
        k1, k2 = jax.random.split(key)
        N, D, H, W = (8, 128, 56, 56)
        outC = 128
        x = jax.random.normal(k1, (N, D, H, W), dtype=jnp.float32)
        w_out = jax.random.normal(k2, (outC, D), dtype=jnp.float32) * (1.0 / np.sqrt(D))
        b_out = jnp.zeros((outC,), dtype=jnp.float32)
        return {'x': x, 'w_out': w_out, 'b_out': b_out}
    _L1_conv_all = _L1_conv_setup()
    _L1_conv_in = {k: v for k, v in _L1_conv_all.items() if k in ('w_out', 'b_out')}
    del _L1_conv_all

    def _L2_attn_setup():
        import jax, jax.numpy as jnp
        import numpy as np
        HEADS = 8
        DIM_HEAD = 32
        EPS = 1e-05

        def _inst_norm(t):
            mu = jnp.mean(t, axis=-1, keepdims=True)
            var = jnp.var(t, axis=-1, keepdims=True)
            return (t - mu) / jnp.sqrt(var + EPS)
        key = jax.random.key(seed)
        k1, k2, k3, k4 = jax.random.split(key, 4)
        b, n, dim = (4, 4096, 128)
        inner = HEADS * DIM_HEAD
        x = jax.random.normal(k1, (b, n, dim), dtype=jnp.float32)
        w_qkv = jax.random.normal(k2, (dim, 3 * inner), dtype=jnp.float32) * (1.0 / DIM_HEAD)
        w_out = jax.random.normal(k3, (inner, dim), dtype=jnp.float32) * dim ** (-0.5)
        b_out = jax.random.normal(k4, (dim,), dtype=jnp.float32) * 0.01
        return {'x': x, 'w_qkv': w_qkv, 'w_out': w_out, 'b_out': b_out}
    _L2_attn_all = _L2_attn_setup()
    _L2_attn_in = {k: v for k, v in _L2_attn_all.items() if k in ('w_qkv', 'w_out', 'b_out')}
    del _L2_attn_all

    def _L2_ffn_setup():
        import jax, jax.numpy as jnp
        import numpy as np
        BN_EPS = 0.001

        def _bn(h, g, b, m, v):
            return g * (h - m) * jax.lax.rsqrt(v + BN_EPS) + b
        key = jax.random.key(seed)
        ks = jax.random.split(key, 8)
        B, F, Df = (128, 32, 128)
        E, H, D = (8, 128, 128)
        s1 = 1.0 / np.sqrt(Df)
        s2 = 1.0 / np.sqrt(H)
        return {'x': jax.random.normal(ks[0], (B, F, Df), jnp.float32), 'Wr': jax.random.normal(ks[1], (Df, E), jnp.float32) * s1, 'br': jnp.zeros((E,), jnp.float32), 'W1': jax.random.normal(ks[2], (E, Df, H), jnp.float32) * s1, 'b1': jnp.zeros((E, H), jnp.float32), 'g1': jnp.ones((E, H), jnp.float32), 'be1': jnp.zeros((E, H), jnp.float32), 'm1': jnp.zeros((E, H), jnp.float32), 'v1': jnp.ones((E, H), jnp.float32), 'W2': jax.random.normal(ks[3], (E, H, H), jnp.float32) * s2, 'b2': jnp.zeros((E, H), jnp.float32), 'g2': jnp.ones((E, H), jnp.float32), 'be2': jnp.zeros((E, H), jnp.float32), 'm2': jnp.zeros((E, H), jnp.float32), 'v2': jnp.ones((E, H), jnp.float32), 'Wo': jax.random.normal(ks[4], (E, H, D), jnp.float32) * s2, 'bo': jnp.zeros((E, D), jnp.float32)}
    _L2_ffn_all = _L2_ffn_setup()
    _L2_ffn_in = {k: v for k, v in _L2_ffn_all.items() if k in ('Wr', 'br', 'W1', 'b1', 'g1', 'be1', 'm1', 'v1', 'W2', 'b2', 'g2', 'be2', 'm2', 'v2', 'Wo', 'bo')}
    del _L2_ffn_all

    def _L3_attn_setup():
        import jax, jax.numpy as jnp
        import numpy as np
        DIM = 128
        H_GLOBAL = 8
        H_LOCAL = 4
        WINDOW = 5
        HALF = WINDOW // 2
        B, S = (4, 1024)
        EPS = 1e-05

        def layer_norm(x, g, b):
            mu = jnp.mean(x, axis=-1, keepdims=True)
            var = jnp.mean(jnp.square(x - mu), axis=-1, keepdims=True)
            return (x - mu) * jax.lax.rsqrt(var + EPS) * g + b

        def qkv_proj(x, in_w, in_b):
            qkv = x @ in_w.T + in_b
            return jnp.split(qkv, 3, axis=-1)

        def global_mha(x, in_w, in_b, out_w, out_b, nh):
            Bq, Sq, D = x.shape
            hd = D // nh
            q, k, v = qkv_proj(x, in_w, in_b)
            q = q.reshape(Bq, Sq, nh, hd)
            k = k.reshape(Bq, Sq, nh, hd)
            v = v.reshape(Bq, Sq, nh, hd)
            scores = jnp.einsum('bqhd,bkhd->bhqk', q, k) / np.sqrt(hd).astype(np.float32)
            attn = jax.nn.softmax(scores, axis=-1)
            o = jnp.einsum('bhqk,bkhd->bqhd', attn, v).reshape(Bq, Sq, D)
            return o @ out_w.T + out_b

        def local_mha(x, in_w, in_b, out_w, out_b, nh):
            Bq, Sq, D = x.shape
            hd = D // nh
            q, k, v = qkv_proj(x, in_w, in_b)
            kp = jnp.pad(k, ((0, 0), (HALF, HALF), (0, 0)))
            vp = jnp.pad(v, ((0, 0), (HALF, HALF), (0, 0)))
            k_win = jnp.stack([kp[:, j:j + Sq] for j in range(WINDOW)], axis=2)
            v_win = jnp.stack([vp[:, j:j + Sq] for j in range(WINDOW)], axis=2)
            q = q.reshape(Bq, Sq, nh, hd)
            k_win = k_win.reshape(Bq, Sq, WINDOW, nh, hd)
            v_win = v_win.reshape(Bq, Sq, WINDOW, nh, hd)
            scores = jnp.einsum('bshd,bswhd->bshw', q, k_win) / np.sqrt(hd).astype(np.float32)
            idx = jnp.arange(Sq)[:, None] + jnp.arange(-HALF, HALF + 1)[None, :]
            valid = (idx >= 0) & (idx < Sq)
            scores = jnp.where(valid[None, :, None, :], scores, -jnp.inf)
            attn = jax.nn.softmax(scores, axis=-1)
            o = jnp.einsum('bshw,bswhd->bshd', attn, v_win).reshape(Bq, Sq, D)
            return o @ out_w.T + out_b
        key = jax.random.key(seed)
        ks = jax.random.split(key, 8)
        sc = 0.02
        d = DIM
        return {'x': jax.random.normal(ks[0], (B, S, d), jnp.float32), 'g_in_w': jax.random.normal(ks[1], (3 * d, d), jnp.float32) * sc, 'g_in_b': jnp.zeros((3 * d,), jnp.float32), 'g_out_w': jax.random.normal(ks[2], (d, d), jnp.float32) * sc, 'g_out_b': jnp.zeros((d,), jnp.float32), 't_in_w': jax.random.normal(ks[3], (3 * d, d), jnp.float32) * sc, 't_in_b': jnp.zeros((3 * d,), jnp.float32), 't_out_w': jax.random.normal(ks[4], (d, d), jnp.float32) * sc, 't_out_b': jnp.zeros((d,), jnp.float32), 'fus_w1': jax.random.normal(ks[5], (2 * d, 2 * d), jnp.float32) * sc, 'fus_b1': jnp.zeros((2 * d,), jnp.float32), 'fus_w2': jax.random.normal(ks[6], (d, 2 * d), jnp.float32) * sc, 'fus_b2': jnp.zeros((d,), jnp.float32), 'ffn_w1': jax.random.normal(ks[7], (2 * d, d), jnp.float32) * sc, 'ffn_b1': jnp.zeros((2 * d,), jnp.float32), 'ffn_w2': jax.random.normal(jax.random.fold_in(key, 9), (d, 2 * d), jnp.float32) * sc, 'ffn_b2': jnp.zeros((d,), jnp.float32), 'gn_g': jnp.ones((d,), jnp.float32), 'gn_b': jnp.zeros((d,), jnp.float32), 'fn_g': jnp.ones((d,), jnp.float32), 'fn_b': jnp.zeros((d,), jnp.float32)}
    _L3_attn_all = _L3_attn_setup()
    _L3_attn_in = {k: v for k, v in _L3_attn_all.items() if k in ('g_in_w', 'g_in_b', 'g_out_w', 'g_out_b', 't_in_w', 't_in_b', 't_out_w', 't_out_b', 'fus_w1', 'fus_b1', 'fus_w2', 'fus_b2', 'ffn_w1', 'ffn_b1', 'ffn_w2', 'ffn_b2', 'gn_g', 'gn_b', 'fn_g', 'fn_b')}
    del _L3_attn_all

    def _L3_ffn_setup():
        import jax, jax.numpy as jnp
        import numpy as np
        B, N, D = (16, 2048, 128)
        NUM_EXPERTS, TOP_K, HEADS = (4, 2, 4)
        N_EDGES = 524288
        LN_EPS = 1e-05

        def _layernorm(x, g, b):
            mu = x.mean(-1, keepdims=True)
            var = ((x - mu) ** 2).mean(-1, keepdims=True)
            return (x - mu) * jax.lax.rsqrt(var + LN_EPS) * g + b

        def _forward(x, edge_index, W_gat, att_src, att_dst, b_gat, ln_gamma, ln_beta, W1, b1, W2, b2):
            Bc, Nc, Dc = x.shape
            M = Bc * Nc
            x_flat = x.reshape(M, Dc)
            h = (x_flat @ W_gat).reshape(M, HEADS, NUM_EXPERTS)
            loops = jnp.arange(M, dtype=edge_index.dtype)
            src = jnp.concatenate([edge_index[0], loops])
            dst = jnp.concatenate([edge_index[1], loops])
            a_src = (h * att_src).sum(-1)
            a_dst = (h * att_dst).sum(-1)
            e = jax.nn.leaky_relu(a_src[src] + a_dst[dst], negative_slope=0.2)
            e_max = jax.ops.segment_max(e, dst, num_segments=M)
            ee = jnp.exp(e - e_max[dst])
            denom = jax.ops.segment_sum(ee, dst, num_segments=M)
            alpha = ee / (denom[dst] + 1e-16)
            msg = h[src] * alpha[:, :, None]
            agg = jax.ops.segment_sum(msg, dst, num_segments=M).reshape(M, HEADS * NUM_EXPERTS) + b_gat
            scores = _layernorm(agg, ln_gamma, ln_beta).reshape(M, HEADS, NUM_EXPERTS).mean(1)
            scores = scores.reshape(Bc, Nc, NUM_EXPERTS)
            topk_s, topk_i = jax.lax.top_k(scores, TOP_K)
            w = jax.nn.softmax(topk_s, axis=-1)
            out = jnp.zeros_like(x)
            for ei in range(NUM_EXPERTS):
                g = jnp.where(topk_i == ei, w, 0.0).sum(-1)
                hh = jax.nn.gelu(x @ W1[ei] + b1[ei], approximate=False)
                out = out + g[..., None] * (hh @ W2[ei] + b2[ei])
            return out
        key = jax.random.key(seed)
        ks = jax.random.split(key, 8)
        s = 0.05
        return {'x': jax.random.normal(ks[0], (B, N, D), jnp.float32), 'W_gat': jax.random.normal(ks[1], (D, HEADS * NUM_EXPERTS), jnp.float32) * s, 'att_src': jax.random.normal(ks[2], (HEADS, NUM_EXPERTS), jnp.float32) * s, 'att_dst': jax.random.normal(ks[3], (HEADS, NUM_EXPERTS), jnp.float32) * s, 'b_gat': jnp.zeros((HEADS * NUM_EXPERTS,), jnp.float32), 'ln_gamma': jnp.ones((HEADS * NUM_EXPERTS,), jnp.float32), 'ln_beta': jnp.zeros((HEADS * NUM_EXPERTS,), jnp.float32), 'W1': jax.random.normal(ks[4], (NUM_EXPERTS, D, 2 * D), jnp.float32) * s, 'b1': jnp.zeros((NUM_EXPERTS, 2 * D), jnp.float32), 'W2': jax.random.normal(ks[5], (NUM_EXPERTS, 2 * D, D), jnp.float32) * s, 'b2': jnp.zeros((NUM_EXPERTS, D), jnp.float32), 'edge_index': jax.random.randint(ks[6], (2, N_EDGES), 0, B * N, jnp.int32)}
    _L3_ffn_all = _L3_ffn_setup()
    _L3_ffn_in = {k: v for k, v in _L3_ffn_all.items() if k in ('W_gat', 'att_src', 'att_dst', 'b_gat', 'ln_gamma', 'ln_beta', 'W1', 'b1', 'W2', 'b2', 'edge_index')}
    del _L3_ffn_all
    return {'x': x, 'L0_conv_gn_gamma': _L0_conv_in['gn_gamma'], 'L0_conv_gn_beta': _L0_conv_in['gn_beta'], 'L0_conv_qkv_w': _L0_conv_in['qkv_w'], 'L0_conv_qkv_b': _L0_conv_in['qkv_b'], 'L0_conv_proj_w': _L0_conv_in['proj_w'], 'L0_conv_proj_b': _L0_conv_in['proj_b'], 'L1_conv_w_out': _L1_conv_in['w_out'], 'L1_conv_b_out': _L1_conv_in['b_out'], 'L2_attn_w_qkv': _L2_attn_in['w_qkv'], 'L2_attn_w_out': _L2_attn_in['w_out'], 'L2_attn_b_out': _L2_attn_in['b_out'], 'L2_ffn_Wr': _L2_ffn_in['Wr'], 'L2_ffn_br': _L2_ffn_in['br'], 'L2_ffn_W1': _L2_ffn_in['W1'], 'L2_ffn_b1': _L2_ffn_in['b1'], 'L2_ffn_g1': _L2_ffn_in['g1'], 'L2_ffn_be1': _L2_ffn_in['be1'], 'L2_ffn_m1': _L2_ffn_in['m1'], 'L2_ffn_v1': _L2_ffn_in['v1'], 'L2_ffn_W2': _L2_ffn_in['W2'], 'L2_ffn_b2': _L2_ffn_in['b2'], 'L2_ffn_g2': _L2_ffn_in['g2'], 'L2_ffn_be2': _L2_ffn_in['be2'], 'L2_ffn_m2': _L2_ffn_in['m2'], 'L2_ffn_v2': _L2_ffn_in['v2'], 'L2_ffn_Wo': _L2_ffn_in['Wo'], 'L2_ffn_bo': _L2_ffn_in['bo'], 'L3_attn_g_in_w': _L3_attn_in['g_in_w'], 'L3_attn_g_in_b': _L3_attn_in['g_in_b'], 'L3_attn_g_out_w': _L3_attn_in['g_out_w'], 'L3_attn_g_out_b': _L3_attn_in['g_out_b'], 'L3_attn_t_in_w': _L3_attn_in['t_in_w'], 'L3_attn_t_in_b': _L3_attn_in['t_in_b'], 'L3_attn_t_out_w': _L3_attn_in['t_out_w'], 'L3_attn_t_out_b': _L3_attn_in['t_out_b'], 'L3_attn_fus_w1': _L3_attn_in['fus_w1'], 'L3_attn_fus_b1': _L3_attn_in['fus_b1'], 'L3_attn_fus_w2': _L3_attn_in['fus_w2'], 'L3_attn_fus_b2': _L3_attn_in['fus_b2'], 'L3_attn_ffn_w1': _L3_attn_in['ffn_w1'], 'L3_attn_ffn_b1': _L3_attn_in['ffn_b1'], 'L3_attn_ffn_w2': _L3_attn_in['ffn_w2'], 'L3_attn_ffn_b2': _L3_attn_in['ffn_b2'], 'L3_attn_gn_g': _L3_attn_in['gn_g'], 'L3_attn_gn_b': _L3_attn_in['gn_b'], 'L3_attn_fn_g': _L3_attn_in['fn_g'], 'L3_attn_fn_b': _L3_attn_in['fn_b'], 'L3_ffn_W_gat': _L3_ffn_in['W_gat'], 'L3_ffn_att_src': _L3_ffn_in['att_src'], 'L3_ffn_att_dst': _L3_ffn_in['att_dst'], 'L3_ffn_b_gat': _L3_ffn_in['b_gat'], 'L3_ffn_ln_gamma': _L3_ffn_in['ln_gamma'], 'L3_ffn_ln_beta': _L3_ffn_in['ln_beta'], 'L3_ffn_W1': _L3_ffn_in['W1'], 'L3_ffn_b1': _L3_ffn_in['b1'], 'L3_ffn_W2': _L3_ffn_in['W2'], 'L3_ffn_b2': _L3_ffn_in['b2'], 'L3_ffn_edge_index': _L3_ffn_in['edge_index']}

def reference(x, L0_conv_gn_gamma, L0_conv_gn_beta, L0_conv_qkv_w, L0_conv_qkv_b, L0_conv_proj_w, L0_conv_proj_b, L1_conv_w_out, L1_conv_b_out, L2_attn_w_qkv, L2_attn_w_out, L2_attn_b_out, L2_ffn_Wr, L2_ffn_br, L2_ffn_W1, L2_ffn_b1, L2_ffn_g1, L2_ffn_be1, L2_ffn_m1, L2_ffn_v1, L2_ffn_W2, L2_ffn_b2, L2_ffn_g2, L2_ffn_be2, L2_ffn_m2, L2_ffn_v2, L2_ffn_Wo, L2_ffn_bo, L3_attn_g_in_w, L3_attn_g_in_b, L3_attn_g_out_w, L3_attn_g_out_b, L3_attn_t_in_w, L3_attn_t_in_b, L3_attn_t_out_w, L3_attn_t_out_b, L3_attn_fus_w1, L3_attn_fus_b1, L3_attn_fus_w2, L3_attn_fus_b2, L3_attn_ffn_w1, L3_attn_ffn_b1, L3_attn_ffn_w2, L3_attn_ffn_b2, L3_attn_gn_g, L3_attn_gn_b, L3_attn_fn_g, L3_attn_fn_b, L3_ffn_W_gat, L3_ffn_att_src, L3_ffn_att_dst, L3_ffn_b_gat, L3_ffn_ln_gamma, L3_ffn_ln_beta, L3_ffn_W1, L3_ffn_b1, L3_ffn_W2, L3_ffn_b2, L3_ffn_edge_index):
    import jax
    import jax.numpy as jnp

    def _L0_conv_ref(x, gn_gamma, gn_beta, qkv_w, qkv_b, proj_w, proj_b):
        import jax, jax.numpy as jnp
        import numpy as np
        GROUPS = 8
        EPS = 1e-05

        def _group_norm(x, gamma, beta):
            B, C, H, W = x.shape
            g = x.reshape(B, GROUPS, C // GROUPS, H, W)
            mean = g.mean(axis=(2, 3, 4), keepdims=True)
            var = g.var(axis=(2, 3, 4), keepdims=True)
            g = (g - mean) * jax.lax.rsqrt(var + EPS)
            g = g.reshape(B, C, H, W)
            return g * gamma[None, :, None, None] + beta[None, :, None, None]
        B, C, H, W = x.shape
        num_heads = 4
        head_dim = C // num_heads
        scale = head_dim ** (-0.5)
        N = H * W
        h = _group_norm(x, gn_gamma, gn_beta)
        qkv = jnp.einsum('oc,bchw->bohw', qkv_w, h) + qkv_b[None, :, None, None]
        q, k, v = jnp.split(qkv, 3, axis=1)
        q = q.reshape(B, num_heads, head_dim, N)
        k = k.reshape(B, num_heads, head_dim, N)
        v = v.reshape(B, num_heads, head_dim, N)
        attn = jax.nn.softmax(jnp.einsum('bhdn,bhdm->bhnm', q, k) * scale, axis=-1)
        out = jnp.einsum('bhnm,bhdm->bhdn', attn, v).reshape(B, C, H, W)
        return x + jnp.einsum('oc,bchw->bohw', proj_w, out) + proj_b[None, :, None, None]

    def _L1_conv_ref(x, w_out, b_out):
        import jax, jax.numpy as jnp
        import numpy as np
        KSIZE = 5
        PAD = 2
        DILATE = 1
        STRIDE = 1
        NHEADS = 8

        def extract_patches(x, ksize=KSIZE, pad=PAD, dilate=DILATE, stride=STRIDE):
            N, D, H, W = x.shape
            xp = jnp.pad(x, ((0, 0), (0, 0), (pad, pad), (pad, pad)))
            Ho = (H + 2 * pad - dilate * (ksize - 1) - 1) // stride + 1
            Wo = (W + 2 * pad - dilate * (ksize - 1) - 1) // stride + 1
            slices = []
            for i in range(ksize):
                for j in range(ksize):
                    r0, c0 = (i * dilate, j * dilate)
                    slices.append(xp[:, :, r0:r0 + (Ho - 1) * stride + 1:stride, c0:c0 + (Wo - 1) * stride + 1:stride])
            return jnp.stack(slices, axis=2)
        N, D, H, W = x.shape
        K2 = KSIZE * KSIZE
        hdim = D // NHEADS
        patches = extract_patches(x)
        p = patches.reshape(N, NHEADS, hdim, K2, H, W)
        q = x.reshape(N, NHEADS, hdim, 1, H, W)
        scores = (p * q).sum(axis=2, keepdims=True)
        att = jax.nn.softmax(scores, axis=3)
        out = (p * att).sum(axis=3).reshape(N, D, H, W)
        out = jnp.einsum('ndhw,od->nohw', out, w_out) + b_out[None, :, None, None]
        return out

    def _L2_attn_ref(x, w_qkv, w_out, b_out):
        import jax, jax.numpy as jnp
        import numpy as np
        HEADS = 8
        DIM_HEAD = 32
        EPS = 1e-05

        def _inst_norm(t):
            mu = jnp.mean(t, axis=-1, keepdims=True)
            var = jnp.var(t, axis=-1, keepdims=True)
            return (t - mu) / jnp.sqrt(var + EPS)
        b, n, dim = x.shape
        qkv = x @ w_qkv
        q, k, v = jnp.split(qkv, 3, axis=-1)
        to_heads = lambda t: t.reshape(b, n, HEADS, DIM_HEAD).transpose(0, 2, 1, 3)
        q, k, v = (to_heads(q), to_heads(k), to_heads(v))
        k = _inst_norm(k)
        v = _inst_norm(v)
        dots = jnp.einsum('bhnd,bhne->bhde', k, v)
        out = jnp.einsum('bhnd,bhde->bhne', q, dots) * (1.0 / n)
        out = out.transpose(0, 2, 1, 3).reshape(b, n, HEADS * DIM_HEAD)
        return out @ w_out + b_out

    def _L2_ffn_ref(x, Wr, br, W1, b1, g1, be1, m1, v1, W2, b2, g2, be2, m2, v2, Wo, bo):
        import jax, jax.numpy as jnp
        import numpy as np
        BN_EPS = 0.001

        def _bn(h, g, b, m, v):
            return g * (h - m) * jax.lax.rsqrt(v + BN_EPS) + b
        feat = jnp.mean(x, axis=0)
        w = jax.nn.softmax(feat @ Wr + br, axis=-1)
        h = jnp.einsum('bfd,edh->bfeh', x, W1) + b1
        h = jax.nn.relu(_bn(h, g1, be1, m1, v1))
        h = jnp.einsum('bfeh,ehk->bfek', h, W2) + b2
        h = jax.nn.relu(_bn(h, g2, be2, m2, v2))
        y = jnp.einsum('bfeh,ehd->bfed', h, Wo) + bo
        return jnp.einsum('bfed,fe->bfd', y, w)

    def _L3_attn_ref(x, g_in_w, g_in_b, g_out_w, g_out_b, t_in_w, t_in_b, t_out_w, t_out_b, fus_w1, fus_b1, fus_w2, fus_b2, ffn_w1, ffn_b1, ffn_w2, ffn_b2, gn_g, gn_b, fn_g, fn_b):
        import jax, jax.numpy as jnp
        import numpy as np
        DIM = 128
        H_GLOBAL = 8
        H_LOCAL = 4
        WINDOW = 5
        HALF = WINDOW // 2
        B, S = (4, 1024)
        EPS = 1e-05

        def layer_norm(x, g, b):
            mu = jnp.mean(x, axis=-1, keepdims=True)
            var = jnp.mean(jnp.square(x - mu), axis=-1, keepdims=True)
            return (x - mu) * jax.lax.rsqrt(var + EPS) * g + b

        def qkv_proj(x, in_w, in_b):
            qkv = x @ in_w.T + in_b
            return jnp.split(qkv, 3, axis=-1)

        def global_mha(x, in_w, in_b, out_w, out_b, nh):
            Bq, Sq, D = x.shape
            hd = D // nh
            q, k, v = qkv_proj(x, in_w, in_b)
            q = q.reshape(Bq, Sq, nh, hd)
            k = k.reshape(Bq, Sq, nh, hd)
            v = v.reshape(Bq, Sq, nh, hd)
            scores = jnp.einsum('bqhd,bkhd->bhqk', q, k) / np.sqrt(hd).astype(np.float32)
            attn = jax.nn.softmax(scores, axis=-1)
            o = jnp.einsum('bhqk,bkhd->bqhd', attn, v).reshape(Bq, Sq, D)
            return o @ out_w.T + out_b

        def local_mha(x, in_w, in_b, out_w, out_b, nh):
            Bq, Sq, D = x.shape
            hd = D // nh
            q, k, v = qkv_proj(x, in_w, in_b)
            kp = jnp.pad(k, ((0, 0), (HALF, HALF), (0, 0)))
            vp = jnp.pad(v, ((0, 0), (HALF, HALF), (0, 0)))
            k_win = jnp.stack([kp[:, j:j + Sq] for j in range(WINDOW)], axis=2)
            v_win = jnp.stack([vp[:, j:j + Sq] for j in range(WINDOW)], axis=2)
            q = q.reshape(Bq, Sq, nh, hd)
            k_win = k_win.reshape(Bq, Sq, WINDOW, nh, hd)
            v_win = v_win.reshape(Bq, Sq, WINDOW, nh, hd)
            scores = jnp.einsum('bshd,bswhd->bshw', q, k_win) / np.sqrt(hd).astype(np.float32)
            idx = jnp.arange(Sq)[:, None] + jnp.arange(-HALF, HALF + 1)[None, :]
            valid = (idx >= 0) & (idx < Sq)
            scores = jnp.where(valid[None, :, None, :], scores, -jnp.inf)
            attn = jax.nn.softmax(scores, axis=-1)
            o = jnp.einsum('bshw,bswhd->bshd', attn, v_win).reshape(Bq, Sq, D)
            return o @ out_w.T + out_b
        x_global = global_mha(x, g_in_w, g_in_b, g_out_w, g_out_b, H_GLOBAL)
        x_local = local_mha(x, t_in_w, t_in_b, t_out_w, t_out_b, H_LOCAL)
        x_comb = jnp.concatenate([x_global, x_local], axis=-1)
        x_fused = jax.nn.silu(x_comb @ fus_w1.T + fus_b1) @ fus_w2.T + fus_b2
        x = layer_norm(x + x_fused, gn_g, gn_b)
        x_ffn = jax.nn.silu(x @ ffn_w1.T + ffn_b1) @ ffn_w2.T + ffn_b2
        x = layer_norm(x + x_ffn, fn_g, fn_b)
        return x

    def _L3_ffn_ref(x, W_gat, att_src, att_dst, b_gat, ln_gamma, ln_beta, W1, b1, W2, b2, edge_index):
        import jax, jax.numpy as jnp
        import numpy as np
        B, N, D = (16, 2048, 128)
        NUM_EXPERTS, TOP_K, HEADS = (4, 2, 4)
        N_EDGES = 524288
        LN_EPS = 1e-05

        def _layernorm(x, g, b):
            mu = x.mean(-1, keepdims=True)
            var = ((x - mu) ** 2).mean(-1, keepdims=True)
            return (x - mu) * jax.lax.rsqrt(var + LN_EPS) * g + b

        def _forward(x, edge_index, W_gat, att_src, att_dst, b_gat, ln_gamma, ln_beta, W1, b1, W2, b2):
            Bc, Nc, Dc = x.shape
            M = Bc * Nc
            x_flat = x.reshape(M, Dc)
            h = (x_flat @ W_gat).reshape(M, HEADS, NUM_EXPERTS)
            loops = jnp.arange(M, dtype=edge_index.dtype)
            src = jnp.concatenate([edge_index[0], loops])
            dst = jnp.concatenate([edge_index[1], loops])
            a_src = (h * att_src).sum(-1)
            a_dst = (h * att_dst).sum(-1)
            e = jax.nn.leaky_relu(a_src[src] + a_dst[dst], negative_slope=0.2)
            e_max = jax.ops.segment_max(e, dst, num_segments=M)
            ee = jnp.exp(e - e_max[dst])
            denom = jax.ops.segment_sum(ee, dst, num_segments=M)
            alpha = ee / (denom[dst] + 1e-16)
            msg = h[src] * alpha[:, :, None]
            agg = jax.ops.segment_sum(msg, dst, num_segments=M).reshape(M, HEADS * NUM_EXPERTS) + b_gat
            scores = _layernorm(agg, ln_gamma, ln_beta).reshape(M, HEADS, NUM_EXPERTS).mean(1)
            scores = scores.reshape(Bc, Nc, NUM_EXPERTS)
            topk_s, topk_i = jax.lax.top_k(scores, TOP_K)
            w = jax.nn.softmax(topk_s, axis=-1)
            out = jnp.zeros_like(x)
            for ei in range(NUM_EXPERTS):
                g = jnp.where(topk_i == ei, w, 0.0).sum(-1)
                hh = jax.nn.gelu(x @ W1[ei] + b1[ei], approximate=False)
                out = out + g[..., None] * (hh @ W2[ei] + b2[ei])
            return out
        return _forward(x, edge_index, W_gat, att_src, att_dst, b_gat, ln_gamma, ln_beta, W1, b1, W2, b2)

    def _gn(v, G=32, eps=1e-05):
        B_, C_, H_, W_ = v.shape
        g = v.reshape(B_, G, C_ // G, H_, W_)
        m = jnp.mean(g, axis=(2, 3, 4), keepdims=True)
        s = jnp.var(g, axis=(2, 3, 4), keepdims=True)
        return ((g - m) / jnp.sqrt(s + eps)).reshape(v.shape)

    def _ln_c(v, eps=1e-06):
        m = jnp.mean(v, axis=1, keepdims=True)
        s = jnp.var(v, axis=1, keepdims=True)
        return (v - m) / jnp.sqrt(s + eps)

    def _ln_t(v, eps=1e-05):
        m = jnp.mean(v, axis=-1, keepdims=True)
        s = jnp.var(v, axis=-1, keepdims=True)
        return (v - m) / jnp.sqrt(s + eps)

    def _to_tokens(v):
        B_, C_, H_, W_ = v.shape
        return v.reshape(B_, C_, H_ * W_).transpose(0, 2, 1)

    def _from_tokens(t, like):
        B_, C_, H_, W_ = like.shape
        return t.transpose(0, 2, 1).reshape(B_, C_, H_, W_)
    x = _L0_conv_ref(x, L0_conv_gn_gamma, L0_conv_gn_beta, L0_conv_qkv_w, L0_conv_qkv_b, L0_conv_proj_w, L0_conv_proj_b)
    x = x + _L1_conv_ref(_gn(x), L1_conv_w_out, L1_conv_b_out)
    t = _to_tokens(x)
    t = t + _L2_attn_ref(_ln_t(t), L2_attn_w_qkv, L2_attn_w_out, L2_attn_b_out)
    t = t + _L2_ffn_ref(_ln_t(t), L2_ffn_Wr, L2_ffn_br, L2_ffn_W1, L2_ffn_b1, L2_ffn_g1, L2_ffn_be1, L2_ffn_m1, L2_ffn_v1, L2_ffn_W2, L2_ffn_b2, L2_ffn_g2, L2_ffn_be2, L2_ffn_m2, L2_ffn_v2, L2_ffn_Wo, L2_ffn_bo)
    t = t + _L3_attn_ref(_ln_t(t), L3_attn_g_in_w, L3_attn_g_in_b, L3_attn_g_out_w, L3_attn_g_out_b, L3_attn_t_in_w, L3_attn_t_in_b, L3_attn_t_out_w, L3_attn_t_out_b, L3_attn_fus_w1, L3_attn_fus_b1, L3_attn_fus_w2, L3_attn_fus_b2, L3_attn_ffn_w1, L3_attn_ffn_b1, L3_attn_ffn_w2, L3_attn_ffn_b2, L3_attn_gn_g, L3_attn_gn_b, L3_attn_fn_g, L3_attn_fn_b)
    t = t + _L3_ffn_ref(_ln_t(t), L3_ffn_W_gat, L3_ffn_att_src, L3_ffn_att_dst, L3_ffn_b_gat, L3_ffn_ln_gamma, L3_ffn_ln_beta, L3_ffn_W1, L3_ffn_b1, L3_ffn_W2, L3_ffn_b2, L3_ffn_edge_index)
    x = _from_tokens(t, x)
    return x

_drawn_inputs = setup_inputs


def setup_inputs(seed=0):
    import zlib

    import numpy as np

    out = dict(_drawn_inputs(seed))
    spreads = {'L0_conv_gn_gamma': (1.0, 0.2),
     'L0_conv_gn_beta': (0.0, 0.1),
     'L1_conv_b_out': (0.0, 0.1),
     'L2_ffn_br': (0.0, 0.644),
     'L2_ffn_b1': (0.0, 0.541),
     'L2_ffn_g1': (1.0, 0.567),
     'L2_ffn_be1': (0.0, 0.511),
     'L2_ffn_m1': (0.0, 0.538),
     'L2_ffn_v1': (1.0, 0.6),
     'L2_ffn_b2': (0.0, 0.365),
     'L2_ffn_g2': (1.0, 0.2),
     'L2_ffn_be2': (0.0, 0.433),
     'L2_ffn_m2': (0.0, 0.409),
     'L2_ffn_v2': (1.0, 0.6),
     'L2_ffn_bo': (0.0, 0.281),
     'L3_attn_g_in_b': (0.0, 0.8),
     'L3_attn_g_out_b': (0.0, 0.8),
     'L3_attn_t_in_b': (0.0, 0.8),
     'L3_attn_t_out_b': (0.0, 0.8),
     'L3_attn_fus_b1': (0.0, 0.8),
     'L3_attn_fus_b2': (0.0, 0.772),
     'L3_attn_ffn_b1': (0.0, 0.8),
     'L3_attn_ffn_b2': (0.0, 0.1),
     'L3_attn_gn_g': (1.0, 0.2),
     'L3_attn_gn_b': (0.0, 0.1),
     'L3_attn_fn_g': (1.0, 0.2),
     'L3_attn_fn_b': (0.0, 0.1),
     'L3_ffn_b_gat': (0.0, 0.328),
     'L3_ffn_ln_gamma': (1.0, 0.6),
     'L3_ffn_ln_beta': (0.0, 0.759),
     'L3_ffn_b1': (0.0, 0.577),
     'L3_ffn_b2': (0.0, 0.285)}
    factors = {'L0_conv_qkv_b': 4.676,
     'L0_conv_proj_b': 4.816,
     'L2_attn_b_out': 5.77,
     'L3_attn_g_in_w': 8.0,
     'L3_attn_g_out_w': 8.0,
     'L3_attn_t_in_w': 8.0,
     'L3_attn_t_out_w': 8.0,
     'L3_attn_fus_w1': 8.0,
     'L3_attn_fus_w2': 7.332,
     'L3_attn_ffn_w1': 3.415,
     'L3_attn_ffn_w2': 3.192,
     'L3_ffn_att_src': 8.0,
     'L3_ffn_att_dst': 8.0}
    for name, (base, spread) in spreads.items():
        noise = np.random.default_rng([zlib.crc32(name.encode()), seed]).standard_normal(out[name].shape)
        drawn = base * np.exp(spread * noise) if base else spread * noise
        out[name] = jnp.asarray(drawn.astype(out[name].dtype))
    for name, factor in factors.items():
        out[name] = (out[name] * factor).astype(out[name].dtype)
    return out
```

```python
import itertools
from contextlib import ExitStack, contextmanager

import concourse.bass as bass
from concourse import mybir

F32 = mybir.dt.float32
BF16 = mybir.dt.bfloat16
I32 = mybir.dt.int32
ALU = mybir.AluOpType
ACT = mybir.ActivationFunctionType
AX = mybir.AxisListType

P = 128
B, IMG = 4, 32
N = IMG * IMG
NT = N // P
M = B * N
MT = M // P
BANK = 512
NC2 = N // BANK
ROW = 32
E1, E2 = 8, 4
GH, GE = 4, 4
EDGES = 524288
EW = EDGES // P
NEG = -1.0e30


SERIAL = itertools.count()


@contextmanager
def stage(nc, *names, pool_dma=False):
    with ExitStack() as c:
        sems = [c.enter_context(nc.semaphore(f"{n}_{next(SERIAL)}")) for n in names]
        with nc.Block() as block:
            yield (block, *sems)
        nums = sorted(s.num for s in sems)
        cuts = [i for i in range(1, len(nums)) if nums[i] != nums[i - 1] + 1]
        for i, j in zip([0] + cuts, cuts + [len(nums)]):
            if pool_dma:
                nc.gpsimd.dma_reset(range(nums[i], nums[j - 1] + 1))
            nc.gpsimd.sem_clear(range(nums[i], nums[j - 1] + 1))
        nc.all_engine_barrier(sem_only=True)


def sbuf(nc, name, shape, dt):
    return nc.sbuf_tensor(f"{name}_{next(SERIAL)}", shape, dt)


def psum(nc, name, shape, dt):
    return nc.psum_tensor(f"{name}_{next(SERIAL)}", shape, dt)


def linker(engine, done):
    count = [0]

    def link(instruction):
        count[0] += 1
        instruction.then_inc(done, 1)
        engine.wait_ge(done, count[0])

    return link


def affine(nc, on_act, out, in_, scale=1.0, bias=0.0, func=ACT.Identity):
    if on_act:
        return nc.scalar.activation(out, in_, func, bias=bias, scale=scale)
    return nc.vector.tensor_scalar(out, in_, scale, bias, ALU.mult, ALU.add)


def product_pass(nc, ps, n, product, evacuate, by="ad"):
    ring = ps.shape[1]
    with stage(nc, "product_ready", "off_by_act", "off_by_dve") as (block, ready, by_act, by_dve):
        done = {"a": by_act, "d": by_dve}
        share = {e: [i for i in range(n) if by[i % len(by)] == e] for e in "ad"}

        @block.tensor
        def _(pe):
            for i in range(n):
                if i >= ring:
                    e = by[(i - ring) % len(by)]
                    pe.wait_ge(done[e], share[e].index(i - ring) + 1)
                product(i, ps[:, i % ring]).then_inc(ready, 1)

        @block.scalar
        def _(act):
            for i in share["a"]:
                act.wait_ge(ready, i + 1)
                evacuate(True, i, ps[:, i % ring]).then_inc(by_act, 1)

        @block.vector
        def _(dve):
            for i in share["d"]:
                dve.wait_ge(ready, i + 1)
                evacuate(False, i, ps[:, i % ring]).then_inc(by_dve, 1)


def turn_tiles(nc, ps, ident, pairs, combine=None):
    def product(i, bank):
        for k, tile in enumerate(pairs[i][0]):
            last = nc.tensor.transpose(bank[0:tile.shape[1], k * P:(k + 1) * P], tile, ident[:])
        return last

    def evacuate(on_act, i, bank):
        tiles, out = pairs[i]
        in_ = bank[0:out.shape[0], 0:len(tiles) * P].rearrange("p (k n) -> p k n", n=P)
        if combine is not None:
            return combine(on_act, i, out, in_)
        if on_act:
            return nc.scalar.copy(out, in_)
        return nc.vector.tensor_copy(out, in_)

    product_pass(nc, ps, len(pairs), product, evacuate)



def make_constants(nc, k):
    with stage(nc, "made") as (block, made):
        @block.gpsimd
        def _(pool):
            link = linker(pool, made)

            def select(out, base, pattern, fill, compare):
                link(nc.gpsimd.affine_select(out=out, in_=out, compare_op=compare, fill=fill, base=base,
                                             pattern=pattern, channel_multiplier=1))

            def same_group(t, size, value):
                link(nc.gpsimd.memset(t[:], value))
                n = P // size
                if t.shape[1] == n:
                    low, high, view = [[-size, n]], [[size, n]], t[:]
                else:
                    low, high = [[-size, n], [0, size]], [[size, n], [0, size]]
                    view = t[:].rearrange("p (n s) -> p n s", s=size)
                select(view, 0, low, 0.0, ALU.is_ge)
                link(nc.gpsimd.affine_select(out=view, in_=view, compare_op=ALU.is_ge, fill=0.0,
                                             base=size - 1, pattern=high, channel_multiplier=-1))

            link(nc.gpsimd.memset(k.ident[:], 0.0))
            select(k.ident[:], 0, [[-1, P]], 1.0, ALU.not_equal)
            link(nc.gpsimd.tensor_copy(k.ident_b[:], k.ident[:]))
            same_group(k.mean16, 16, 1.0 / 16)
            same_group(k.mean4, 4, 1.0 / 4)
            same_group(k.block32, 32, 1.0 / N)
            same_group(k.heads16, 16, 1.0)
            same_group(k.heads32, 32, 1.0)
            for t, d in ((k.spread16, 16), (k.spread32, 32)):
                link(nc.gpsimd.memset(t[:], 0.0))
                select(t[:].rearrange("p (r d) -> p r d", d=d), 0, [[-1, t.shape[1] // d], [0, d]], 1.0,
                       ALU.not_equal)
            link(nc.gpsimd.memset(k.ones_row[:], 1.0))
            link(nc.gpsimd.memset(k.eps[:, 0:1], 1e-5))
            link(nc.gpsimd.memset(k.eps[:, 1:2], 1e-3))
            link(nc.gpsimd.memset(k.window_mask[:], 0.0))
            for t, w in ((0, 0), (0, 1), (NT - 1, 3), (NT - 1, 4)):
                v = k.window_mask[:, t, w:w + 1]
                if t == 0:
                    select(v, w - 2, [[0, 1]], NEG, ALU.is_ge)
                else:
                    link(nc.gpsimd.affine_select(out=v, in_=v, compare_op=ALU.is_ge, fill=NEG,
                                                 base=P - 1 - (w - 2), pattern=[[0, 1]],
                                                 channel_multiplier=-1))


C_GN_G, C_GN_B, C_QKV_B, C_PROJ_B, C_L1_B = 0, 1, 2, 5, 6
C_MOE = 7
C_G_IN = C_MOE + 80
C_G_OUT, C_T_IN, C_T_OUT, C_FUS1, C_FFN1, C_B1 = C_G_IN + 3, C_G_IN + 4, C_G_IN + 7, C_G_IN + 8, C_G_IN + 10, C_G_IN + 12
C_ROWS = C_B1 + 2 * E2


def load_weights(nc, k, w):
    with ExitStack() as c:
        table = c.enter_context(sbuf(nc, "table", [P, P], F32))
        raw = c.enter_context(sbuf(nc, "raw", [P, 27, P], F32))
        ps = c.enter_context(psum(nc, "ps_w", [P, 8, BANK], F32))

        rows = [(C_GN_G, w["L0_conv_gn_gamma"]), (C_GN_B, w["L0_conv_gn_beta"]), (C_QKV_B, w["L0_conv_qkv_b"]),
                (C_PROJ_B, w["L0_conv_proj_b"]), (C_L1_B, w["L1_conv_b_out"])]
        rows += [(C_MOE + E1 * i, w[f"L2_ffn_{n}"]) for i, n in enumerate("b1 g1 be1 m1 v1 b2 g2 be2 m2 v2".split())]
        rows += [(C_G_IN, w["L3_attn_g_in_b"]), (C_G_OUT, w["L3_attn_g_out_b"]),
                 (C_T_IN, w["L3_attn_t_in_b"]), (C_T_OUT, w["L3_attn_t_out_b"]), (C_FUS1, w["L3_attn_fus_b1"]),
                 (C_FFN1, w["L3_attn_ffn_b1"]), (C_B1, w["L3_ffn_b1"])]

        def as_rows(a):
            if len(a.shape) == 1:
                return a.rearrange("(r n) -> r n", n=P)
            return a.rearrange("e (r n) -> (e r) n", n=P) if a.shape[1] > P else a

        sources = []
        for name in ("L0_conv_qkv_w", "L0_conv_proj_w", "L1_conv_w_out", "L3_attn_g_in_w", "L3_attn_g_out_w",
                     "L3_attn_t_in_w", "L3_attn_t_out_w", "L3_attn_fus_w1", "L3_attn_fus_w2", "L3_attn_ffn_w1",
                     "L3_attn_ffn_w2"):
            a = w[name]
            for r in range(a.shape[0] // P):
                for q in range(a.shape[1] // P):
                    sources.append(a[r * P:(r + 1) * P, q * P:(q + 1) * P])
        for g in range(2):
            sources.append(w["L2_attn_w_qkv"][:, g * P:(g + 1) * P])

        straight = [(k.w_kv[:], w["L2_attn_w_qkv"][:, 2 * P:6 * P]),
                    (k.w_o2[:], w["L2_attn_w_out"].rearrange("(g e) o -> e g o", g=2)),
                    (k.m1[:], w["L2_ffn_W1"].rearrange("e d h -> d e h")),
                    (k.m2[:], w["L2_ffn_W2"].rearrange("e d h -> d e h")),
                    (k.mo[:], w["L2_ffn_Wo"].rearrange("e d h -> d e h")),
                    (k.mo_b[:], w["L2_ffn_bo"]), (k.wr[:], w["L2_ffn_Wr"]),
                    (k.w_gat[:], w["L3_ffn_W_gat"]),
                    (k.x1[:], w["L3_ffn_W1"].rearrange("e d h -> d e h")),
                    (k.x2[:], w["L3_ffn_W2"].rearrange("e (s h) d -> h e s d", h=P)),
                    (k.x2_b[:], w["L3_ffn_b2"])]
        straight += [(k.rows[0:1, i, 0:n], w[name].rearrange("(a n) -> a n", a=1)) for i, (name, n) in enumerate(
            (("L2_attn_b_out", P), ("L2_ffn_br", E1), ("L3_attn_fus_b2", P), ("L3_attn_ffn_b2", P)))]
        straight += [(k.wide[:, i, :], w[name].partition_broadcast(P)) for i, name in enumerate(
            ("L3_attn_gn_g", "L3_attn_gn_b", "L3_attn_fn_g", "L3_attn_fn_b"))]
        straight += [(k.gat[:, i, :], w[name].partition_broadcast(P)) for i, name in enumerate(
            ("L3_ffn_b_gat", "L3_ffn_ln_gamma", "L3_ffn_ln_beta"))]
        straight += [(k.gat[:, 3 + i, :], w[name].rearrange("h e -> (h e)").partition_broadcast(P))
                     for i, name in enumerate(("L3_ffn_att_src", "L3_ffn_att_dst"))]
        straight += [(k.x_cm[:], w["x"].rearrange("b c h w -> c b (h w)"))]

        with stage(nc, "cleared", "loaded") as (block, cleared, loaded):
            n_row_loads = len(rows)

            @block.gpsimd
            def _(pool):
                nc.gpsimd.memset(table[:], 0.0).then_inc(cleared, 1)

            @block.sync
            def _(sp):
                for out, in_ in straight:
                    sp.dma_start(out, in_).then_inc(loaded, 16)
                sp.wait_ge(loaded, 16 * (len(straight) + len(sources) + n_row_loads))

            @block.scalar
            def _(act):
                for i, source in enumerate(sources):
                    act.dma_start(raw[:, i, :], source).then_inc(loaded, 16)
                act.wait_ge(cleared, 1)
                for r, a in rows:
                    v = as_rows(a)
                    act.dma_start(table[r:r + v.shape[0], :], v).then_inc(loaded, 16)

        tiles = [raw[:, i, :] for i in range(len(sources))]
        flat = []
        for i in range(0, len(tiles), 4):
            flat.append((tiles[i:i + 4], k.turned[:, i:min(i + 4, len(tiles)), :]))
        flat.append(([table[:]], k.cols[:].unsqueeze(1)))
        turn_tiles(nc, ps, k.ident, flat)

        with stage(nc, "scaled", "done") as (block, scaled, done):
            @block.scalar
            def _(act):
                for j in range(2):
                    v = C_MOE + E1 * (4 + 5 * j)
                    nc.scalar.activation(k.bn[:, j, 0, :], k.cols[:, v:v + E1], ACT.Sqrt,
                                         bias=k.eps[:, 1:2]).then_inc(scaled, 1)

            @block.vector
            def _(dve):
                link = linker(dve, done)
                link(nc.vector.tensor_scalar(k.qb[:, 0:1], k.cols[:, C_QKV_B:C_QKV_B + 1], 32 ** -0.5, None, ALU.mult))
                link(nc.vector.tensor_scalar(k.qb[:, 1:2], k.cols[:, C_G_IN:C_G_IN + 1], 16 ** -0.5, None, ALU.mult))
                link(nc.vector.tensor_scalar(k.qb[:, 3:4], k.cols[:, C_T_IN:C_T_IN + 1], 32 ** -0.5, None, ALU.mult))
                dve.wait_ge(scaled, 2)
                for j in range(2):
                    b_, g_, be_, m_ = (k.cols[:, C_MOE + E1 * (i + 5 * j):C_MOE + E1 * (i + 5 * j + 1)] for i in range(4))
                    link(nc.vector.reciprocal(k.bn[:, j, 0, :], k.bn[:, j, 0, :]))
                    link(nc.vector.tensor_tensor(k.bn[:, j, 0, :], k.bn[:, j, 0, :], g_, ALU.mult))
                    link(nc.vector.tensor_tensor(k.bn[:, j, 1, :], b_, m_, ALU.subtract))
                    link(nc.vector.tensor_tensor(k.bn[:, j, 1, :], k.bn[:, j, 1, :], k.bn[:, j, 0, :], ALU.mult))
                    link(nc.vector.tensor_tensor(k.bn[:, j, 1, :], k.bn[:, j, 1, :], be_, ALU.add))



def group_norm(nc, k, x, out, mean_matrix, gamma, beta):
    with ExitStack() as c:
        stats = c.enter_context(sbuf(nc, "gn_stats", [P, NC2, 6], F32))
        s = c.enter_context(sbuf(nc, "gn_s", [P, 8], F32))
        ps = c.enter_context(psum(nc, "gn_ps", [P, BANK], F32))
        block, chained, ready, averaged, rooted = c.enter_context(stage(nc, "chained", "moments", "averaged", "rooted"))

        @block.vector
        def _(dve):
            link = linker(dve, chained)
            for i in range(NC2):
                link(nc.vector.bn_stats(stats[:, i, :], x[:, i * BANK:(i + 1) * BANK]))
            link(nc.vector.bn_aggr(s[:, 0:2], stats[:].rearrange("p a b -> p (a b)")))
            nc.vector.scalar_tensor_tensor(s[:, 1:2], s[:, 0:1], s[:, 0:1], s[:, 1:2], ALU.mult, ALU.add).then_inc(ready, 1)
            dve.wait_ge(averaged, 1)
            link(nc.vector.tensor_copy(s[:, 2:4], ps[:, 0:2]))
            link(nc.vector.tensor_tensor(s[:, 4:5], s[:, 2:3], s[:, 2:3], ALU.mult))
            nc.vector.tensor_tensor(s[:, 5:6], s[:, 3:4], s[:, 4:5], ALU.subtract).then_inc(ready, 1)
            dve.wait_ge(rooted, 1)
            link(nc.vector.reciprocal(s[:, 6:7], s[:, 6:7]))
            if gamma is not None:
                link(nc.vector.tensor_tensor(s[:, 6:7], s[:, 6:7], gamma, ALU.mult))
            link(nc.vector.tensor_tensor(s[:, 7:8], s[:, 2:3], s[:, 6:7], ALU.mult))
            if beta is not None:
                link(nc.vector.tensor_tensor(s[:, 7:8], beta, s[:, 7:8], ALU.subtract))
            else:
                link(nc.vector.tensor_scalar(s[:, 7:8], s[:, 7:8], -1.0, None, ALU.mult))
            in_ = x.rearrange("p (h w) -> p h w", w=IMG) if len(out.shape) == 3 else x
            link(nc.vector.tensor_scalar(out, in_, s[:, 6:7], s[:, 7:8], ALU.mult, ALU.add))

        @block.tensor
        def _(pe):
            pe.wait_ge(ready, 1)
            nc.tensor.matmul(ps[:, 0:2], mean_matrix[:], s[:, 0:2], start=True, stop=True).then_inc(averaged, 1)

        @block.scalar
        def _(act):
            act.wait_ge(ready, 2)
            nc.scalar.activation(s[:, 6:7], s[:, 5:6], ACT.Sqrt, bias=k.eps[:, 0:1]).then_inc(rooted, 1)


def layer_norm(nc, k, x, out, gamma=None, beta=None):
    with ExitStack() as c:
        stats = c.enter_context(sbuf(nc, "ln_stats", [P, NT, 6], F32))
        s = c.enter_context(sbuf(nc, "ln_s", [P, NT, 2], F32))
        block, chained, ready, rooted, ready_shift, off = c.enter_context(
            stage(nc, "chained", "variance", "rooted", "shift", "normed"))

        @block.vector
        def _(dve):
            link = linker(dve, chained)
            for t in range(NT):
                nc.vector.bn_stats(stats[:, t, :], x[:, t, :]).then_inc(off, 1)
            for t in range(NT):
                dve.wait_ge(off, t + 1)
                last = nc.vector.bn_aggr(s[:, t, :], stats[:, t, :])
                last.then_inc(ready, 1)
            dve.wait_ge(rooted, 1)
            link(nc.vector.reciprocal(s[:, :, 1], s[:, :, 1]))
            for t in range(NT):
                last = nc.vector.tensor_scalar(out[:, t, :], x[:, t, :], s[:, t, 0:1], s[:, t, 1:2],
                                               ALU.subtract, ALU.mult)
                last.then_inc(ready_shift, 1)
            if gamma is not None:
                dve.wait_ge(ready_shift, NT)
                for g, op in ((gamma, ALU.mult), (beta, ALU.add)):
                    link(nc.vector.tensor_tensor(out, out, g.unsqueeze(1).broadcast_to([P, NT, P]), op))

        @block.scalar
        def _(act):
            act.wait_ge(ready, NT)
            nc.scalar.activation(s[:, :, 1], s[:, :, 1], ACT.Sqrt, bias=k.eps[:, 0:1]).then_inc(rooted, 1)


STACKS = {16: [((0, 0, 0, 1, 1, 2), (0, 1, 2, 0, 1, 0))],
          32: [((0, 0, 1), (0, 1, 0)), ((0, 1, 2), (2, 1, 0))]}
STACK = 96
S_STEPS = (2, 2, 1, 1, 1, 1, 0, 0)


def split_parts(nc, k, pairs):
    with stage(nc, "rounded", "rest_ready", "done") as (block, rounded, rest_ready, done):
        @block.scalar
        def _(act):
            for part in range(2):
                for j, (x, parts) in enumerate(pairs):
                    if part == 1:
                        act.wait_ge(rest_ready, j + 1)
                    nc.scalar.copy(parts[:, part], x).then_inc(rounded, 1)

        @block.vector
        def _(dve):
            n = len(pairs)
            for j, (x, parts) in enumerate(pairs):
                dve.wait_ge(rounded, j + 1)
                nc.vector.tensor_tensor(x, x, parts[:, 0], ALU.subtract).then_inc(rest_ready, 1)
            for j, (x, parts) in enumerate(pairs):
                dve.wait_ge(rounded, n + j + 1)
                nc.vector.tensor_tensor(parts[:, 2], x, parts[:, 1], ALU.subtract).then_inc(done, 1)


def stack_parts(nc, k, hd, parts):
    heads = P // hd
    with stage(nc, "stored") as (block, stored):
        @block.sync
        def _(sp):
            for j in range(2):
                sp.dma_start(k.parts_dram[j].rearrange("s p n -> p s n"), parts[j]).then_inc(stored, 16)
            sp.wait_ge(stored, 32)
            for g in range(2):
                for j in range(2):
                    for slot, blocks in enumerate(STACKS[hd]):
                        for r, part in enumerate(blocks[j]):
                            half = slice(g * heads // 2, (g + 1) * heads // 2)
                            slots = k.stacks[r * hd:(r + 1) * hd, j].rearrange(
                                "p (h s) n -> p h s n", s=len(STACKS[hd]))[:, half, slot, :]
                            source = k.parts_dram[j, part].rearrange("(h r) n -> r h n", r=hd)[:, half, :]
                            sp.dma_start(slots, source).then_inc(k.stacked[g], 16)


def dense_attention(nc, k, hd, o_cm):
    heads = P // hd
    per = len(STACKS[hd])
    share = 32 // hd
    groups = heads // share
    items, at_step = [], {}

    def schedule(step, new):
        at_step[step] = list(range(len(items), len(items) + len(new)))
        items.extend(new)

    def tiles(h, lo, hi):
        return [("s", h, t, n) for t in range(lo, hi) for n in range(NC2)]

    rows_of = {}
    schedule("first", tiles(0, 0, NT))
    rows_of[0] = list(range(len(items), len(items) + NC2))
    items += [("r", 0, n) for n in range(NC2)]
    for h in range(heads):
        lo = 0
        for m in range(NT):
            hi = lo + S_STEPS[m]
            schedule((h, m), tiles(h + 1, lo, hi) if h + 1 < heads else [])
            lo = hi
            if m == NT - 1 and h + 1 < heads:
                rows_of[h + 1] = list(range(len(items), len(items) + NC2))
                items += [("r", h + 1, n) for n in range(NC2)]
    order = {"s": {}, "r": {}}
    for i, item in enumerate(items):
        order[item[0]][i] = len(order[item[0]])
    RING = 2
    with ExitStack() as c:
        ring = c.enter_context(psum(nc, "att_ring", [P, RING, BANK], F32))
        ST = c.enter_context(psum(nc, "att_ST", [P, 2, N], F32))
        O = c.enter_context(psum(nc, "att_O", [64, NC2, BANK], F32))
        probs = c.enter_context(sbuf(nc, "att_probs", [P, 3, N], F32))
        half_max = c.enter_context(sbuf(nc, "att_half_max", [P, 2, NT, NC2], F32))
        shift = c.enter_context(sbuf(nc, "att_shift", [P, 2, NT], F32))
        shift_parts = c.enter_context(sbuf(nc, "att_shift_parts", [P, 2, NT, 3], BF16))
        sums = c.enter_context(sbuf(nc, "att_sums", [64, NC2, BANK], F32))
        rden = c.enter_context(sbuf(nc, "att_rden", [32, NC2, BANK], F32))
        (block, ring_ready, reduced, rows_off, chained, parts_ready, st_ready, probs_ready, mixed_ready,
         off_by_act, off_by_dve, normed) = c.enter_context(stage(nc, "ring_ready", "reduced", "rows_off", "chained", "parts_ready", "st_ready",
                                         "probs_ready", "mixed_ready", "off_by_act", "off_by_dve", "normed"))

        @block.tensor
        def _(pe):
            def bank_free(i):
                if i >= RING:
                    kind = items[i - RING][0]
                    pe.wait_ge(reduced if kind == "s" else rows_off, order[kind][i - RING] + 1)

            def scores(i):
                _, h, t, n = items[i]
                bank_free(i)
                nc.tensor.matmul(ring[:, i % RING], k.stacks[0:STACK, 0, per * h, t * P:(t + 1) * P],
                                 k.stacks[0:STACK, 1, per * h, n * BANK:(n + 1) * BANK], start=True,
                                 stop=True).then_inc(ring_ready, 1)

            def shift_rows(h):
                pe.wait_ge(parts_ready, h + 1)
                for i in rows_of[h]:
                    n = items[i][2]
                    bank_free(i)
                    for t in range(4):
                        last = nc.tensor.matmul(ring[STACK:STACK + 3, i % RING, t * P:(t + 1) * P],
                                                shift_parts[:, h % 2, 4 * n + t, :], k.ident_b[:], start=True,
                                                stop=True, tile_position=(0, STACK))
                    last.then_inc(ring_ready, 1)

            def scores_transposed(h, m):
                s = h * NT + m
                if m == 0:
                    pe.wait_ge(rows_off, NC2 * (h + 1))
                if s >= 2:
                    pe.wait_ge(probs_ready, s - 1)
                for n in range(NC2):
                    for j in range(per):
                        rows = STACK + 3 if j == per - 1 else STACK
                        last = nc.tensor.matmul(ST[:, s % 2, n * BANK:(n + 1) * BANK],
                                                k.stacks[0:rows, 1, per * h + j, m * P:(m + 1) * P],
                                                k.stacks[0:rows, 0, per * h + j, n * BANK:(n + 1) * BANK],
                                                start=(j == 0), stop=(j == per - 1))
                last.then_inc(st_ready, 1)

            def mix(h, m):
                s = h * NT + m
                pe.wait_ge(probs_ready, s + 1)
                g, first, last_step = h // share, h % share == 0 and m == 0, h % share == share - 1 and m == NT - 1
                for n, off in enumerate((off_by_act, off_by_dve)):
                    if first and g >= 1:
                        pe.wait_ge(off, g)
                    last = nc.tensor.matmul(O[:, n], k.v_ext[:, m, h, :], probs[:, s % 3, n * BANK:(n + 1) * BANK],
                                            start=first, stop=last_step)
                last.then_inc(mixed_ready, 1)

            pe.wait_ge(k.stacked[0], 16 * 6 * 2)
            for i in at_step["first"]:
                scores(i)
            shift_rows(0)
            for h in range(heads):
                if h == heads // 2 - 1:
                    pe.wait_ge(k.stacked[1], 16 * 6 * 2)
                for m in range(NT):
                    for i in at_step[(h, m)]:
                        scores(i)
                    if m == NT - 1 and h + 1 < heads:
                        shift_rows(h + 1)
                    scores_transposed(h, m)
                    if h * NT + m >= 1:
                        mix(*divmod(h * NT + m - 1, NT))
            mix(heads - 1, NT - 1)

        @block.scalar
        def _(act):
            def rows(h):
                for i in rows_of[h]:
                    n = items[i][2]
                    act.wait_ge(ring_ready, i + 1)
                    nc.scalar.copy(k.stacks[STACK:STACK + 3, 0, per * h + per - 1, n * BANK:(n + 1) * BANK],
                                   ring[STACK:STACK + 3, i % RING, :]).then_inc(rows_off, 1)

            def carry_off(g):
                act.wait_ge(mixed_ready, NT * share * (g + 1))
                if g >= 1:
                    act.wait_ge(normed, g)
                nc.scalar.copy(sums[:, 0], O[:, 0]).then_inc(off_by_act, 1)

            rows(0)
            for h in range(heads):
                for m in range(NT):
                    s = h * NT + m
                    if m == NT - 1 and h + 1 < heads:
                        rows(h + 1)
                    act.wait_ge(st_ready, s + 1)
                    if s >= 3:
                        act.wait_ge(mixed_ready, s - 2)
                    nc.scalar.activation(probs[:, s % 3, :], ST[:, s % 2, :], ACT.Exp).then_inc(probs_ready, 1)
                    if m == 0 and h % share == 0 and h > 0:
                        carry_off(h // share - 1)
            carry_off(groups - 1)

        @block.vector
        def _(dve):
            link = linker(dve, chained)

            def maxima(indices):
                for i in indices:
                    _, h, t, n = items[i]
                    dve.wait_ge(ring_ready, i + 1)
                    nc.vector.tensor_reduce(half_max[:, h % 2, t, n:n + 1], ring[:, i % RING], AX.X, ALU.max,
                                            negate=True).then_inc(reduced, 1)
                    if t == NT - 1 and n == NC2 - 1:
                        parts(h)

            def parts(h):
                a, p_ = shift[:, h % 2], shift_parts[:, h % 2]
                dve.wait_ge(reduced, NC2 * NT * (h + 1))
                link(nc.vector.tensor_tensor(a, half_max[:, h % 2, :, 0], half_max[:, h % 2, :, 1], ALU.min))
                link(nc.vector.tensor_copy(p_[:, :, 0], a))
                link(nc.vector.tensor_tensor(a, a, p_[:, :, 0], ALU.subtract))
                link(nc.vector.tensor_copy(p_[:, :, 1], a))
                nc.vector.tensor_tensor(p_[:, :, 2], a, p_[:, :, 1], ALU.subtract).then_inc(parts_ready, 1)

            def norm(g):
                dve.wait_ge(mixed_ready, NT * share * (g + 1))
                if g >= 1:
                    dve.wait_ge(normed, g)
                nc.vector.tensor_copy(sums[:, 1], O[:, 1]).then_inc(off_by_dve, 1)
                dve.wait_ge(off_by_dve, g + 1)
                dve.wait_ge(off_by_act, g + 1)
                link(nc.vector.reciprocal(rden[:], sums[32:64]))
                nc.vector.tensor_tensor(o_cm[32 * g:32 * g + 32, :].rearrange("p (n m) -> p n m", m=BANK), sums[0:32],
                                        rden[:], ALU.mult).then_inc(normed, 1)

            maxima(at_step["first"])
            for h in range(heads):
                for m in range(NT):
                    maxima(at_step[(h, m)])
                    if m == 0 and h % share == 0 and h > 0:
                        norm(h // share - 1)
            norm(groups - 1)
    for g in range(2):
        nc.gpsimd.sem_clear(k.stacked[g])
    nc.all_engine_barrier(sem_only=True)


def local_attention(nc, k, K, H, q, shifted_k, shifted_v, heads, spread, w_out, out, mask=None):
    KH = K * H
    per = P // H
    sets = [(s, min(per, K - s)) for s in range(0, K, per)]
    with ExitStack() as c:
        att = c.enter_context(sbuf(nc, "loc_att", [P, NT, KH], F32))
        att_t = c.enter_context(sbuf(nc, "loc_att_t", [P, len(sets), N], F32))
        small = c.enter_context(sbuf(nc, "loc_small", [P, 2, NT, H], F32))
        prod = c.enter_context(sbuf(nc, "loc_prod", [P, 3, N], F32))

        per_bank = BANK // KH if KH * 2 > BANK else min(NT, BANK // KH)
        n_banks = -(-NT // per_bank)
        with ExitStack() as c2:
            scores = c2.enter_context(psum(nc, "loc_scores", [P, n_banks, BANK], F32))
            block, product_ready, scored, chained, exped = c2.enter_context(
                stage(nc, "product_ready", "scored", "chained", "exped"))
            where = [(t // per_bank, (t % per_bank) * KH) for t in range(NT)]

            @block.tensor
            def _(pe):
                for s in range(K):
                    pe.wait_ge(product_ready, NC2 * (s + 1))
                    for t in range(NT):
                        b_, o_ = where[t]
                        last = nc.tensor.matmul(scores[:, b_, o_ + s * H:o_ + (s + 1) * H],
                                                prod[:, s % 3, t * P:(t + 1) * P], heads[:], start=True, stop=True)
                    last.then_inc(scored, 1)

            @block.vector
            def _(dve):
                for s in range(K):
                    if s >= 3:
                        dve.wait_ge(scored, s - 2)
                    for n in range(NC2):
                        a, b_ = q(n), shifted_k(s, n)
                        o_ = prod[:, s % 3, n * BANK:(n + 1) * BANK]
                        if len(a.shape) == 3:
                            o_ = o_.rearrange("p (h w) -> p h w", w=IMG)
                        nc.vector.tensor_tensor(o_, a, b_, ALU.mult).then_inc(product_ready, 1)
                link = linker(dve, chained)
                dve.wait_ge(scored, K)
                a4 = att[:].rearrange("p t (s h) -> p t s h", h=H)
                top, total = small[:, 0], small[:, 1]
                for b_ in range(n_banks):
                    lo, hi = b_ * per_bank, min(NT, (b_ + 1) * per_bank)
                    in_ = scores[:, b_, 0:(hi - lo) * KH].rearrange("p (t s h) -> p t s h", s=K, h=H)
                    if mask is not None:
                        link(nc.vector.tensor_tensor(a4[:, lo:hi], in_, mask[:, lo:hi].unsqueeze(3).broadcast_to(
                            [P, hi - lo, K, H]), ALU.add))
                    else:
                        link(nc.vector.tensor_copy(a4[:, lo:hi], in_))
                link(nc.vector.tensor_reduce(top, a4.rearrange("p t s h -> p t h s"), AX.X, ALU.max))
                for t in range(NT):
                    link(nc.vector.tensor_tensor(a4[:, t], a4[:, t], top[:, t].unsqueeze(1).broadcast_to([P, K, H]),
                                                 ALU.subtract))
                dve.wait_ge(exped, 1)
                link(nc.vector.tensor_reduce(total, a4.rearrange("p t s h -> p t h s"), AX.X, ALU.add))
                link(nc.vector.reciprocal(total, total))
                for t in range(NT):
                    link(nc.vector.tensor_tensor(a4[:, t], a4[:, t], total[:, t].unsqueeze(1).broadcast_to([P, K, H]),
                                                 ALU.mult))

            @block.scalar
            def _(act):
                act.wait_ge(chained, n_banks + 1 + NT)
                nc.scalar.activation(att[:], att[:], ACT.Exp).then_inc(exped, 1)

        with ExitStack() as c2:
            ps = c2.enter_context(psum(nc, "loc_ps", [P, 8, BANK], F32))
            pairs = []
            for i, (s, n_s) in enumerate(sets):
                for t in range(0, NT, 4):
                    pairs.append(([att[:, u, s * H:(s + n_s) * H] for u in range(t, t + 4)],
                                  att_t[0:n_s * H, i, t * P:(t + 4) * P].rearrange("p (k n) -> p k n", n=P)))
            turn_tiles(nc, ps, k.ident, pairs)

        with ExitStack() as c2:
            wide = c2.enter_context(psum(nc, "loc_wide", [P, 4, BANK], F32))
            acc = c2.enter_context(psum(nc, "loc_acc", [P, NC2, BANK], F32))
            weighed = c2.enter_context(sbuf(nc, "loc_weighed", [P, 4, BANK], F32))
            block, spread_ready, weighed_ready, summed, off = c2.enter_context(
                stage(nc, "spread_ready", "weighed_ready", "summed", "off"))
            steps = [(s, n) for s in range(K) for n in range(NC2)]

            @block.tensor
            def _(pe):
                for i in range(len(steps) + 2):
                    if i < len(steps):
                        s, n = steps[i]
                        if i >= 4:
                            pe.wait_ge(weighed_ready, i - 3)
                        j = s // per
                        rows = sets[j][1] * H
                        nc.tensor.matmul(wide[:, i % 4], spread[0:rows, (s - sets[j][0]) * P:(s - sets[j][0] + 1) * P],
                                         att_t[0:rows, j, n * BANK:(n + 1) * BANK], start=True,
                                         stop=True).then_inc(spread_ready, 1)
                    if i >= 2:
                        s, n = steps[i - 2]
                        pe.wait_ge(weighed_ready, i - 1)
                        nc.tensor.matmul(acc[:, n], w_out, weighed[:, (i - 2) % 4], start=(s == 0),
                                         stop=(s == K - 1)).then_inc(summed, 1)

            @block.vector
            def _(dve):
                for i, (s, n) in enumerate(steps):
                    dve.wait_ge(spread_ready, i + 1)
                    if i >= 4:
                        dve.wait_ge(summed, i - 3)
                    v = shifted_v(s, n)
                    a, o_ = wide[:, i % 4], weighed[:, i % 4]
                    if len(v.shape) == 3:
                        a, o_ = (y.rearrange("p (h w) -> p h w", w=IMG) for y in (a, o_))
                    nc.vector.tensor_tensor(o_, a, v, ALU.mult).then_inc(weighed_ready, 1)
                dve.wait_ge(summed, len(steps))
                for n in range(NC2):
                    out(n, acc[:, n]).then_inc(off, 1)


def chunk(a, n, size=BANK):
    return a[:, n * size:(n + 1) * size]


def turn_image(nc, k, ps, x, out, combine=None):
    pairs = [([x[:, t, :] if len(x.shape) == 3 else chunk(x, t, P) for t in range(u, u + 4)],
              out[:, u:u + 4, :] if len(out.shape) == 3 else
              chunk(out, u // 4).rearrange("p (k n) -> p k n", n=P)) for u in range(0, NT, 4)]
    turn_tiles(nc, ps, k.ident, pairs, combine)


def copy_blocks(nc, pairs, engine_name="vector"):
    with stage(nc, "by_act", "by_dve") as (block, by_act, by_dve):
        @block.scalar
        def _(act):
            for out, in_ in pairs[1::2]:
                nc.scalar.copy(out, in_).then_inc(by_act, 1)

        @block.vector
        def _(dve):
            for out, in_ in pairs[0::2]:
                nc.vector.tensor_copy(out, in_).then_inc(by_dve, 1)


def dense_queries_keys(nc, k, ps, hd, x, qk, parts, weights, scale_bias):
    product_pass(nc, ps, 4, lambda i, bank: nc.tensor.matmul(bank, weights[i // 2], chunk(x, i % 2), start=True,
                                                             stop=True),
                 lambda on_act, i, bank: affine(nc, on_act, chunk(qk[:, i // 2], i % 2), bank, *scale_bias[i // 2]))
    split_parts(nc, k, [(qk[:, j], parts[:, j]) for j in range(2)])
    stack_parts(nc, k, hd, [parts[:, j] for j in range(2)])


def dense_values(nc, k, ps, hd, x, weights):
    share = 32 // hd

    def product(i, bank):
        for t in range(4):
            last = nc.tensor.matmul(bank[:, t * P:(t + 1) * P], chunk(x, 4 * i + t, P), weights, start=True, stop=True)
        return last

    def evacuate(on_act, i, bank):
        for j in range(share):
            heads = k.v_ext[:, 4 * i:4 * i + 4].rearrange("p t (g j) d -> p t g j d", j=share)[
                :, :, :, j, j * hd:(j + 1) * hd]
            last = affine(nc, on_act, heads, bank.rearrange("p (t g j d) -> p t g j d", t=4, j=share, d=hd)[:, :, :, j])
        return last

    product_pass(nc, ps, 2, product, evacuate)


@contextmanager
def dense_buffers(nc, k, hd):
    heads, share = P // hd, 32 // hd
    with ExitStack() as c:
        k.stacks = c.enter_context(sbuf(nc, "stacks", [P, 2, 8, N], BF16))
        k.v_ext = c.enter_context(sbuf(nc, "v_ext", [P, NT, heads, 64], F32))
        with stage(nc, "made", "zeroed") as (block, made, zeroed):
            @block.gpsimd
            def _(pool):
                nc.gpsimd.memset(k.stacks[STACK:STACK + 3, 1], 1.0).then_inc(made, 1)

            @block.vector
            def _(dve):
                nc.vector.memset(k.v_ext[:], 0.0).then_inc(zeroed, 1)
                dve.wait_ge(zeroed, 1)
                for j in range(share):
                    nc.vector.memset(k.v_ext[:].rearrange("p t (g j) d -> p (t g) j d", j=share)[
                        :, :, j, 32 + j * hd:32 + (j + 1) * hd], 1.0).then_inc(made, 1)
        yield


def add_value_bias(nc, o_cm, bias):
    with stage(nc, "by_act", "by_dve") as (block, by_act, by_dve):
        @block.scalar
        def _(act):
            affine(nc, True, chunk(o_cm, 0), chunk(o_cm, 0), 1.0, bias).then_inc(by_act, 1)

        @block.vector
        def _(dve):
            affine(nc, False, chunk(o_cm, 1), chunk(o_cm, 1), 1.0, bias).then_inc(by_dve, 1)



def attention_of_images(nc, k, b):
    with ExitStack() as c:
        def sb(name, shape):
            return c.enter_context(sbuf(nc, name, shape, F32))

        x, h = sb("l0_x", [P, N]), sb("l0_h", [P, N])
        copy_blocks(nc, [(x[:], k.x_cm[:, b, :])])
        group_norm(nc, k, x[:], h[:], k.mean16, k.cols[:, C_GN_G:C_GN_G + 1], k.cols[:, C_GN_B:C_GN_B + 1])
        with ExitStack() as c2:
            qk = c2.enter_context(sbuf(nc, "l0_qk", [P, 2, N], F32))
            o_cm = c2.enter_context(sbuf(nc, "l0_o", [P, N], F32))
            parts = c2.enter_context(sbuf(nc, "l0_parts", [P, 2, 3, N], BF16))
            with ExitStack() as c3:
                ps = c3.enter_context(psum(nc, "l0_ps", [P, 8, BANK], F32))
                dense_queries_keys(nc, k, ps, 32, h, qk, parts, [k.turned[:, i, :] for i in range(2)],
                                   [(32 ** -0.5, k.qb[:, 0:1]), (1.0, k.cols[:, C_QKV_B + 1:C_QKV_B + 2])])
                dense_values(nc, k, ps, 32, h, k.turned[:, 2, :])
            dense_attention(nc, k, 32, o_cm)
            with ExitStack() as c3:
                ps = c3.enter_context(psum(nc, "l0_ps", [P, 8, BANK], F32))
                add_value_bias(nc, o_cm, k.cols[:, C_QKV_B + 2:C_QKV_B + 3])
                product_pass(nc, ps, NC2, lambda i, bank: nc.tensor.matmul(
                    bank, k.turned[:, 3, :], chunk(o_cm, i), start=True, stop=True),
                    lambda on_act, i, bank: nc.vector.scalar_tensor_tensor(
                        chunk(x, i), bank, k.cols[:, C_PROJ_B:C_PROJ_B + 1], chunk(x, i), ALU.add, ALU.add), by="d")

        R = IMG + 4
        pad = sb("l1_pad", [P, R, R])
        with stage(nc, "cleared") as (block, cleared):
            @block.vector
            def _(dve):
                nc.vector.memset(pad[:], 0.0).then_inc(cleared, 1)
        group_norm(nc, k, x[:], pad[:, 2:2 + IMG, 2:2 + IMG], k.mean4, None, None)
        rows = BANK // IMG

        def window(s, n):
            i, j = divmod(s, 5)
            return pad[:, n * rows + i:n * rows + i + rows, j:j + IMG]

        def out(n, acc):
            return nc.vector.scalar_tensor_tensor(chunk(x, n), acc, k.cols[:, C_L1_B:C_L1_B + 1], chunk(x, n),
                                                  ALU.add, ALU.add)

        local_attention(nc, k, 25, 8, lambda n: window(12, n), window, window, k.heads16, k.spread16,
                        k.turned[:, 4, :], out)
        with ExitStack() as c2:
            ps = c2.enter_context(psum(nc, "l1_ps", [P, 8, BANK], F32))
            tm = c2.enter_context(sbuf(nc, "l1_tm", [P, NT, P], F32))
            turn_image(nc, k, ps, x, tm)
            copy_blocks(nc, [(k.t_tm[:, b], tm[:])])


def linear_attention(nc, k, b):
    with ExitStack() as c:
        def sb(name, shape):
            return c.enter_context(sbuf(nc, name, shape, F32))

        G = 16
        t_tm, xn, xc = sb("l2_t", [P, NT, P]), sb("l2_xn", [P, NT, P]), sb("l2_xc", [P, N])
        kv, sq = sb("l2_kv", [P, NT, 4 * P]), sb("l2_sq", [P, NT, 4 * P])
        st = sb("l2_st", [P, 2, NT * G])
        dots, mo, g = sb("l2_dots", [P, 2, P]), sb("l2_mo", [P, 2, P]), sb("l2_g", [P, P])
        ps = c.enter_context(psum(nc, "l2_ps", [P, 8, BANK], F32))
        copy_blocks(nc, [(t_tm[:], k.t_tm[:, b])])
        layer_norm(nc, k, t_tm, xn[:])
        turn_image(nc, k, ps, xn, xc)
        product_pass(nc, ps, NT, lambda i, bank: nc.tensor.matmul(bank, chunk(xc, i, P), k.w_kv[:], start=True, stop=True),
                     lambda on_act, i, bank: affine(nc, on_act, kv[:, i, :], bank))
        with stage(nc, "chained", "squared", "rooted") as (block, chained, squared, rooted):
            groups = kv[:].rearrange("p t (g d) -> p (t g) d", d=32)
            squares = sq[:].rearrange("p t (g d) -> p (t g) d", d=32)

            @block.vector
            def _(dve):
                link = linker(dve, chained)

                def wide(a):
                    return a.unsqueeze(2).broadcast_to([P, NT * G, 32])

                link(nc.vector.tensor_reduce(st[:, 0], groups, AX.X, ALU.add))
                link(nc.vector.tensor_scalar(st[:, 0], st[:, 0], 1.0 / 32, None, ALU.mult))
                link(nc.vector.tensor_tensor(groups, groups, wide(st[:, 0]), ALU.subtract))
                dve.wait_ge(squared, 1)
                link(nc.vector.tensor_reduce(st[:, 1], squares, AX.X, ALU.add))
                dve.wait_ge(rooted, 1)
                link(nc.vector.reciprocal(st[:, 1], st[:, 1]))
                link(nc.vector.tensor_tensor(groups, groups, wide(st[:, 1]), ALU.mult))

            @block.scalar
            def _(act):
                act.wait_ge(chained, 3)
                nc.scalar.activation(sq[:], kv[:], ACT.Square).then_inc(squared, 1)
                act.wait_ge(chained, 4)
                nc.scalar.activation(st[:, 1], st[:, 1], ACT.Sqrt, bias=k.eps[:, 0:1], scale=1.0 / 32).then_inc(rooted, 1)

        def dots_product(i, bank):
            for t in range(NT):
                last = nc.tensor.matmul(bank[:, 0:P], kv[:, t, (2 + i) * P:(3 + i) * P], kv[:, t, i * P:(i + 1) * P],
                                        start=(t == 0), stop=(t == NT - 1))
            return last

        product_pass(nc, ps, 2, dots_product, lambda on_act, i, bank: nc.vector.tensor_tensor(
            dots[:, i], bank[:, 0:P], k.block32[:], ALU.mult), by="d")
        product_pass(nc, ps, 2, lambda i, bank: nc.tensor.matmul(bank[:, 0:P], dots[:, i], k.w_o2[:, i], start=True,
                                                                 stop=True),
                     lambda on_act, i, bank: affine(nc, on_act, mo[:, i], bank[:, 0:P]))

        def g_product(i, bank):
            for j in range(2):
                last = nc.tensor.matmul(bank[:, 0:P], k.turned[:, k.t_q2 + j, :], mo[:, j], start=(j == 0), stop=(j == 1))
            return last

        product_pass(nc, ps, 1, g_product, lambda on_act, i, bank: affine(nc, on_act, g[:], bank[:, 0:P]))

        def out_product(i, bank):
            for t in range(4):
                o_ = bank[:, t * P:(t + 1) * P]
                nc.tensor.matmul(o_, chunk(xc, 4 * i + t, P), g[:], start=True, stop=False)
                last = nc.tensor.matmul(o_, k.ones_row[:], k.rows[0:1, 0, :], start=False, stop=True)
            return last

        product_pass(nc, ps, 2, out_product, lambda on_act, i, bank: nc.vector.tensor_tensor(
            t_tm[:, 4 * i:4 * i + 4].rearrange("p t n -> p (t n)"), bank,
            t_tm[:, 4 * i:4 * i + 4].rearrange("p t n -> p (t n)"), ALU.add), by="d")
        layer_norm(nc, k, t_tm, xn[:])
        turn_image(nc, k, ps, xn, xc)
        copy_blocks(nc, [(k.t_tm[:, b], t_tm[:]), (k.xn_cm[:, b], xc[:])])


def mixture_weights(nc, k):
    with ExitStack() as c:
        feat = c.enter_context(sbuf(nc, "mw_feat", [P, N], F32))
        s = c.enter_context(sbuf(nc, "mw_s", [P, 2, NT], F32))
        ps = c.enter_context(psum(nc, "mw_ps", [P, 8, BANK], F32))
        with stage(nc, "chained") as (block, chained):
            @block.vector
            def _(dve):
                link = linker(dve, chained)
                link(nc.vector.tensor_tensor(feat[:], k.xn_cm[:, 0], k.xn_cm[:, 1], ALU.add))
                for b in range(2, B):
                    link(nc.vector.tensor_tensor(feat[:], feat[:], k.xn_cm[:, b], ALU.add))
                link(nc.vector.tensor_scalar(feat[:], feat[:], 1.0 / B, None, ALU.mult))

        def product(i, bank):
            for t in range(NT):
                o_ = bank[:, t * E1:(t + 1) * E1]
                nc.tensor.matmul(o_, chunk(feat, t, P), k.wr[:], start=True, stop=False)
                last = nc.tensor.matmul(o_, k.ones_row[:], k.rows[0:1, 1, 0:E1], start=False, stop=True)
            return last

        product_pass(nc, ps, 1, product, lambda on_act, i, bank: affine(
            nc, on_act, k.mix[:].rearrange("p t e -> p (t e)"), bank[:, 0:NT * E1]))
        with stage(nc, "chained", "exped") as (block, chained, exped):
            @block.vector
            def _(dve):
                link = linker(dve, chained)
                link(nc.vector.tensor_reduce(s[:, 0], k.mix[:], AX.X, ALU.max))
                link(nc.vector.tensor_tensor(k.mix[:], k.mix[:], s[:, 0].unsqueeze(2).broadcast_to([P, NT, E1]),
                                             ALU.subtract))
                dve.wait_ge(exped, 1)
                link(nc.vector.tensor_reduce(s[:, 1], k.mix[:], AX.X, ALU.add))
                link(nc.vector.reciprocal(s[:, 1], s[:, 1]))
                link(nc.vector.tensor_tensor(k.mix[:], k.mix[:], s[:, 1].unsqueeze(2).broadcast_to([P, NT, E1]),
                                             ALU.mult))

            @block.scalar
            def _(act):
                act.wait_ge(chained, 2)
                nc.scalar.activation(k.mix[:], k.mix[:], ACT.Exp).then_inc(exped, 1)

        turn_tiles(nc, ps, k.ident, [([k.mix[:, t] for t in range(u, u + 4)],
                                      k.mix_t[:, u * P:(u + 4) * P].rearrange("p (k n) -> p k n", n=P)) for u in (0, 4)])


def mixture(nc, k, xc, t_tm, weight, weight_t, experts, bias, hidden, out_parts):
    with ExitStack() as c:
        ps = c.enter_context(psum(nc, "mx_ps", [P, 8, BANK], F32))

        def bias_product(i, bank):
            for t in range(4):
                last = nc.tensor.matmul(bank[:, t * P:(t + 1) * P], chunk(weight_t, 4 * i + t, P), bias, start=True,
                                        stop=True)
            return last

        product_pass(nc, ps, 2, bias_product, lambda on_act, i, bank: nc.vector.tensor_tensor(
            t_tm[:, 4 * i:4 * i + 4].rearrange("p t n -> p (t n)"), bank,
            t_tm[:, 4 * i:4 * i + 4].rearrange("p t n -> p (t n)"), ALU.add), by="d")

        n_h = hidden.n
        block, hidden_ready, hidden_off, out_ready, added = c.enter_context(
            stage(nc, "hidden_ready", "hidden_off", "out_ready", "added"))
        RING = 6

        @block.tensor
        def _(pe):
            for e in range(experts + 1):
                if e < experts:
                    for i in range(n_h):
                        g = e * n_h + i
                        if g >= RING:
                            pe.wait_ge(hidden_off, g - RING + 1)
                        need = hidden.needs(i)
                        if need is not None:
                            pe.wait_ge(hidden_off, e * n_h + need + 1)
                        hidden.product(e, i, ps[:, g % RING]).then_inc(hidden_ready, 1)
                if e >= 1:
                    for u in range(2):
                        o = 2 * (e - 1) + u
                        pe.wait_ge(hidden_off, e * n_h)
                        if o >= 2:
                            pe.wait_ge(added, 4 * (o - 1))
                        for t in range(4):
                            parts = out_parts(e - 1, 4 * u + t)
                            for j, (lhs, rhs) in enumerate(parts):
                                last = nc.tensor.matmul(ps[:, 6 + u, t * P:(t + 1) * P], lhs, rhs, start=(j == 0),
                                                        stop=(j == len(parts) - 1))
                        last.then_inc(out_ready, 1)

        @block.scalar
        def _(act):
            for e in range(experts):
                for i in range(n_h):
                    g = e * n_h + i
                    if i == 0 and e >= 2:
                        act.wait_ge(out_ready, 2 * (e - 1))
                    act.wait_ge(hidden_ready, g + 1)
                    hidden.evacuate(e, i, ps[:, g % RING]).then_inc(hidden_off, 1)

        @block.vector
        def _(dve):
            for e in range(experts):
                for u in range(2):
                    dve.wait_ge(out_ready, 2 * e + u + 1)
                    for t in range(4):
                        tt = 4 * u + t
                        if e >= 1:
                            dve.wait_ge(added, 8 * (e - 1) + tt + 1)
                        nc.vector.scalar_tensor_tensor(t_tm[:, tt], ps[:, 6 + u, t * P:(t + 1) * P],
                                                       weight[:, tt, e:e + 1], t_tm[:, tt], ALU.mult,
                                                       ALU.add).then_inc(added, 1)


class Hidden:

    def __init__(self, n, needs, product, evacuate):
        self.n, self.needs, self.product, self.evacuate = n, needs, product, evacuate


def batch_normed_mixture(nc, k, b):
    with ExitStack() as c:
        t_tm = c.enter_context(sbuf(nc, "bm_t", [P, NT, P], F32))
        xc = c.enter_context(sbuf(nc, "bm_x", [P, N], F32))
        h1 = c.enter_context(sbuf(nc, "bm_h1", [P, N], F32))
        h2 = c.enter_context(sbuf(nc, "bm_h2", [P, 2, N], F32))
        copy_blocks(nc, [(t_tm[:], k.t_tm[:, b]), (xc[:], k.xn_cm[:, b])])

        def product(e, i, bank):
            if i < 2:
                return nc.tensor.matmul(bank, k.m1[:, e], chunk(xc, i), start=True, stop=True)
            return nc.tensor.matmul(bank, k.m2[:, e], chunk(h1, i % 2), start=True, stop=True)

        def evacuate(e, i, bank):
            out = chunk(h1, i) if i < 2 else h2[:, e % 2, (i % 2) * BANK:(i % 2 + 1) * BANK]
            j = i // 2
            return nc.scalar.activation(out, bank, ACT.Relu, bias=k.bn[:, j, 1, e:e + 1], scale=k.bn[:, j, 0, e:e + 1])

        hidden = Hidden(4, lambda i: None if i < 2 else i - 2, product, evacuate)
        mixture(nc, k, xc, t_tm, k.mix, k.mix_t, E1, k.mo_b[:], hidden,
                lambda e, t: [(h2[:, e % 2, t * P:(t + 1) * P], k.mo[:, e])])
        copy_blocks(nc, [(k.t_tm[:, b], t_tm[:])])


def two_attentions(nc, k, b):
    with ExitStack() as c:
        def sb(name, shape):
            return c.enter_context(sbuf(nc, name, shape, F32))

        t_tm, xn, xc = sb("l3_t", [P, NT, P]), sb("l3_xn", [P, NT, P]), sb("l3_xc", [P, N])
        both = sb("l3_both", [P, 2, N])
        copy_blocks(nc, [(t_tm[:], k.t_tm[:, b])])
        layer_norm(nc, k, t_tm, xn[:])
        with ExitStack() as c2:
            ps = c2.enter_context(psum(nc, "l3_ps", [P, 8, BANK], F32))
            turn_image(nc, k, ps, xn, xc)
        with ExitStack() as c2:
            qk = c2.enter_context(sbuf(nc, "l3_qk", [P, 2, N], F32))
            o_cm = c2.enter_context(sbuf(nc, "l3_o", [P, N], F32))
            parts = c2.enter_context(sbuf(nc, "l3_parts", [P, 2, 3, N], BF16))
            with ExitStack() as c3:
                ps = c3.enter_context(psum(nc, "l3_ps", [P, 8, BANK], F32))
                dense_queries_keys(nc, k, ps, 16, xc, qk, parts, [k.turned[:, k.t_g_in + i, :] for i in range(2)],
                                   [(16 ** -0.5, k.qb[:, 1:2]), (1.0, k.cols[:, C_G_IN + 1:C_G_IN + 2])])
                dense_values(nc, k, ps, 16, xc, k.turned[:, k.t_g_in + 2, :])
            dense_attention(nc, k, 16, o_cm)
            with ExitStack() as c3:
                ps = c3.enter_context(psum(nc, "l3_ps", [P, 8, BANK], F32))
                add_value_bias(nc, o_cm, k.cols[:, C_G_IN + 2:C_G_IN + 3])
                product_pass(nc, ps, NC2, lambda i, bank: nc.tensor.matmul(
                    bank, k.turned[:, k.t_g_out, :], chunk(o_cm, i), start=True, stop=True),
                    lambda on_act, i, bank: affine(nc, on_act, chunk(both[:, 0], i), bank, 1.0,
                                                   k.cols[:, C_G_OUT:C_G_OUT + 1]))
        with ExitStack() as c2:
            q = c2.enter_context(sbuf(nc, "l3_q", [P, N], F32))
            pads = c2.enter_context(sbuf(nc, "l3_pads", [P, 2, N + 4], F32))
            with ExitStack() as c3:
                ps = c3.enter_context(psum(nc, "l3_ps", [P, 8, BANK], F32))
                with stage(nc, "cleared") as (block, cleared):
                    @block.vector
                    def _(dve):
                        nc.vector.memset(pads[:], 0.0).then_inc(cleared, 1)

                def evacuate(on_act, i, bank):
                    j = i // 2
                    if j == 0:
                        return affine(nc, on_act, chunk(q, i), bank, 32 ** -0.5, k.qb[:, 3:4])
                    out = pads[:, j - 1, 2 + (i % 2) * BANK:2 + (i % 2 + 1) * BANK]
                    return affine(nc, on_act, out, bank, 1.0, k.cols[:, C_T_IN + j:C_T_IN + j + 1])

                product_pass(nc, ps, 6, lambda i, bank: nc.tensor.matmul(
                    bank, k.turned[:, k.t_t_in + i // 2, :], chunk(xc, i % 2), start=True, stop=True), evacuate)

            def window(j):
                return lambda s, n: pads[:, j, s + n * BANK:s + (n + 1) * BANK]

            local_attention(nc, k, 5, 4, lambda n: chunk(q, n), window(0), window(1), k.heads32, k.spread32,
                            k.turned[:, k.t_t_out, :],
                            lambda n, acc: nc.vector.tensor_scalar(chunk(both[:, 1], n), acc,
                                                                   k.cols[:, C_T_OUT:C_T_OUT + 1], None, ALU.add),
                            mask=k.window_mask)
        ps = c.enter_context(psum(nc, "l3_ps", [P, 8, BANK], F32))
        hid = sb("l3_hid", [P, 2, N])
        x2 = sb("l3_x2", [P, NT, P])

        def two_layers(inputs, w1, bias1, w2, bias_row, residual):
            def product(i, bank):
                for j, x in enumerate(inputs):
                    last = nc.tensor.matmul(bank, k.turned[:, w1(i // 2, j), :], chunk(x, i % 2), start=(j == 0),
                                            stop=(j == len(inputs) - 1))
                return last

            def evacuate(on_act, i, bank):
                return nc.scalar.activation(chunk(hid[:, i // 2], i % 2), bank, ACT.Silu,
                                            bias=k.cols[:, bias1 + i // 2:bias1 + i // 2 + 1])

            product_pass(nc, ps, 4, product, evacuate, by="a")

            def out_product(i, bank):
                for t in range(4):
                    o_ = bank[:, t * P:(t + 1) * P]
                    for j in range(2):
                        nc.tensor.matmul(o_, chunk(hid[:, j], 4 * i + t, P), k.turned[:, w2 + j, :], start=(j == 0),
                                         stop=False)
                    last = nc.tensor.matmul(o_, k.ones_row[:], k.rows[0:1, bias_row, :], start=False, stop=True)
                return last

            product_pass(nc, ps, 2, out_product, lambda on_act, i, bank: nc.vector.tensor_tensor(
                residual[:, 4 * i:4 * i + 4].rearrange("p t n -> p (t n)"), bank,
                residual[:, 4 * i:4 * i + 4].rearrange("p t n -> p (t n)"), ALU.add), by="d")

        two_layers([both[:, 0], both[:, 1]], lambda half, j: k.t_fus1 + 2 * half + j, C_FUS1, k.t_fus2, 2, xn)
        layer_norm(nc, k, xn, x2[:], k.wide[:, 0], k.wide[:, 1])
        turn_image(nc, k, ps, x2, xc)
        two_layers([xc], lambda half, j: k.t_ffn1 + half, C_FFN1, k.t_ffn2, 3, x2)
        layer_norm(nc, k, x2, xn[:], k.wide[:, 2], k.wide[:, 3])
        with stage(nc, "added") as (block, added):
            @block.vector
            def _(dve):
                nc.vector.tensor_tensor(t_tm[:], t_tm[:], xn[:], ALU.add).then_inc(added, 1)
        layer_norm(nc, k, t_tm, xn[:])
        turn_image(nc, k, ps, xn, xc)
        h = sb("l3_h", [P, NT, GH * GE])

        def gat_product(i, bank):
            for t in range(NT):
                last = nc.tensor.matmul(bank[:, 16 * t:16 * t + 16], chunk(xc, t, P), k.w_gat[:], start=True, stop=True)
            return last

        product_pass(nc, ps, 1, gat_product, lambda on_act, i, bank: affine(
            nc, on_act, h[:].rearrange("p t f -> p (t f)"), bank[:, 0:NT * 16]))
        copy_blocks(nc, [(k.t_tm[:, b], t_tm[:]), (k.xn_cm[:, b], xc[:]), (k.h_tm[:, b], h[:])])


def gelu_mixture(nc, k, b, out):
    with ExitStack() as c:
        t_tm = c.enter_context(sbuf(nc, "gm_t", [P, NT, P], F32))
        xc = c.enter_context(sbuf(nc, "gm_x", [P, N], F32))
        hid = c.enter_context(sbuf(nc, "gm_h", [P, 2, 2, N], F32))
        gates = c.enter_context(sbuf(nc, "gm_g", [P, NT, E2], F32))
        gates_t = c.enter_context(sbuf(nc, "gm_gt", [E2, N], F32))
        copy_blocks(nc, [(t_tm[:], k.t_tm[:, b]), (xc[:], k.xn_cm[:, b]), (gates[:], k.gates[:, b])])
        with ExitStack() as c2:
            ps = c2.enter_context(psum(nc, "gm_ps", [P, 8, BANK], F32))
            turn_tiles(nc, ps, k.ident, [([gates[:, t] for t in range(u, u + 4)],
                                          gates_t[:, u * P:(u + 4) * P].rearrange("p (k n) -> p k n", n=P)) for u in (0, 4)])

        def product(e, i, bank):
            half, n = divmod(i, 2)
            return nc.tensor.matmul(bank, k.x1[:, e, half * P:(half + 1) * P], chunk(xc, n), start=True, stop=True)

        def evacuate(e, i, bank):
            half, n = divmod(i, 2)
            return nc.scalar.activation(chunk(hid[:, e % 2, half], n), bank, ACT.Gelu,
                                        bias=k.cols[:, C_B1 + 2 * e + half:C_B1 + 2 * e + half + 1])

        hidden = Hidden(4, lambda i: None, product, evacuate)
        mixture(nc, k, xc, t_tm, gates, gates_t, E2, k.x2_b[:], hidden,
                lambda e, t: [(hid[:, e % 2, s, t * P:(t + 1) * P], k.x2[:, e, s]) for s in range(2)])
        with ExitStack() as c2:
            ps = c2.enter_context(psum(nc, "gm_ps2", [P, 8, BANK], F32))
            turn_image(nc, k, ps, t_tm, xc)
        with stage(nc, "stored") as (block, stored):
            @block.sync
            def _(sp):
                sp.dma_start(out[b].rearrange("c h w -> c (h w)"), xc[:]).then_inc(stored, 16)
                sp.wait_ge(stored, 16)



ROUNDS = 12
LIST = 8 * ROUNDS
SLOTS = 16
FEAT = GH + GH * GE
PIECE = 1024
SUB = 128
CLASSES = 8


def code_edges(nc, k, e):
    ends = e.edge_index.rearrange("s (p n) -> s p n", p=P)
    with ExitStack() as c:
        raw = c.enter_context(sbuf(nc, "ce_raw", [P, 2, PIECE], I32))
        a = c.enter_context(sbuf(nc, "ce_a", [P, 2, PIECE], I32))
        f = c.enter_context(sbuf(nc, "ce_f", [P, 3, PIECE], F32))
        with nc.Fori(0, EW // PIECE) as i:
            with stage(nc, "loaded", "chained") as (block, loaded, chained):
                @block.sync
                def _(sp):
                    for s in range(2):
                        sp.dma_start(raw[:, s], ends[s, :, bass.ds(i * PIECE, PIECE)]).then_inc(loaded, 16)

                @block.vector
                def _(dve):
                    link = linker(dve, chained)
                    src, dst = raw[:, 0], raw[:, 1]
                    piece = bass.ds(i * PIECE, PIECE)
                    dve.wait_ge(loaded, 32)
                    link(nc.vector.tensor_scalar(a[:, 0], dst, P - 1, 17, ALU.bitwise_and, ALU.logical_shift_left))
                    link(nc.vector.tensor_scalar(a[:, 1], dst, 7, 12, ALU.logical_shift_right, ALU.logical_shift_left))
                    link(nc.vector.tensor_tensor(a[:, 0], a[:, 0], a[:, 1], ALU.bitwise_or))
                    link(nc.vector.tensor_scalar(a[:, 1], src, float(M - 1), None, ALU.min))
                    link(nc.vector.scalar_tensor_tensor(f[:, 0], a[:, 0], 1.0, a[:, 1], ALU.add, ALU.add))
                    link(nc.vector.tensor_scalar(f[:, 1], dst, float(M), None, ALU.is_lt))
                    link(nc.vector.scalar_tensor_tensor(f[:, 2], src, float(M - 1), f[:, 1], ALU.is_lt, ALU.mult))
                    link(nc.vector.tensor_tensor(e.codes[:, piece], f[:, 0], f[:, 2], ALU.mult))
                    link(nc.vector.tensor_tensor(f[:, 1], f[:, 1], f[:, 2], ALU.subtract))
                    link(nc.vector.tensor_scalar(a[:, 0], dst, 63, None, ALU.bitwise_and))
                    link(nc.vector.tensor_scalar(a[:, 1], dst, 6, None, ALU.logical_shift_right))
                    for d in range(2):
                        link(nc.vector.scalar_tensor_tensor(e.digits[:, d, piece], a[:, d], 1.0, f[:, 1], ALU.add,
                                                            ALU.mult))


def count_last(nc, k, e):
    with ExitStack() as c:
        hot = c.enter_context(sbuf(nc, "cl_hot", [P, 2, 2, 2, 64, SUB // 2], BF16))
        total = c.enter_context(sbuf(nc, "cl_total", [P, P], F32))
        fold = c.enter_context(sbuf(nc, "cl_fold", [P, 64], F32))
        place = c.enter_context(sbuf(nc, "cl_place", [P, 2, P], F32))
        ps = c.enter_context(psum(nc, "cl_ps", [P, BANK], F32))
        ps2 = c.enter_context(psum(nc, "cl_ps2", [P, BANK], F32))
        with stage(nc, "made") as (block, made):
            @block.gpsimd
            def _(pool):
                link = linker(pool, made)
                link(nc.gpsimd.memset(total[:], 0.0))
                link(nc.gpsimd.memset(place[:], 0.0))
                for odd in range(2):
                    for half in range(2):
                        v = place[:, odd, :]
                        link(nc.gpsimd.affine_select(out=v, in_=v, compare_op=ALU.not_equal, fill=1.0,
                                                     base=64 * (odd - half), pattern=[[-1, P]], channel_multiplier=1))
                    v = place[:, odd, 64 * (1 - odd):64 * (2 - odd)]
                    link(nc.gpsimd.memset(v, 0.0))
        per = 4
        with nc.Fori(0, EW // (per * SUB)) as i:
            with stage(nc, "hot_ready", "multiplied", "added") as (block, hot_ready, multiplied, added):
                @block.vector
                def _(dve):
                    for s in range(per):
                        if s >= 2:
                            dve.wait_ge(multiplied, s - 1)
                        for d in range(2):
                            for v in range(64):
                                nc.vector.tensor_scalar(hot[:, s % 2, d, :, v, :], e.digits[:, d, bass.ds(
                                    (i * per + s) * SUB, SUB)].rearrange("p (a m) -> p a m", a=2),
                                                        float(v + 1), None, ALU.is_equal).then_inc(hot_ready, 1)
                    dve.wait_ge(multiplied, per)
                    nc.vector.tensor_tensor(total[:], total[:], ps[:, 0:P], ALU.add).then_inc(added, 1)

                @block.tensor
                def _(pe):
                    for s in range(per):
                        pe.wait_ge(hot_ready, 128 * (s + 1))
                        for m in range(SUB // 2):
                            low, high = (hot[:, s % 2, d, :, :, m].rearrange("p a v -> p (a v)") for d in range(2))
                            last = nc.tensor.matmul(ps[:, 0:P], low, high, start=(s == 0 and m == 0),
                                                    stop=(s == per - 1 and m == SUB // 2 - 1))
                        last.then_inc(multiplied, 1)
        with stage(nc, "folded", "placed", "copied") as (block, folded, placed, copied):
            @block.tensor
            def _(pe):
                pe.wait_ge(folded, 2)
                for odd in range(2):
                    rhs = fold[:].rearrange("p (t o) -> p o t", o=2)[:, odd, :]
                    last = nc.tensor.matmul(ps2[:, 0:MT], place[:, odd, :], rhs, start=(odd == 0), stop=(odd == 1))
                last.then_inc(placed, 1)

            @block.vector
            def _(dve):
                for half in range(2):
                    r = slice(64 * half, 64 * half + 64)
                    nc.vector.tensor_copy(fold[r, :], total[r, 64 * half:64 * half + 64]).then_inc(folded, 1)
                dve.wait_ge(placed, 1)
                nc.vector.tensor_copy(e.count[:], ps2[:, 0:MT]).then_inc(copied, 1)


def largest_count(nc, e, candidates, low, scratch):
    with stage(nc, "counted", "reduced", "whole") as (block, counted, reduced, whole):
        @block.vector
        def _(dve):
            nc.vector.tensor_scalar(scratch, candidates, low, None, ALU.is_gt, ALU.add,
                                    accum_out=e.most[:, 0:1]).then_inc(counted, 1)
            dve.wait_ge(reduced, 1)
            nc.vector.tensor_copy(e.most_int[:], e.most[:, 1:2]).then_inc(whole, 1)

        @block.gpsimd
        def _(pool):
            pool.wait_ge(counted, 1)
            nc.gpsimd.partition_all_reduce(e.most[:, 1:2], e.most[:, 0:1], P,
                                           bass.bass_isa.ReduceOp.max).then_inc(reduced, 1)
    return nc.values_load(e.most_int[0:1, 0:1], min_val=0, max_val=EDGES)


def take_largest(nc, link, candidates, out, rounds):
    for r in range(rounds):
        o_ = out[:, 8 * r:8 * r + 8]
        link(nc.vector.max(o_, candidates))
        link(nc.vector.match_replace(candidates, o_, candidates, 0.0))


def gather_lists(nc, e, source, lists, candidates, high, spread):
    with stage(nc, "chained", "stored", "loaded") as (block, chained, stored, loaded):
        @block.vector
        def _(dve):
            link = linker(dve, chained)
            take_largest(nc, link, source, e.list[:], ROUNDS)
            dve.wait_ge(loaded, 16 * CLASSES)
            link(nc.vector.scalar_tensor_tensor(candidates, candidates, high, candidates, ALU.is_le, ALU.mult))

        @block.sync
        def _(sp):
            sp.wait_ge(chained, 2 * ROUNDS)
            sp.dma_start(lists, e.list[:]).then_inc(stored, 16)
            sp.wait_ge(stored, 16)
            for c in range(CLASSES):
                sp.dma_start(candidates[16 * c:16 * c + 16, :], spread(lists, c)).then_inc(loaded, 16)


def take_in(nc, k, e, candidates):
    with ExitStack() as c:
        def sb(name, shape, dt=F32):
            return c.enter_context(sbuf(nc, name, shape, dt))

        code, f = sb("ti_code", [P, SLOTS]), sb("ti_f", [P, 3, SLOTS])
        whole = sb("ti_int", [P, 3, SLOTS], I32)
        row = sb("ti_row", [P, SLOTS, FEAT])
        hot, z, p, y = sb("ti_hot", [P, MT, SLOTS]), sb("ti_z", [P, GH, MT, SLOTS]), sb("ti_p", [P, GH, MT, SLOTS]), sb(
            "ti_y", [P, GH, MT, SLOTS])
        n = sb("ti_new", [P, 4, GH, MT])
        block, chained, indexed, gathered, shifted, exped = c.enter_context(
            stage(nc, "chained", "indexed", "gathered", "shifted", "exped", pool_dma=True))

        @block.vector
        def _(dve):
            link = linker(dve, chained)
            take_largest(nc, link, candidates, code, SLOTS // 8)
            valid, local, tile = (f[:, i] for i in range(3))
            link(nc.vector.tensor_scalar(valid, code[:], e.bounds[:, 2:3], None, ALU.is_gt))
            link(nc.vector.tensor_scalar(local, code[:], e.bounds[:, 2:3], -1.0, ALU.subtract, ALU.add))
            link(nc.vector.tensor_tensor(local, local, valid, ALU.mult))
            link(nc.vector.tensor_copy(whole[:, 0], local))
            nc.vector.tensor_scalar(whole[:, 1], whole[:, 0], M - 1, None, ALU.bitwise_and).then_inc(indexed, 1)
            link(nc.vector.tensor_scalar(whole[:, 2], whole[:, 0], 12, None, ALU.logical_shift_right))
            link(nc.vector.tensor_copy(tile, whole[:, 2]))
            link(nc.vector.scalar_tensor_tensor(tile, tile, 1.0, valid, ALU.add, ALU.mult))
            link(nc.vector.tensor_tensor(hot[:], e.tiles[:].unsqueeze(2).broadcast_to([P, MT, SLOTS]),
                                         tile.unsqueeze(1).broadcast_to([P, MT, SLOTS]), ALU.is_equal))
            link(nc.vector.tensor_scalar(hot[:], hot[:], -NEG, NEG, ALU.mult, ALU.add))
            dve.wait_ge(gathered, 16 * SLOTS)
            score = row[:, :, 0:GH].rearrange("p j h -> p h j")

            def zh(h):
                return z[:, h]

            for h in range(GH):
                link(nc.vector.tensor_tensor(zh(h), hot[:], score[:, h].unsqueeze(1).broadcast_to([P, MT, SLOTS]), ALU.add))
            z3 = z[:].rearrange("p h t j -> p (h t) j")
            flat = [n[:, i].rearrange("p h t -> p (h t)") for i in range(4)]
            top, shift = e.top[:].rearrange("p h t -> p (h t)"), e.shift[:].rearrange("p h t -> p (h t)")
            a_dst = e.a_dst[:].rearrange("p h t -> p (h t)")

            def wide(a):
                return a.unsqueeze(2).broadcast_to([P, GH * MT, SLOTS])

            link(nc.vector.tensor_reduce(flat[0], z3, AX.X, ALU.max))
            link(nc.vector.tensor_tensor(top, top, flat[0], ALU.max))
            link(nc.vector.tensor_tensor(flat[0], top, a_dst, ALU.add))
            link(nc.vector.scalar_tensor_tensor(flat[0], flat[0], 0.2, flat[0], ALU.mult, ALU.max))
            link(nc.vector.tensor_tensor(flat[1], shift, flat[0], ALU.subtract))
            link(nc.vector.tensor_copy(shift, flat[0]))
            link(nc.vector.tensor_tensor(z3, z3, wide(a_dst), ALU.add))
            link(nc.vector.scalar_tensor_tensor(z3, z3, 0.2, z3, ALU.mult, ALU.max))
            nc.vector.tensor_tensor(z3, z3, wide(shift), ALU.subtract).then_inc(shifted, 1)
            dve.wait_ge(exped, 2)
            p3 = p[:].rearrange("p h t j -> p (h t) j")
            den = e.den[:].rearrange("p h t -> p (h t)")
            link(nc.vector.tensor_reduce(flat[2], p3, AX.X, ALU.add))
            link(nc.vector.tensor_tensor(den, den, flat[1], ALU.mult))
            link(nc.vector.tensor_tensor(den, den, flat[2], ALU.add))
            for v in range(GE):
                num = e.num[:, v].rearrange("p h t -> p (h t)")
                for h in range(GH):
                    value = row[:, :, GH + h * GE + v].unsqueeze(1).broadcast_to([P, MT, SLOTS])
                    link(nc.vector.tensor_tensor(y[:, h], p[:, h], value, ALU.mult))
                link(nc.vector.tensor_reduce(flat[3], y[:].rearrange("p h t j -> p (h t) j"), AX.X, ALU.add))
                link(nc.vector.tensor_tensor(num, num, flat[1], ALU.mult))
                link(nc.vector.tensor_tensor(num, num, flat[3], ALU.add))

        @block.gpsimd
        def _(pool):
            pool.wait_ge(indexed, 1)
            for j in range(SLOTS):
                nc.gpsimd.indirect_dma_start(row[:, j, :], None, e.features, bass.IndirectOffsetOnAxis(
                    ap=whole[:, 1, j:j + 1], axis=0)).then_inc(gathered, 16)
            pool.wait_ge(gathered, 16 * SLOTS)

        @block.scalar
        def _(act):
            act.wait_ge(shifted, 1)
            flat = n[:, 1].rearrange("p h t -> p (h t)")
            nc.scalar.activation(flat, flat, ACT.Exp).then_inc(exped, 1)
            nc.scalar.activation(p[:], z[:], ACT.Exp).then_inc(exped, 1)


def start_sums(nc, k, e):
    with ExitStack() as c:
        def sb(name, shape, dt=F32):
            return c.enter_context(sbuf(nc, name, shape, dt))

        prod = sb("ss_prod", [P, MT, GH * GE])
        rows = sb("ss_rows", [P, MT, FEAT])
        last_row = sb("ss_last", [P, FEAT])
        n = sb("ss_n", [P, 4, GH, MT])
        block, chained, stored, loaded, exped = c.enter_context(stage(nc, "chained", "stored", "loaded", "exped"))
        h3 = k.h_tm[:].rearrange("p b t f -> p (b t) f")
        own, last, e_own, e_last = (n[:, i] for i in range(4))

        @block.vector
        def _(dve):
            link = linker(dve, chained)
            for i in range(2):
                link(nc.vector.tensor_tensor(prod[:], h3, k.gat[:, 3 + i].unsqueeze(1).broadcast_to([P, MT, GH * GE]),
                                             ALU.mult))
                out = (own if i == 0 else e.a_dst[:]).rearrange("p h t -> p t h")
                link(nc.vector.tensor_reduce(out, prod[:].rearrange("p t (h v) -> p t h v", v=GE), AX.X, ALU.add))
            link(nc.vector.tensor_copy(rows[:, :, 0:GH], own.rearrange("p h t -> p t h")))
            link(nc.vector.tensor_copy(rows[:, :, GH:FEAT], h3))
            dve.wait_ge(loaded, 16)
            link(nc.vector.tensor_scalar(last[:, 0], e.count[:], 0.5, NEG, ALU.is_lt, ALU.mult))
            for h in range(GH - 1, -1, -1):
                link(nc.vector.tensor_scalar(last[:, h], last[:, 0], last_row[:, h:h + 1], None, ALU.add))
            link(nc.vector.tensor_tensor(e.top[:], own, last, ALU.max))
            for x, out in ((own, e_own), (last, e_last), (e.top[:], e.shift[:])):
                link(nc.vector.tensor_tensor(out, x, e.a_dst[:], ALU.add))
                link(nc.vector.scalar_tensor_tensor(out, out, 0.2, out, ALU.mult, ALU.max))
            for x in (e_own, e_last):
                link(nc.vector.tensor_tensor(x, x, e.shift[:], ALU.subtract))
            dve.wait_ge(exped, 1)
            link(nc.vector.tensor_tensor(e_last, e_last, e.count[:].unsqueeze(1).broadcast_to([P, GH, MT]), ALU.mult))
            link(nc.vector.tensor_tensor(e.den[:], e_own, e_last, ALU.add))
            for v in range(GE):
                value = h3.rearrange("p t (h v) -> p v h t", v=GE)[:, v]
                link(nc.vector.tensor_tensor(e.num[:, v], e_own, value, ALU.mult))
                for h in range(GH):
                    link(nc.vector.scalar_tensor_tensor(e.num[:, v, h], e_last[:, h],
                                                        last_row[:, GH + h * GE + v:GH + h * GE + v + 1],
                                                        e.num[:, v, h], ALU.mult, ALU.add))

        @block.sync
        def _(sp):
            sp.wait_ge(chained, 6)
            sp.dma_start(e.features.rearrange("(t p) f -> p t f", p=P), rows[:]).then_inc(stored, 16)
            sp.wait_ge(stored, 16)
            sp.dma_start(last_row[:], e.features[M - 1].partition_broadcast(P)).then_inc(loaded, 16)

        @block.scalar
        def _(act):
            act.wait_ge(chained, 6 + 1 + GH + 1 + 6 + 2)
            nc.scalar.activation(n[:, 2:4], n[:, 2:4], ACT.Exp).then_inc(exped, 1)


def choose_experts(nc, k, e):
    with ExitStack() as c:
        def sb(name, shape):
            return c.enter_context(sbuf(nc, name, shape, F32))

        agg, sq = sb("ch_agg", [P, MT, GH * GE]), sb("ch_sq", [P, MT, GH * GE])
        st = sb("ch_st", [P, 6, MT])
        s, rank = sb("ch_s", [P, GE, MT]), sb("ch_rank", [P, GE, MT])
        block, chained, rooted, exped, final = c.enter_context(stage(nc, "chained", "rooted", "exped", "final"))

        @block.vector
        def _(dve):
            link = linker(dve, chained)
            link(nc.vector.tensor_scalar(e.den[:], e.den[:], 1e-16, None, ALU.add))
            link(nc.vector.reciprocal(e.den[:], e.den[:]))
            for v in range(GE):
                out = agg[:].rearrange("p t (h v) -> p v h t", v=GE)[:, v]
                link(nc.vector.tensor_tensor(out, e.num[:, v], e.den[:], ALU.mult))

            def param(i):
                return k.gat[:, i].unsqueeze(1).broadcast_to([P, MT, GH * GE])

            def wide(a):
                return a.unsqueeze(2).broadcast_to([P, MT, GH * GE])

            link(nc.vector.tensor_tensor(agg[:], agg[:], param(0), ALU.add))
            link(nc.vector.tensor_reduce(st[:, 0], agg[:], AX.X, ALU.add))
            link(nc.vector.tensor_scalar(st[:, 0], st[:, 0], 1.0 / 16, None, ALU.mult))
            link(nc.vector.tensor_tensor(agg[:], agg[:], wide(st[:, 0]), ALU.subtract))
            link(nc.vector.tensor_tensor(sq[:], agg[:], agg[:], ALU.mult))
            link(nc.vector.tensor_reduce(st[:, 1], sq[:], AX.X, ALU.add))
            dve.wait_ge(rooted, 1)
            link(nc.vector.reciprocal(st[:, 1], st[:, 1]))
            link(nc.vector.tensor_tensor(agg[:], agg[:], wide(st[:, 1]), ALU.mult))
            link(nc.vector.tensor_tensor(agg[:], agg[:], param(1), ALU.mult))
            link(nc.vector.tensor_tensor(agg[:], agg[:], param(2), ALU.add))
            link(nc.vector.tensor_reduce(s[:].rearrange("p v t -> p t v"), agg[:].rearrange("p t (h v) -> p t v h", v=GE),
                                         AX.X, ALU.add))
            link(nc.vector.tensor_scalar(s[:], s[:], 1.0 / GH, None, ALU.mult))
            for i in range(GE):
                link(nc.vector.memset(rank[:, i], float(GE - 1 - i)))
            for i in range(GE):
                for j in range(i + 1, GE):
                    link(nc.vector.tensor_tensor(st[:, 2], s[:, i], s[:, j], ALU.is_ge))
                    link(nc.vector.tensor_tensor(rank[:, j], rank[:, j], st[:, 2], ALU.add))
                    link(nc.vector.tensor_tensor(rank[:, i], rank[:, i], st[:, 2], ALU.subtract))
            link(nc.vector.tensor_scalar(rank[:], rank[:], 1.5, None, ALU.is_lt))
            link(nc.vector.tensor_reduce(st[:, 3], s[:].rearrange("p v t -> p t v"), AX.X, ALU.max))
            nc.vector.tensor_tensor(s[:], s[:], st[:, 3].unsqueeze(1).broadcast_to([P, GE, MT]), ALU.subtract).then_inc(final, 1)
            dve.wait_ge(exped, 1)
            link(nc.vector.tensor_tensor(s[:], s[:], rank[:], ALU.mult))
            link(nc.vector.tensor_reduce(st[:, 4], s[:].rearrange("p v t -> p t v"), AX.X, ALU.add))
            link(nc.vector.reciprocal(st[:, 4], st[:, 4]))
            link(nc.vector.tensor_tensor(k.gates[:].rearrange("p b t v -> p v (b t)"), s[:],
                                         st[:, 4].unsqueeze(1).broadcast_to([P, GE, MT]), ALU.mult))

        @block.scalar
        def _(act):
            act.wait_ge(chained, 2 + GE + 6)
            nc.scalar.activation(st[:, 1], st[:, 1], ACT.Sqrt, bias=k.eps[:, 0:1], scale=1.0 / 16).then_inc(rooted, 1)
            act.wait_ge(final, 1)
            nc.scalar.activation(s[:], s[:], ACT.Exp).then_inc(exped, 1)


class Edges:
    pass


def route(nc, k, edge_index):
    with ExitStack() as c:
        def sb(name, shape, dt=F32):
            return c.enter_context(sbuf(nc, name, shape, dt))

        e = Edges()
        e.edge_index = edge_index
        e.codes = sb("codes", [P, EW])
        e.count = sb("count", [P, MT])
        e.list = sb("list", [P, LIST])
        e.most, e.most_int = sb("most", [P, 2]), sb("most_int", [P, 1], I32)
        e.bounds = sb("bounds", [P, 4])
        bounds_int = sb("bounds_int", [P, 2], I32)
        e.tiles = sb("tiles", [P, MT])
        e.features = nc.dram_tensor("features", [M, FEAT], F32).ap()
        lists = [nc.dram_tensor(f"lists_{i}", [P, LIST], F32).ap() for i in range(2)]
        with ExitStack() as c2:
            e.digits = c2.enter_context(sbuf(nc, "digits", [P, 2, EW], BF16))
            code_edges(nc, k, e)
            count_last(nc, k, e)
        e.top, e.shift, e.den, e.a_dst = (sb(f"gat_{n}", [P, GH, MT]) for n in ("top", "shift", "den", "a_dst"))
        e.num = sb("gat_num", [P, GE, GH, MT])
        by_class = sb("by_class", [P, CLASSES * LIST])
        by_owner = sb("by_owner", [P, 16 * LIST])
        scratch = sb("count_scratch", [P, EW])

        with stage(nc, "made", "chained") as (block, made, chained):
            @block.gpsimd
            def _(pool):
                nc.gpsimd.iota(bounds_int[:, 0:1], [[0, 1]], base=0, channel_multiplier=1 << 17).then_inc(made, 1)
                nc.gpsimd.iota(e.tiles[:], [[1, MT]], base=1, channel_multiplier=0,
                               allow_small_or_imprecise_dtypes=True).then_inc(made, 1)

            @block.vector
            def _(dve):
                link = linker(dve, chained)
                dve.wait_ge(made, 2)
                link(nc.vector.tensor_copy(e.bounds[:, 2:3], bounds_int[:, 0:1]))
                link(nc.vector.tensor_scalar(e.bounds[:, 3:4], e.bounds[:, 2:3], float(1 << 17), None, ALU.add))
                link(nc.vector.tensor_scalar(bounds_int[:, 1:2], bounds_int[:, 0:1], 21, 21, ALU.logical_shift_right,
                                             ALU.logical_shift_left))
                link(nc.vector.tensor_copy(e.bounds[:, 0:1], bounds_int[:, 1:2]))
                link(nc.vector.tensor_scalar(e.bounds[:, 1:2], e.bounds[:, 0:1], float(1 << 21), None, ALU.add))

        start_sums(nc, k, e)

        def to_class(lists, c):
            return lists.rearrange("(j q) n -> j (q n)", q=CLASSES)

        def to_owners(lists, c):
            return lists[16 * c:16 * c + 16, :].rearrange("j n -> (j n)").partition_broadcast(16)

        most = largest_count(nc, e, e.codes[:], 0.5, scratch[:])
        with nc.Fori(0, most, LIST):
            gather_lists(nc, e, e.codes[:], lists[0], by_class[:], e.bounds[:, 1:2], to_class)
            most_a = largest_count(nc, e, by_class[:], e.bounds[:, 0:1], scratch[:, 0:CLASSES * LIST])
            with nc.Fori(0, most_a, LIST):
                gather_lists(nc, e, by_class[:], lists[1], by_owner[:], e.bounds[:, 3:4], to_owners)
                most_b = largest_count(nc, e, by_owner[:], e.bounds[:, 2:3], scratch[:, 0:16 * LIST])
                with nc.Fori(0, most_b, SLOTS):
                    take_in(nc, k, e, by_owner[:])
        choose_experts(nc, k, e)



class Kept:
    pass


def build(nc, w, out):
    with ExitStack() as c:
        def sb(name, shape, dt=F32):
            return c.enter_context(sbuf(nc, name, shape, dt))

        k = Kept()
        k.xn_cm = sb("xn_cm", [P, B, N])
        k.t_tm = sb("t_tm", [P, B, NT, P])
        k.h_tm, k.gates = sb("h_tm", [P, B, NT, GH * GE]), sb("gates", [P, B, NT, E2])
        k.ident, k.mean16, k.mean4, k.block32 = (sb(n, [P, P]) for n in ("ident", "mean16", "mean4", "block32"))
        k.heads16, k.heads32 = sb("heads16", [P, 8]), sb("heads32", [P, 4])
        k.spread16, k.spread32 = sb("spread16", [P, 16 * P]), sb("spread32", [20, 5 * P])
        k.ones_row, k.eps, k.window_mask = sb("ones_row", [1, P]), sb("eps", [P, 2]), sb("window_mask", [P, NT, 5])
        k.turned = sb("turned", [P, 25, P])
        k.t_g_in, k.t_g_out, k.t_t_in, k.t_t_out, k.t_fus1, k.t_fus2, k.t_ffn1, k.t_ffn2, k.t_q2 = (
            5, 8, 9, 12, 13, 17, 19, 21, 23)
        k.cols, k.qb, k.bn = sb("cols", [P, P]), sb("qb", [P, 4]), sb("bn", [P, 2, 2, E1])
        k.ident_b = sb("ident_b", [P, P], BF16)
        k.parts_dram = nc.dram_tensor("parts_dram", [2, 3, P, N], BF16).ap()
        k.stacked = [c.enter_context(nc.semaphore(f"stacked_{g}")) for g in range(2)]
        k.w_kv, k.w_o2 = sb("w_kv", [P, 4 * P]), sb("w_o2", [P, 2, P])
        k.m1, k.m2, k.mo = (sb(n, [P, E1, P]) for n in ("m1", "m2", "mo"))
        k.mo_b, k.wr, k.mix, k.mix_t = sb("mo_b", [E1, P]), sb("wr", [P, E1]), sb("mix", [P, NT, E1]), sb("mix_t", [E1, N])
        k.w_gat, k.gat = sb("w_gat", [P, GH * GE]), sb("gat", [P, 5, GH * GE])
        k.x1, k.x2, k.x2_b = sb("x1", [P, E2, 2 * P]), sb("x2", [P, E2, 2, P]), sb("x2_b", [E2, P])
        k.rows, k.wide = sb("rows", [1, 4, P]), sb("wide", [P, 4, P])

        with ExitStack() as c2:
            k.x_cm = c2.enter_context(sbuf(nc, "x_cm", [P, B, N], F32))
            make_constants(nc, k)
            load_weights(nc, k, w)
            with dense_buffers(nc, k, 32), nc.Fori(0, B) as b:
                attention_of_images(nc, k, b)
        with nc.Fori(0, B) as b:
            linear_attention(nc, k, b)
        mixture_weights(nc, k)
        with nc.Fori(0, B) as b:
            batch_normed_mixture(nc, k, b)
        with dense_buffers(nc, k, 16), nc.Fori(0, B) as b:
            two_attentions(nc, k, b)
        route(nc, k, w["L3_ffn_edge_index"])
        with nc.Fori(0, B) as b:
            gelu_mixture(nc, k, b, out)



NAMES = """x L0_conv_gn_gamma L0_conv_gn_beta L0_conv_qkv_w L0_conv_qkv_b L0_conv_proj_w L0_conv_proj_b L1_conv_w_out
L1_conv_b_out L2_attn_w_qkv L2_attn_w_out L2_attn_b_out L2_ffn_Wr L2_ffn_br L2_ffn_W1 L2_ffn_b1 L2_ffn_g1 L2_ffn_be1
L2_ffn_m1 L2_ffn_v1 L2_ffn_W2 L2_ffn_b2 L2_ffn_g2 L2_ffn_be2 L2_ffn_m2 L2_ffn_v2 L2_ffn_Wo L2_ffn_bo L3_attn_g_in_w
L3_attn_g_in_b L3_attn_g_out_w L3_attn_g_out_b L3_attn_t_in_w L3_attn_t_in_b L3_attn_t_out_w L3_attn_t_out_b
L3_attn_fus_w1 L3_attn_fus_b1 L3_attn_fus_w2 L3_attn_fus_b2 L3_attn_ffn_w1 L3_attn_ffn_b1 L3_attn_ffn_w2
L3_attn_ffn_b2 L3_attn_gn_g L3_attn_gn_b L3_attn_fn_g L3_attn_fn_b L3_ffn_W_gat L3_ffn_att_src L3_ffn_att_dst
L3_ffn_b_gat L3_ffn_ln_gamma L3_ffn_ln_beta L3_ffn_W1 L3_ffn_b1 L3_ffn_W2 L3_ffn_b2 L3_ffn_edge_index""".split()


def kernel(**inputs):
    import numpy as np
    import concourse.bacc as bacc
    from concourse.bass_utils import run_bass_kernel_spmd

    nc = bacc.Bacc("TRN2", target_bir_lowering=False, num_devices=1)
    arrays = {name: np.ascontiguousarray(inputs[name]) for name in NAMES}
    w = {name: nc.dram_tensor(name, a.shape, mybir.dt.from_np(a.dtype), kind="ExternalInput").ap()
         for name, a in arrays.items()}
    out = nc.dram_tensor("out", [B, P, IMG, IMG], F32, kind="ExternalOutput").ap()
    build(nc, w, out)
    return run_bass_kernel_spmd(nc, [arrays], core_ids=[0]).results[0]["out"]
```

```python
import itertools
from contextlib import ExitStack, contextmanager

import concourse.bass as bass
from concourse import mybir

F32 = mybir.dt.float32
BF16 = mybir.dt.bfloat16
I32 = mybir.dt.int32
ALU = mybir.AluOpType
ACT = mybir.ActivationFunctionType
AX = mybir.AxisListType

P = 128
B, IMG = 4, 32
N = IMG * IMG
NT = N // P
M = B * N
MT = M // P
BANK = 512
NC2 = N // BANK
ROW = 32
E1, E2 = 8, 4
GH, GE = 4, 4
EDGES = 524288
EW = EDGES // P
NEG = -1.0e30


SERIAL = itertools.count()


@contextmanager
def stage(nc, *names, pool_dma=False):
    with ExitStack() as c:
        sems = [c.enter_context(nc.semaphore(f"{n}_{next(SERIAL)}")) for n in names]
        with nc.Block() as block:
            yield (block, *sems)
        nums = sorted(s.num for s in sems)
        if not nums:
            nc.all_engine_barrier(sem_only=True)
            return
        cuts = [i for i in range(1, len(nums)) if nums[i] != nums[i - 1] + 1]
        for i, j in zip([0] + cuts, cuts + [len(nums)]):
            if pool_dma:
                nc.gpsimd.dma_reset(range(nums[i], nums[j - 1] + 1))
            nc.gpsimd.sem_clear(range(nums[i], nums[j - 1] + 1))
        nc.all_engine_barrier(sem_only=True)


def sbuf(nc, name, shape, dt):
    return nc.sbuf_tensor(f"{name}_{next(SERIAL)}", shape, dt)


def psum(nc, name, shape, dt):
    return nc.psum_tensor(f"{name}_{next(SERIAL)}", shape, dt)


def linker(engine, done):
    count = [0]

    def link(instruction):
        count[0] += 1
        instruction.then_inc(done, 1)
        engine.wait_ge(done, count[0])

    return link


def affine(nc, on_act, out, in_, scale=1.0, bias=0.0, func=ACT.Identity):
    if on_act:
        return nc.scalar.activation(out, in_, func, bias=bias, scale=scale)
    return nc.vector.tensor_scalar(out, in_, scale, bias, ALU.mult, ALU.add)


def product_pass(nc, ps, n, product, evacuate, by="ad"):
    ring = ps.shape[1]
    with stage(nc, "product_ready", "off_by_act", "off_by_dve") as (block, ready, by_act, by_dve):
        done = {"a": by_act, "d": by_dve}
        share = {e: [i for i in range(n) if by[i % len(by)] == e] for e in "ad"}

        @block.tensor
        def _(pe):
            for i in range(n):
                if i >= ring:
                    e = by[(i - ring) % len(by)]
                    pe.wait_ge(done[e], share[e].index(i - ring) + 1)
                product(i, ps[:, i % ring]).then_inc(ready, 1)

        @block.scalar
        def _(act):
            for i in share["a"]:
                act.wait_ge(ready, i + 1)
                evacuate(True, i, ps[:, i % ring]).then_inc(by_act, 1)

        @block.vector
        def _(dve):
            for i in share["d"]:
                dve.wait_ge(ready, i + 1)
                evacuate(False, i, ps[:, i % ring]).then_inc(by_dve, 1)


def turn_tiles(nc, ps, ident, pairs, combine=None):
    def product(i, bank):
        for k, tile in enumerate(pairs[i][0]):
            last = nc.tensor.transpose(bank[0:tile.shape[1], k * P:(k + 1) * P], tile, ident[:])
        return last

    def evacuate(on_act, i, bank):
        tiles, out = pairs[i]
        in_ = bank[0:out.shape[0], 0:len(tiles) * P].rearrange("p (k n) -> p k n", n=P)
        if combine is not None:
            return combine(on_act, i, out, in_)
        if on_act:
            return nc.scalar.copy(out, in_)
        return nc.vector.tensor_copy(out, in_)

    product_pass(nc, ps, len(pairs), product, evacuate)



def make_constants(nc, k):
    with stage(nc, "made") as (block, made):
        @block.gpsimd
        def _(pool):
            link = linker(pool, made)

            def select(out, base, pattern, fill, compare):
                link(nc.gpsimd.affine_select(out=out, in_=out, compare_op=compare, fill=fill, base=base,
                                             pattern=pattern, channel_multiplier=1))

            def same_group(t, size, value):
                link(nc.gpsimd.memset(t[:], value))
                n = P // size
                if t.shape[1] == n:
                    low, high, view = [[-size, n]], [[size, n]], t[:]
                else:
                    low, high = [[-size, n], [0, size]], [[size, n], [0, size]]
                    view = t[:].rearrange("p (n s) -> p n s", s=size)
                select(view, 0, low, 0.0, ALU.is_ge)
                link(nc.gpsimd.affine_select(out=view, in_=view, compare_op=ALU.is_ge, fill=0.0,
                                             base=size - 1, pattern=high, channel_multiplier=-1))

            link(nc.gpsimd.memset(k.ident[:], 0.0))
            select(k.ident[:], 0, [[-1, P]], 1.0, ALU.not_equal)
            link(nc.gpsimd.tensor_copy(k.ident_b[:], k.ident[:]))
            same_group(k.mean16, 16, 1.0 / 16)
            same_group(k.mean4, 4, 1.0 / 4)
            same_group(k.block32, 32, 1.0 / N)
            for t, d, shifts in ((k.place16, 16, 13), (k.place32, 32, 5)):
                link(nc.gpsimd.memset(t[:], 0.0))
                H = P // d
                same_group(t[:, (shifts - 1) * H:shifts * H], d, 1.0)
            for t, d in ((k.spread16, 16), (k.spread32, 32)):
                n = SPREAD * P // d
                link(nc.gpsimd.memset(t[:], 0.0))
                for part in range(3):
                    select(t[:].rearrange("p (r d) -> p r d", d=d), -part * n, [[-1, n], [0, d]], 1.0, ALU.not_equal)
            link(nc.gpsimd.memset(k.ones_row[:], 1.0))
            link(nc.gpsimd.memset(k.eps[:, 0:1], 1e-5))
            link(nc.gpsimd.memset(k.eps[:, 1:2], 1e-3))
            link(nc.gpsimd.memset(k.window_mask[:], 0.0))
            for t, w in ((0, 0), (0, 1), (NT - 1, 3), (NT - 1, 4)):
                v = k.window_mask[:, t, w:w + 1]
                if t == 0:
                    select(v, w - 2, [[0, 1]], NEG, ALU.is_ge)
                else:
                    link(nc.gpsimd.affine_select(out=v, in_=v, compare_op=ALU.is_ge, fill=NEG,
                                                 base=P - 1 - (w - 2), pattern=[[0, 1]],
                                                 channel_multiplier=-1))


C_GN_G, C_GN_B, C_QKV_B, C_PROJ_B, C_L1_B = 0, 1, 2, 5, 6
C_MOE = 7
C_G_IN = C_MOE + 80
C_G_OUT, C_T_IN, C_T_OUT, C_FUS1, C_FFN1, C_B1 = C_G_IN + 3, C_G_IN + 4, C_G_IN + 7, C_G_IN + 8, C_G_IN + 10, C_G_IN + 12
C_ROWS = C_B1 + 2 * E2


def load_weights(nc, k, w):
    with ExitStack() as c:
        table = c.enter_context(sbuf(nc, "table", [P, P], F32))
        raw = c.enter_context(sbuf(nc, "raw", [P, 27, P], F32))
        ps = c.enter_context(psum(nc, "ps_w", [P, 8, BANK], F32))

        rows = [(C_GN_G, w["L0_conv_gn_gamma"]), (C_GN_B, w["L0_conv_gn_beta"]), (C_QKV_B, w["L0_conv_qkv_b"]),
                (C_PROJ_B, w["L0_conv_proj_b"]), (C_L1_B, w["L1_conv_b_out"])]
        rows += [(C_MOE + E1 * i, w[f"L2_ffn_{n}"]) for i, n in enumerate("b1 g1 be1 m1 v1 b2 g2 be2 m2 v2".split())]
        rows += [(C_G_IN, w["L3_attn_g_in_b"]), (C_G_OUT, w["L3_attn_g_out_b"]),
                 (C_T_IN, w["L3_attn_t_in_b"]), (C_T_OUT, w["L3_attn_t_out_b"]), (C_FUS1, w["L3_attn_fus_b1"]),
                 (C_FFN1, w["L3_attn_ffn_b1"]), (C_B1, w["L3_ffn_b1"])]

        def as_rows(a):
            if len(a.shape) == 1:
                return a.rearrange("(r n) -> r n", n=P)
            return a.rearrange("e (r n) -> (e r) n", n=P) if a.shape[1] > P else a

        sources = []
        for name in ("L0_conv_qkv_w", "L0_conv_proj_w", "L1_conv_w_out", "L3_attn_g_in_w", "L3_attn_g_out_w",
                     "L3_attn_t_in_w", "L3_attn_t_out_w", "L3_attn_fus_w1", "L3_attn_fus_w2", "L3_attn_ffn_w1",
                     "L3_attn_ffn_w2"):
            a = w[name]
            for r in range(a.shape[0] // P):
                for q in range(a.shape[1] // P):
                    sources.append(a[r * P:(r + 1) * P, q * P:(q + 1) * P])
        for g in range(2):
            sources.append(w["L2_attn_w_qkv"][:, g * P:(g + 1) * P])

        straight = [(k.w_kv[:], w["L2_attn_w_qkv"][:, 2 * P:6 * P]),
                    (k.w_o2[:], w["L2_attn_w_out"].rearrange("(g e) o -> e g o", g=2)),
                    (k.m1[:], w["L2_ffn_W1"].rearrange("e d h -> d e h")),
                    (k.m2[:], w["L2_ffn_W2"].rearrange("e d h -> d e h")),
                    (k.mo[:], w["L2_ffn_Wo"].rearrange("e d h -> d e h")),
                    (k.mo_b[:], w["L2_ffn_bo"]), (k.wr[:], w["L2_ffn_Wr"]),
                    (k.w_gat[:], w["L3_ffn_W_gat"]),
                    (k.x1[:], w["L3_ffn_W1"].rearrange("e d h -> d e h")),
                    (k.x2[:], w["L3_ffn_W2"].rearrange("e (s h) d -> h e s d", h=P)),
                    (k.x2_b[:], w["L3_ffn_b2"])]
        straight += [(k.rows[0:1, i, 0:n], w[name].rearrange("(a n) -> a n", a=1)) for i, (name, n) in enumerate(
            (("L2_attn_b_out", P), ("L2_ffn_br", E1), ("L3_attn_fus_b2", P), ("L3_attn_ffn_b2", P)))]
        straight += [(k.wide[:, i, :], w[name].partition_broadcast(P)) for i, name in enumerate(
            ("L3_attn_gn_g", "L3_attn_gn_b", "L3_attn_fn_g", "L3_attn_fn_b"))]
        straight += [(k.gat[:, i, :], w[name].partition_broadcast(P)) for i, name in enumerate(
            ("L3_ffn_b_gat", "L3_ffn_ln_gamma", "L3_ffn_ln_beta"))]
        straight += [(k.gat[:, 3 + i, :], w[name].rearrange("h e -> (h e)").partition_broadcast(P))
                     for i, name in enumerate(("L3_ffn_att_src", "L3_ffn_att_dst"))]
        straight += [(k.x_cm[:], w["x"].rearrange("b c h w -> c b (h w)"))]

        with stage(nc, "cleared", "loaded") as (block, cleared, loaded):
            n_row_loads = len(rows)

            @block.gpsimd
            def _(pool):
                nc.gpsimd.memset(table[:], 0.0).then_inc(cleared, 1)

            @block.sync
            def _(sp):
                for out, in_ in straight:
                    sp.dma_start(out, in_).then_inc(loaded, 16)
                sp.wait_ge(loaded, 16 * (len(straight) + len(sources) + n_row_loads))

            @block.scalar
            def _(act):
                for i, source in enumerate(sources):
                    act.dma_start(raw[:, i, :], source).then_inc(loaded, 16)
                act.wait_ge(cleared, 1)
                for r, a in rows:
                    v = as_rows(a)
                    act.dma_start(table[r:r + v.shape[0], :], v).then_inc(loaded, 16)

        tiles = [raw[:, i, :] for i in range(len(sources))]
        flat = []
        for i in range(0, len(tiles), 4):
            flat.append((tiles[i:i + 4], k.turned[:, i:min(i + 4, len(tiles)), :]))
        flat.append(([table[:]], k.cols[:].unsqueeze(1)))
        turn_tiles(nc, ps, k.ident, flat)

        with stage(nc, "scaled", "done") as (block, scaled, done):
            @block.scalar
            def _(act):
                for j in range(2):
                    v = C_MOE + E1 * (4 + 5 * j)
                    nc.scalar.activation(k.bn[:, j, 0, :], k.cols[:, v:v + E1], ACT.Sqrt,
                                         bias=k.eps[:, 1:2]).then_inc(scaled, 1)

            @block.vector
            def _(dve):
                link = linker(dve, done)
                link(nc.vector.tensor_scalar(k.qb[:, 0:1], k.cols[:, C_QKV_B:C_QKV_B + 1], 32 ** -0.5, None, ALU.mult))
                link(nc.vector.tensor_scalar(k.qb[:, 1:2], k.cols[:, C_G_IN:C_G_IN + 1], 16 ** -0.5, None, ALU.mult))
                link(nc.vector.tensor_scalar(k.qb[:, 3:4], k.cols[:, C_T_IN:C_T_IN + 1], 32 ** -0.5, None, ALU.mult))
                dve.wait_ge(scaled, 2)
                for j in range(2):
                    b_, g_, be_, m_ = (k.cols[:, C_MOE + E1 * (i + 5 * j):C_MOE + E1 * (i + 5 * j + 1)] for i in range(4))
                    link(nc.vector.reciprocal(k.bn[:, j, 0, :], k.bn[:, j, 0, :]))
                    link(nc.vector.tensor_tensor(k.bn[:, j, 0, :], k.bn[:, j, 0, :], g_, ALU.mult))
                    link(nc.vector.tensor_tensor(k.bn[:, j, 1, :], b_, m_, ALU.subtract))
                    link(nc.vector.tensor_tensor(k.bn[:, j, 1, :], k.bn[:, j, 1, :], k.bn[:, j, 0, :], ALU.mult))
                    link(nc.vector.tensor_tensor(k.bn[:, j, 1, :], k.bn[:, j, 1, :], be_, ALU.add))



def group_norm(nc, k, x, out, mean_matrix, gamma, beta):
    with ExitStack() as c:
        stats = c.enter_context(sbuf(nc, "gn_stats", [P, NC2, 6], F32))
        s = c.enter_context(sbuf(nc, "gn_s", [P, 8], F32))
        ps = c.enter_context(psum(nc, "gn_ps", [P, BANK], F32))
        block, chained, ready, averaged, rooted = c.enter_context(stage(nc, "chained", "moments", "averaged", "rooted"))

        @block.vector
        def _(dve):
            link = linker(dve, chained)
            for i in range(NC2):
                link(nc.vector.bn_stats(stats[:, i, :], x[:, i * BANK:(i + 1) * BANK]))
            link(nc.vector.bn_aggr(s[:, 0:2], stats[:].rearrange("p a b -> p (a b)")))
            nc.vector.scalar_tensor_tensor(s[:, 1:2], s[:, 0:1], s[:, 0:1], s[:, 1:2], ALU.mult, ALU.add).then_inc(ready, 1)
            dve.wait_ge(averaged, 1)
            link(nc.vector.tensor_copy(s[:, 2:4], ps[:, 0:2]))
            link(nc.vector.tensor_tensor(s[:, 4:5], s[:, 2:3], s[:, 2:3], ALU.mult))
            nc.vector.tensor_tensor(s[:, 5:6], s[:, 3:4], s[:, 4:5], ALU.subtract).then_inc(ready, 1)
            dve.wait_ge(rooted, 1)
            link(nc.vector.reciprocal(s[:, 6:7], s[:, 6:7]))
            if gamma is not None:
                link(nc.vector.tensor_tensor(s[:, 6:7], s[:, 6:7], gamma, ALU.mult))
            link(nc.vector.tensor_tensor(s[:, 7:8], s[:, 2:3], s[:, 6:7], ALU.mult))
            if beta is not None:
                link(nc.vector.tensor_tensor(s[:, 7:8], beta, s[:, 7:8], ALU.subtract))
            else:
                link(nc.vector.tensor_scalar(s[:, 7:8], s[:, 7:8], -1.0, None, ALU.mult))
            in_ = x.rearrange("p (h w) -> p h w", w=IMG) if len(out.shape) == 3 else x
            link(nc.vector.tensor_scalar(out, in_, s[:, 6:7], s[:, 7:8], ALU.mult, ALU.add))

        @block.tensor
        def _(pe):
            pe.wait_ge(ready, 1)
            nc.tensor.matmul(ps[:, 0:2], mean_matrix[:], s[:, 0:2], start=True, stop=True).then_inc(averaged, 1)

        @block.scalar
        def _(act):
            act.wait_ge(ready, 2)
            nc.scalar.activation(s[:, 6:7], s[:, 5:6], ACT.Sqrt, bias=k.eps[:, 0:1]).then_inc(rooted, 1)


def layer_norm(nc, k, x, out, gamma=None, beta=None):
    with ExitStack() as c:
        stats = c.enter_context(sbuf(nc, "ln_stats", [P, NT, 6], F32))
        s = c.enter_context(sbuf(nc, "ln_s", [P, NT, 2], F32))
        block, chained, ready, rooted, ready_shift, off = c.enter_context(
            stage(nc, "chained", "variance", "rooted", "shift", "normed"))

        @block.vector
        def _(dve):
            link = linker(dve, chained)
            for t in range(NT):
                nc.vector.bn_stats(stats[:, t, :], x[:, t, :]).then_inc(off, 1)
            for t in range(NT):
                dve.wait_ge(off, t + 1)
                last = nc.vector.bn_aggr(s[:, t, :], stats[:, t, :])
                last.then_inc(ready, 1)
            dve.wait_ge(rooted, 1)
            link(nc.vector.reciprocal(s[:, :, 1], s[:, :, 1]))
            for t in range(NT):
                last = nc.vector.tensor_scalar(out[:, t, :], x[:, t, :], s[:, t, 0:1], s[:, t, 1:2],
                                               ALU.subtract, ALU.mult)
                last.then_inc(ready_shift, 1)
            if gamma is not None:
                dve.wait_ge(ready_shift, NT)
                for g, op in ((gamma, ALU.mult), (beta, ALU.add)):
                    link(nc.vector.tensor_tensor(out, out, g.unsqueeze(1).broadcast_to([P, NT, P]), op))

        @block.scalar
        def _(act):
            act.wait_ge(ready, NT)
            nc.scalar.activation(s[:, :, 1], s[:, :, 1], ACT.Sqrt, bias=k.eps[:, 0:1]).then_inc(rooted, 1)


STACKS = {16: [((0, 0, 0, 1, 1, 2), (0, 1, 2, 0, 1, 0))],
          32: [((0, 0, 1), (0, 1, 0)), ((0, 1, 2), (2, 1, 0))]}
STACK = 96
S_STEPS = (2, 2, 1, 1, 1, 1, 0, 0)


def split_parts(nc, k, pairs):
    with stage(nc, "rounded", "rest_ready", "done") as (block, rounded, rest_ready, done):
        @block.scalar
        def _(act):
            for part in range(2):
                for j, (x, parts) in enumerate(pairs):
                    if part == 1:
                        act.wait_ge(rest_ready, j + 1)
                    nc.scalar.copy(parts[:, part], x).then_inc(rounded, 1)

        @block.vector
        def _(dve):
            n = len(pairs)
            for j, (x, parts) in enumerate(pairs):
                dve.wait_ge(rounded, j + 1)
                nc.vector.tensor_tensor(x, x, parts[:, 0], ALU.subtract).then_inc(rest_ready, 1)
            for j, (x, parts) in enumerate(pairs):
                dve.wait_ge(rounded, n + j + 1)
                nc.vector.tensor_tensor(parts[:, 2], x, parts[:, 1], ALU.subtract).then_inc(done, 1)


def store_parts(nc, k, parts):
    with stage(nc) as (block,):
        @block.sync
        def _(sp):
            for j in range(2):
                sp.dma_start(k.parts_dram[j].rearrange("s p n -> p s n"), parts[j]).then_inc(k.parted, 16)


def load_stacks(nc, k, hd):
    heads = P // hd
    with stage(nc) as (block,):
        @block.sync
        def _(sp):
            sp.wait_ge(k.parted, 32)
            for g in range(2):
                for j in range(2):
                    for slot, blocks in enumerate(STACKS[hd]):
                        for r, part in enumerate(blocks[j]):
                            half = slice(g * heads // 2, (g + 1) * heads // 2)
                            slots = k.stacks[r * hd:(r + 1) * hd, j].rearrange(
                                "p (h s) n -> p h s n", s=len(STACKS[hd]))[:, half, slot, :]
                            source = k.parts_dram[j, part].rearrange("(h r) n -> r h n", r=hd)[:, half, :]
                            sp.dma_start(slots, source).then_inc(k.stacked[g], 16)


def dense_attention(nc, k, hd, o_cm, bias):
    heads = P // hd
    per = len(STACKS[hd])
    share = 32 // hd
    groups = heads // share
    items, at_step = [], {}

    def schedule(step, new):
        at_step[step] = list(range(len(items), len(items) + len(new)))
        items.extend(new)

    def tiles(h, lo, hi):
        return [("s", h, t, n) for t in range(lo, hi) for n in range(NC2)]

    rows_of = {}
    schedule("first", tiles(0, 0, NT))
    rows_of[0] = list(range(len(items), len(items) + NC2))
    items += [("r", 0, n) for n in range(NC2)]
    for h in range(heads):
        lo = 0
        for m in range(NT):
            hi = lo + S_STEPS[m]
            schedule((h, m), tiles(h + 1, lo, hi) if h + 1 < heads else [])
            lo = hi
            if m == NT - 1 and h + 1 < heads:
                rows_of[h + 1] = list(range(len(items), len(items) + NC2))
                items += [("r", h + 1, n) for n in range(NC2)]
    order = {"s": {}, "r": {}}
    for i, item in enumerate(items):
        order[item[0]][i] = len(order[item[0]])
    RING = 2
    with ExitStack() as c:
        ring = c.enter_context(psum(nc, "att_ring", [P, RING, BANK], F32))
        ST = c.enter_context(psum(nc, "att_ST", [P, 2, N], F32))
        O = c.enter_context(psum(nc, "att_O", [64, NC2, BANK], F32))
        probs = c.enter_context(sbuf(nc, "att_probs", [P, 3, N], F32))
        half_max = c.enter_context(sbuf(nc, "att_half_max", [P, 2, NT, NC2], F32))
        shift = c.enter_context(sbuf(nc, "att_shift", [P, 2, NT], F32))
        shift_parts = c.enter_context(sbuf(nc, "att_shift_parts", [P, 2, NT, 3], BF16))
        den = c.enter_context(sbuf(nc, "att_den", [P, N], F32))
        (block, ring_ready, reduced, rows_off, chained, parts_ready, st_ready, probs_ready, mixed_ready,
         off_by_act, off_by_dve, normed, biased) = c.enter_context(stage(nc, "ring_ready", "reduced", "rows_off", "chained", "parts_ready", "st_ready",
                                         "probs_ready", "mixed_ready", "off_by_act", "off_by_dve", "normed",
                                         "biased"))

        def rows_of_group(x, g):
            return x[32 * g:32 * g + 32, :].rearrange("p (n m) -> p n m", m=BANK)

        @block.tensor
        def _(pe):
            def bank_free(i):
                if i >= RING:
                    kind = items[i - RING][0]
                    pe.wait_ge(reduced if kind == "s" else rows_off, order[kind][i - RING] + 1)

            def scores(i):
                _, h, t, n = items[i]
                bank_free(i)
                nc.tensor.matmul(ring[:, i % RING], k.stacks[0:STACK, 0, per * h, t * P:(t + 1) * P],
                                 k.stacks[0:STACK, 1, per * h, n * BANK:(n + 1) * BANK], start=True,
                                 stop=True).then_inc(ring_ready, 1)

            def shift_rows(h):
                pe.wait_ge(parts_ready, h + 1)
                for i in rows_of[h]:
                    n = items[i][2]
                    bank_free(i)
                    for t in range(4):
                        last = nc.tensor.matmul(ring[STACK:STACK + 3, i % RING, t * P:(t + 1) * P],
                                                shift_parts[:, h % 2, 4 * n + t, :], k.ident_b[:], start=True,
                                                stop=True, tile_position=(0, STACK))
                    last.then_inc(ring_ready, 1)

            def scores_transposed(h, m):
                s = h * NT + m
                if m == 0:
                    pe.wait_ge(rows_off, NC2 * (h + 1))
                if s >= 2:
                    pe.wait_ge(probs_ready, s - 1)
                for n in range(NC2):
                    for j in range(per):
                        rows = STACK + 3 if j == per - 1 else STACK
                        last = nc.tensor.matmul(ST[:, s % 2, n * BANK:(n + 1) * BANK],
                                                k.stacks[0:rows, 1, per * h + j, m * P:(m + 1) * P],
                                                k.stacks[0:rows, 0, per * h + j, n * BANK:(n + 1) * BANK],
                                                start=(j == 0), stop=(j == per - 1))
                last.then_inc(st_ready, 1)

            def mix(h, m):
                s = h * NT + m
                pe.wait_ge(probs_ready, s + 1)
                g, first, last_step = h // share, h % share == 0 and m == 0, h % share == share - 1 and m == NT - 1
                if first and g >= 1:
                    pe.wait_ge(off_by_act, g)
                    pe.wait_ge(off_by_dve, g)
                for n in range(NC2):
                    last = nc.tensor.matmul(O[:, n], k.v_ext[:, m, h, :], probs[:, s % 3, n * BANK:(n + 1) * BANK],
                                            start=first, stop=last_step)
                last.then_inc(mixed_ready, 1)

            pe.wait_ge(k.stacked[0], 16 * 6 * 2)
            for i in at_step["first"]:
                scores(i)
            shift_rows(0)
            for h in range(heads):
                if h == heads // 2 - 1:
                    pe.wait_ge(k.stacked[1], 16 * 6 * 2)
                for m in range(NT):
                    for i in at_step[(h, m)]:
                        scores(i)
                    if m == NT - 1 and h + 1 < heads:
                        shift_rows(h + 1)
                    scores_transposed(h, m)
                    if h * NT + m >= 1:
                        mix(*divmod(h * NT + m - 1, NT))
            mix(heads - 1, NT - 1)

        @block.scalar
        def _(act):
            def rows(h):
                for i in rows_of[h]:
                    n = items[i][2]
                    act.wait_ge(ring_ready, i + 1)
                    nc.scalar.copy(k.stacks[STACK:STACK + 3, 0, per * h + per - 1, n * BANK:(n + 1) * BANK],
                                   ring[STACK:STACK + 3, i % RING, :]).then_inc(rows_off, 1)

            def carry_off(g):
                act.wait_ge(mixed_ready, NT * share * (g + 1))
                nc.scalar.copy(rows_of_group(o_cm, g), O[0:32]).then_inc(off_by_act, 1)

            rows(0)
            for h in range(heads):
                for m in range(NT):
                    s = h * NT + m
                    if m == NT - 1 and h + 1 < heads:
                        rows(h + 1)
                    act.wait_ge(st_ready, s + 1)
                    if s >= 3:
                        act.wait_ge(mixed_ready, s - 2)
                    nc.scalar.activation(probs[:, s % 3, :], ST[:, s % 2, :], ACT.Exp).then_inc(probs_ready, 1)
                    if m == 0 and h % share == 0 and h > 0:
                        carry_off(h // share - 1)
            carry_off(groups - 1)
            for n in range(NC2):
                act.wait_ge(normed, n + 1)
                affine(nc, True, chunk(o_cm, n), chunk(o_cm, n), 1.0, bias).then_inc(biased, 1)

        @block.vector
        def _(dve):
            link = linker(dve, chained)

            def maxima(indices):
                for i in indices:
                    _, h, t, n = items[i]
                    dve.wait_ge(ring_ready, i + 1)
                    nc.vector.tensor_reduce(half_max[:, h % 2, t, n:n + 1], ring[:, i % RING], AX.X, ALU.max,
                                            negate=True).then_inc(reduced, 1)
                    if t == NT - 1 and n == NC2 - 1:
                        parts(h)

            def parts(h):
                a, p_ = shift[:, h % 2], shift_parts[:, h % 2]
                dve.wait_ge(reduced, NC2 * NT * (h + 1))
                link(nc.vector.tensor_tensor(a, half_max[:, h % 2, :, 0], half_max[:, h % 2, :, 1], ALU.min))
                link(nc.vector.tensor_copy(p_[:, :, 0], a))
                link(nc.vector.tensor_tensor(a, a, p_[:, :, 0], ALU.subtract))
                link(nc.vector.tensor_copy(p_[:, :, 1], a))
                nc.vector.tensor_tensor(p_[:, :, 2], a, p_[:, :, 1], ALU.subtract).then_inc(parts_ready, 1)

            def carry_off(g):
                dve.wait_ge(mixed_ready, NT * share * (g + 1))
                nc.vector.tensor_copy(rows_of_group(den, g), O[32:64]).then_inc(off_by_dve, 1)

            maxima(at_step["first"])
            for h in range(heads):
                for m in range(NT):
                    maxima(at_step[(h, m)])
                    if m == 0 and h % share == 0 and h > 0:
                        carry_off(h // share - 1)
            carry_off(groups - 1)
            dve.wait_ge(off_by_dve, groups)
            for n in range(NC2):
                link(nc.vector.reciprocal(chunk(den, n), chunk(den, n)))
                if n == 0:
                    dve.wait_ge(off_by_act, groups)
                nc.vector.tensor_tensor(chunk(o_cm, n), chunk(o_cm, n), chunk(den, n), ALU.mult).then_inc(normed, 1)
    for sem in (k.parted, *k.stacked):
        nc.gpsimd.sem_clear(sem)
    nc.all_engine_barrier(sem_only=True)


SPREAD = 5


def local_attention(nc, k, K, H, q, shifted_k, shifted_v, place, spread, w_out, out, mask=None, mirrored=False):
    KH = K * H
    first = K // 2 if mirrored else 0
    order = list(range(first, K)) + list(range(first - 1, -1, -1))
    n_a = K - first
    rows_a, rows_b = n_a * H, first * H
    groups = K // SPREAD
    GR = SPREAD * H
    HALF = NT // 2
    with ExitStack() as c:
        parts = c.enter_context(sbuf(nc, "loc_parts", [P, NT, groups, 3 * GR], BF16))
        att_t = c.enter_context(sbuf(nc, "loc_att_t", [3 * GR, groups, N], BF16))

        with ExitStack() as c2:
            att = c2.enter_context(sbuf(nc, "loc_att", [P, NT, KH], F32))
            small = c2.enter_context(sbuf(nc, "loc_small", [P, 2, NT, H], F32))
            prod = c2.enter_context(sbuf(nc, "loc_prod", [P, 3, N], F32))
            in_rows = c2.enter_context(sbuf(nc, "loc_rows", [rows_a, N], F32))
            if mirrored:
                R = IMG + 4
                padded = c2.enter_context(sbuf(nc, "loc_padded", [rows_a, R, R], F32))
                moved = c2.enter_context(sbuf(nc, "loc_moved", [rows_b, IMG, R], F32))
                in_rows_b = c2.enter_context(sbuf(nc, "loc_rows_b", [rows_b, N], F32))
            ps = c2.enter_context(psum(nc, "loc_ps", [P, NC2, BANK], F32))
            turned = c2.enter_context(psum(nc, "loc_turned", [P, NT // 2, 2, BANK // 2], F32))
            (block, product_ready, scored, rows_ready, zeroed, pad_ready, moved_ready, rows_b_ready, turned_ready,
             chained, shifted, exped, weighed, rest_ready, rounded, split) = c2.enter_context(stage(
                nc, "product_ready", "scored", "rows_ready", "zeroed", "pad_ready", "moved_ready", "rows_b_ready",
                "turned_ready", "chained", "shifted", "exped", "weighed", "rest_ready", "rounded", "split"))

            def half(x, u):
                return x[:, HALF * u:HALF * (u + 1)]

            def grouped(u):
                return half(att, u).rearrange("p t (g r) -> p (t g) r", r=GR)

            def part(i, u):
                return half(parts, u)[:, :, :, i * GR:(i + 1) * GR].rearrange("p t g r -> p (t g) r")

            @block.tensor
            def _(pe):
                for j in range(n_a):
                    pe.wait_ge(product_ready, NC2 * (j + 1))
                    for n in range(NC2):
                        last = nc.tensor.matmul(ps[0:rows_a, n], place[:, (n_a - 1 - j) * H:(n_a - 1 - j) * H + rows_a],
                                                prod[:, j % 3, n * BANK:(n + 1) * BANK], start=(j == 0),
                                                stop=(j == n_a - 1))
                    last.then_inc(scored, 1)
                pe.wait_ge(rows_ready, NC2)
                for t in range(NT):
                    last = nc.tensor.transpose(turned[:, t // 2, t % 2, 0:rows_a], in_rows[:, t * P:(t + 1) * P],
                                               k.ident[0:rows_a, 0:rows_a])
                    if not mirrored:
                        last.then_inc(turned_ready, 1)
                if mirrored:
                    for t in range(NT):
                        if t % HALF == 0:
                            pe.wait_ge(rows_b_ready, t // HALF + 1)
                        nc.tensor.transpose(turned[:, t // 2, t % 2, rows_a:KH], in_rows_b[:, t * P:(t + 1) * P],
                                            k.ident[0:rows_b, 0:rows_b]).then_inc(turned_ready, 1)

            if mirrored:
                @block.gpsimd
                def _(pool):
                    nc.gpsimd.memset(padded[:], 0.0).then_inc(zeroed, 1)

                @block.sync
                def _(sp):
                    flat = padded[:].rearrange("p a b -> p (a b)")
                    flat_moved = moved[:].rearrange("p a b -> p (a b)")
                    size = IMG * R - 4
                    sp.wait_ge(pad_ready, NC2)
                    for j in range(1, n_a):
                        dy, dx = divmod(order[j], 5)
                        start = (4 - dy) * R + 4 - dx
                        sp.dma_start(flat_moved[(j - 1) * H:j * H, 0:size],
                                     flat[j * H:(j + 1) * H, start:start + size]).then_inc(moved_ready, 16)

            @block.vector
            def _(dve):
                for j in range(n_a):
                    if j >= 3:
                        dve.wait_ge(scored, j - 2)
                    for n in range(NC2):
                        a, b_ = q(n), shifted_k(order[j], n)
                        o_ = prod[:, j % 3, n * BANK:(n + 1) * BANK]
                        if len(a.shape) == 3:
                            o_ = o_.rearrange("p (h w) -> p h w", w=IMG)
                        nc.vector.tensor_tensor(o_, a, b_, ALU.mult).then_inc(product_ready, 1)
                if mirrored:
                    dve.wait_ge(zeroed, 1)
                    dve.wait_ge(scored, n_a)
                    lines = IMG // NC2
                    for n in range(NC2):
                        nc.vector.tensor_copy(padded[:, 2 + n * lines:2 + (n + 1) * lines, 2:2 + IMG],
                                              ps[0:rows_a, n].rearrange("p (a b) -> p a b", b=IMG)).then_inc(pad_ready, 1)
                link = linker(dve, chained)

                def heads_last(x):
                    return x.rearrange("p t (s h) -> p t s h", h=H)

                def shifts_last(x):
                    return x.rearrange("p t (s h) -> p t h s", h=H)

                def over_shifts(x):
                    return x.unsqueeze(2).broadcast_to([P, HALF, K, H])

                for u in range(2):
                    dve.wait_ge(turned_ready, HALF * (u + 1))
                    scores = turned[:, u * NT // 4:(u + 1) * NT // 4].rearrange("p b j f -> p (b j) f")[:, :, 0:KH]
                    if mask is not None:
                        link(nc.vector.tensor_tensor(heads_last(half(att, u)), heads_last(scores), half(
                            mask, u).unsqueeze(3).broadcast_to([P, HALF, K, H]), ALU.add))
                        scores = half(att, u)
                    link(nc.vector.tensor_reduce(half(small[:, 0], u), shifts_last(scores), AX.X, ALU.max))
                    nc.vector.tensor_tensor(heads_last(half(att, u)), heads_last(scores), over_shifts(
                        half(small[:, 0], u)), ALU.subtract).then_inc(shifted, 1)
                for u in range(2):
                    dve.wait_ge(exped, u + 1)
                    total = half(small[:, 1], u)
                    link(nc.vector.tensor_reduce(total, shifts_last(half(att, u)), AX.X, ALU.add))
                    link(nc.vector.reciprocal(total, total))
                    nc.vector.tensor_tensor(heads_last(half(att, u)), heads_last(half(att, u)), over_shifts(total),
                                            ALU.mult).then_inc(weighed, 1)
                for u in range(2):
                    dve.wait_ge(rounded, u + 1)
                    nc.vector.tensor_tensor(grouped(u), grouped(u), part(0, u), ALU.subtract).then_inc(rest_ready, 1)
                for u in range(2):
                    dve.wait_ge(rounded, 2 + u + 1)
                    nc.vector.tensor_tensor(part(2, u), grouped(u), part(1, u), ALU.subtract).then_inc(split, 1)

            @block.scalar
            def _(act):
                act.wait_ge(scored, n_a)
                lines = IMG // NC2
                for n in range(NC2):
                    o_ = in_rows[:, n * BANK:(n + 1) * BANK]
                    if mirrored:
                        act.wait_ge(pad_ready, n + 1)
                        nc.scalar.copy(o_.rearrange("p (a b) -> p a b", b=IMG),
                                       padded[:, 2 + n * lines:2 + (n + 1) * lines, 2:2 + IMG]).then_inc(rows_ready, 1)
                    else:
                        nc.scalar.copy(o_, ps[0:rows_a, n]).then_inc(rows_ready, 1)
                if mirrored:
                    act.wait_ge(moved_ready, 16 * (n_a - 1))
                    for n in range(NC2):
                        nc.scalar.copy(in_rows_b[:, n * BANK:(n + 1) * BANK].rearrange("p (a b) -> p a b", b=IMG),
                                       moved[:, n * lines:(n + 1) * lines, 0:IMG]).then_inc(rows_b_ready, 1)
                for u in range(2):
                    act.wait_ge(shifted, u + 1)
                    nc.scalar.activation(half(att, u), half(att, u), ACT.Exp).then_inc(exped, 1)
                for u in range(2):
                    act.wait_ge(weighed, u + 1)
                    nc.scalar.copy(part(0, u), grouped(u)).then_inc(rounded, 1)
                for u in range(2):
                    act.wait_ge(rest_ready, u + 1)
                    nc.scalar.copy(part(1, u), grouped(u)).then_inc(rounded, 1)

        with psum(nc, "loc_ps", [P, 8, 2 * BANK], BF16) as ps:
            turn_tiles(nc, ps, k.ident_b, [([parts[:, t, g] for t in range(NT)],
                                            att_t[:, g].rearrange("p (k n) -> p k n", n=P)) for g in range(groups)])

        with ExitStack() as c2:
            wide = c2.enter_context(psum(nc, "loc_wide", [P, 4, BANK], F32))
            acc = c2.enter_context(psum(nc, "loc_acc", [P, NC2, BANK], F32))
            RING = 8
            weighed = c2.enter_context(sbuf(nc, "loc_weighed", [P, RING, BANK], F32))
            partial = c2.enter_context(sbuf(nc, "loc_partial", [P, NC2, BANK], F32))
            block, spread_ready, weighed_ready, summed, added, off = c2.enter_context(
                stage(nc, "spread_ready", "weighed_ready", "summed", "added", "off"))
            steps = [(j, n) for j in range(K) for n in range(NC2)]
            by_pool = [i for i, (j, n) in enumerate(steps) if j % 2 == 1]
            by_pe = [i for i, (j, n) in enumerate(steps) if j % 2 == 0]

            @block.tensor
            def _(pe):
                for i in range(len(steps) + 2):
                    if i < len(steps):
                        j, n = steps[i]
                        if i >= 4:
                            pe.wait_ge(weighed_ready, i - 3)
                        g, column = divmod(j, SPREAD)
                        nc.tensor.matmul(wide[:, i % 4], spread[:, column * P:(column + 1) * P],
                                         att_t[:, g, n * BANK:(n + 1) * BANK], start=True,
                                         stop=True).then_inc(spread_ready, 1)
                    if i >= 2 and i - 2 in by_pe:
                        j, n = steps[i - 2]
                        pe.wait_ge(weighed_ready, i - 1)
                        nc.tensor.matmul(acc[:, n], w_out, weighed[:, (i - 2) % RING], start=(j == 0),
                                         stop=False).then_inc(summed, 1)
                pe.wait_ge(added, len(by_pool))
                for n in range(NC2):
                    nc.tensor.matmul(acc[:, n], w_out, partial[:, n], start=False, stop=True).then_inc(summed, 1)

            @block.gpsimd
            def _(pool):
                for count, i in enumerate(by_pool):
                    j, n = steps[i]
                    pool.wait_ge(weighed_ready, i + 1)
                    if count >= NC2:
                        pool.wait_ge(added, count - NC2 + 1)
                        nc.gpsimd.tensor_tensor(partial[:, n], partial[:, n], weighed[:, i % RING],
                                                ALU.add).then_inc(added, 1)
                    else:
                        nc.gpsimd.tensor_copy(partial[:, n], weighed[:, i % RING]).then_inc(added, 1)

            @block.vector
            def _(dve):
                for i, (j, n) in enumerate(steps):
                    dve.wait_ge(spread_ready, i + 1)
                    if i >= RING:
                        if i - RING in by_pool:
                            dve.wait_ge(added, by_pool.index(i - RING) + 1)
                        else:
                            dve.wait_ge(summed, by_pe.index(i - RING) + 1)
                    v = shifted_v(order[j], n)
                    a, o_ = wide[:, i % 4], weighed[:, i % RING]
                    if len(v.shape) == 3:
                        a, o_ = (y.rearrange("p (h w) -> p h w", w=IMG) for y in (a, o_))
                    nc.vector.tensor_tensor(o_, a, v, ALU.mult).then_inc(weighed_ready, 1)
                for n in range(NC2):
                    dve.wait_ge(summed, len(by_pe) + n + 1)
                    out(n, acc[:, n]).then_inc(off, 1)


def chunk(a, n, size=BANK):
    return a[:, n * size:(n + 1) * size]


def turn_image(nc, k, ps, x, out, combine=None):
    pairs = [([x[:, t, :] if len(x.shape) == 3 else chunk(x, t, P) for t in range(u, u + 4)],
              out[:, u:u + 4, :] if len(out.shape) == 3 else
              chunk(out, u // 4).rearrange("p (k n) -> p k n", n=P)) for u in range(0, NT, 4)]
    turn_tiles(nc, ps, k.ident, pairs, combine)


def copy_blocks(nc, pairs, engine_name="vector"):
    with stage(nc, "by_act", "by_dve") as (block, by_act, by_dve):
        @block.scalar
        def _(act):
            for out, in_ in pairs[1::2]:
                nc.scalar.copy(out, in_).then_inc(by_act, 1)

        @block.vector
        def _(dve):
            for out, in_ in pairs[0::2]:
                nc.vector.tensor_copy(out, in_).then_inc(by_dve, 1)


def dense_queries_keys(nc, k, ps, hd, x, qk, parts, weights, scale_bias):
    product_pass(nc, ps, 4, lambda i, bank: nc.tensor.matmul(bank, weights[i // 2], chunk(x, i % 2), start=True,
                                                             stop=True),
                 lambda on_act, i, bank: affine(nc, on_act, chunk(qk[:, i // 2], i % 2), bank, *scale_bias[i // 2]))
    split_parts(nc, k, [(qk[:, j], parts[:, j]) for j in range(2)])
    store_parts(nc, k, [parts[:, j] for j in range(2)])


def dense_values(nc, k, ps, hd, x, weights):
    share = 32 // hd

    def product(i, bank):
        for t in range(4):
            last = nc.tensor.matmul(bank[:, t * P:(t + 1) * P], chunk(x, 4 * i + t, P), weights, start=True, stop=True)
        return last

    def evacuate(on_act, i, bank):
        for j in range(share):
            heads = k.v_ext[:, 4 * i:4 * i + 4].rearrange("p t (g j) d -> p t g j d", j=share)[
                :, :, :, j, j * hd:(j + 1) * hd]
            last = affine(nc, on_act, heads, bank.rearrange("p (t g j d) -> p t g j d", t=4, j=share, d=hd)[:, :, :, j])
        return last

    product_pass(nc, ps, 2, product, evacuate)


@contextmanager
def dense_buffers(nc, k, hd):
    heads, share = P // hd, 32 // hd
    with ExitStack() as c:
        k.stacks = c.enter_context(sbuf(nc, "stacks", [P, 2, 8, N], BF16))
        k.v_ext = c.enter_context(sbuf(nc, "v_ext", [P, NT, heads, 64], F32))
        with stage(nc, "made", "zeroed") as (block, made, zeroed):
            @block.gpsimd
            def _(pool):
                nc.gpsimd.memset(k.stacks[STACK:STACK + 3, 1], 1.0).then_inc(made, 1)

            @block.vector
            def _(dve):
                nc.vector.memset(k.v_ext[:], 0.0).then_inc(zeroed, 1)
                dve.wait_ge(zeroed, 1)
                for j in range(share):
                    nc.vector.memset(k.v_ext[:].rearrange("p t (g j) d -> p (t g) j d", j=share)[
                        :, :, j, 32 + j * hd:32 + (j + 1) * hd], 1.0).then_inc(made, 1)
        yield



LAST_IMAGE = B - 1


def first_layers(nc, k):
    with ExitStack() as c:
        x = c.enter_context(sbuf(nc, "l0_x", [P, N], F32))
        parts = c.enter_context(sbuf(nc, "l0_parts", [P, 2, 3, N], BF16))
        c.enter_context(dense_buffers(nc, k, 32))
        start_attention(nc, k, 0, parts)
        load_stacks(nc, k, 32)
        with nc.Fori(0, B - 1) as b:
            finish_attention(nc, k, b, x)
            start_attention(nc, k, b + 1, parts)
            local_attention_of_image(nc, k, b, x)
        finish_attention(nc, k, LAST_IMAGE, x)
        local_attention_of_image(nc, k, LAST_IMAGE, x)


def start_attention(nc, k, b, parts):
    with ExitStack() as c:
        h = c.enter_context(sbuf(nc, "l0_h", [P, N], F32))
        qk = c.enter_context(sbuf(nc, "l0_qk", [P, 2, N], F32))
        ps = c.enter_context(psum(nc, "l0_ps", [P, 7, BANK], F32))
        copy_blocks(nc, [(h[:], k.x_cm[:, b, :])])
        group_norm(nc, k, h[:], h[:], k.mean16, k.cols[:, C_GN_G:C_GN_G + 1], k.cols[:, C_GN_B:C_GN_B + 1])
        dense_queries_keys(nc, k, ps, 32, h, qk, parts, [k.turned[:, i, :] for i in range(2)],
                           [(32 ** -0.5, k.qb[:, 0:1]), (1.0, k.cols[:, C_QKV_B + 1:C_QKV_B + 2])])
        dense_values(nc, k, ps, 32, h, k.turned[:, 2, :])


def finish_attention(nc, k, b, x):
    with ExitStack() as c:
        o_cm = c.enter_context(sbuf(nc, "l0_o", [P, N], F32))
        dense_attention(nc, k, 32, o_cm, k.cols[:, C_QKV_B + 2:C_QKV_B + 3])
        ps = c.enter_context(psum(nc, "l0_ps", [P, 8, BANK], F32))
        product_pass(nc, ps, NC2, lambda i, bank: nc.tensor.matmul(
            bank, k.turned[:, 3, :], chunk(o_cm, i), start=True, stop=True),
            lambda on_act, i, bank: nc.vector.scalar_tensor_tensor(
                chunk(x, i), bank, k.cols[:, C_PROJ_B:C_PROJ_B + 1], k.x_cm[:, b, i * BANK:(i + 1) * BANK],
                ALU.add, ALU.add), by="d")


def local_attention_of_image(nc, k, b, x):
    with ExitStack() as c:
        def sb(name, shape):
            return c.enter_context(sbuf(nc, name, shape, F32))

        R = IMG + 4
        pad = sb("l1_pad", [P, R, R])
        with stage(nc, "cleared") as (block, cleared):
            @block.vector
            def _(dve):
                nc.vector.memset(pad[:], 0.0).then_inc(cleared, 1)
        group_norm(nc, k, x[:], pad[:, 2:2 + IMG, 2:2 + IMG], k.mean4, None, None)
        if b is not LAST_IMAGE:
            load_stacks(nc, k, 32)
        rows = BANK // IMG

        def window(s, n):
            i, j = divmod(s, 5)
            return pad[:, n * rows + i:n * rows + i + rows, j:j + IMG]

        def out(n, acc):
            return nc.vector.scalar_tensor_tensor(chunk(x, n), acc, k.cols[:, C_L1_B:C_L1_B + 1], chunk(x, n),
                                                  ALU.add, ALU.add)

        local_attention(nc, k, 25, 8, lambda n: window(12, n), window, window, k.place16, k.spread16,
                        k.turned[:, 4, :], out, mirrored=True)
        with ExitStack() as c2:
            ps = c2.enter_context(psum(nc, "l1_ps", [P, 8, BANK], F32))
            tm = c2.enter_context(sbuf(nc, "l1_tm", [P, NT, P], F32))
            turn_image(nc, k, ps, x, tm)
            copy_blocks(nc, [(k.t_tm[:, b], tm[:])])


def linear_attention(nc, k, b):
    with ExitStack() as c:
        def sb(name, shape):
            return c.enter_context(sbuf(nc, name, shape, F32))

        G = 16
        t_tm, xn, xc = sb("l2_t", [P, NT, P]), sb("l2_xn", [P, NT, P]), sb("l2_xc", [P, N])
        kv, sq = sb("l2_kv", [P, NT, 4 * P]), sb("l2_sq", [P, NT, 4 * P])
        st = sb("l2_st", [P, 2, NT * G])
        dots, mo, g = sb("l2_dots", [P, 2, P]), sb("l2_mo", [P, 2, P]), sb("l2_g", [P, P])
        ps = c.enter_context(psum(nc, "l2_ps", [P, 8, BANK], F32))
        copy_blocks(nc, [(t_tm[:], k.t_tm[:, b])])
        layer_norm(nc, k, t_tm, xn[:])
        turn_image(nc, k, ps, xn, xc)
        product_pass(nc, ps, NT, lambda i, bank: nc.tensor.matmul(bank, chunk(xc, i, P), k.w_kv[:], start=True, stop=True),
                     lambda on_act, i, bank: affine(nc, on_act, kv[:, i, :], bank))
        with stage(nc, "chained", "squared", "rooted") as (block, chained, squared, rooted):
            groups = kv[:].rearrange("p t (g d) -> p (t g) d", d=32)
            squares = sq[:].rearrange("p t (g d) -> p (t g) d", d=32)

            @block.vector
            def _(dve):
                link = linker(dve, chained)

                def wide(a):
                    return a.unsqueeze(2).broadcast_to([P, NT * G, 32])

                link(nc.vector.tensor_reduce(st[:, 0], groups, AX.X, ALU.add))
                link(nc.vector.tensor_scalar(st[:, 0], st[:, 0], 1.0 / 32, None, ALU.mult))
                link(nc.vector.tensor_tensor(groups, groups, wide(st[:, 0]), ALU.subtract))
                dve.wait_ge(squared, 1)
                link(nc.vector.tensor_reduce(st[:, 1], squares, AX.X, ALU.add))
                dve.wait_ge(rooted, 1)
                link(nc.vector.reciprocal(st[:, 1], st[:, 1]))
                link(nc.vector.tensor_tensor(groups, groups, wide(st[:, 1]), ALU.mult))

            @block.scalar
            def _(act):
                act.wait_ge(chained, 3)
                nc.scalar.activation(sq[:], kv[:], ACT.Square).then_inc(squared, 1)
                act.wait_ge(chained, 4)
                nc.scalar.activation(st[:, 1], st[:, 1], ACT.Sqrt, bias=k.eps[:, 0:1], scale=1.0 / 32).then_inc(rooted, 1)

        def dots_product(i, bank):
            for t in range(NT):
                last = nc.tensor.matmul(bank[:, 0:P], kv[:, t, (2 + i) * P:(3 + i) * P], kv[:, t, i * P:(i + 1) * P],
                                        start=(t == 0), stop=(t == NT - 1))
            return last

        product_pass(nc, ps, 2, dots_product, lambda on_act, i, bank: nc.vector.tensor_tensor(
            dots[:, i], bank[:, 0:P], k.block32[:], ALU.mult), by="d")
        product_pass(nc, ps, 2, lambda i, bank: nc.tensor.matmul(bank[:, 0:P], dots[:, i], k.w_o2[:, i], start=True,
                                                                 stop=True),
                     lambda on_act, i, bank: affine(nc, on_act, mo[:, i], bank[:, 0:P]))

        def g_product(i, bank):
            for j in range(2):
                last = nc.tensor.matmul(bank[:, 0:P], k.turned[:, k.t_q2 + j, :], mo[:, j], start=(j == 0), stop=(j == 1))
            return last

        product_pass(nc, ps, 1, g_product, lambda on_act, i, bank: affine(nc, on_act, g[:], bank[:, 0:P]))

        def out_product(i, bank):
            for t in range(4):
                o_ = bank[:, t * P:(t + 1) * P]
                nc.tensor.matmul(o_, chunk(xc, 4 * i + t, P), g[:], start=True, stop=False)
                last = nc.tensor.matmul(o_, k.ones_row[:], k.rows[0:1, 0, :], start=False, stop=True)
            return last

        product_pass(nc, ps, 2, out_product, lambda on_act, i, bank: nc.vector.tensor_tensor(
            t_tm[:, 4 * i:4 * i + 4].rearrange("p t n -> p (t n)"), bank,
            t_tm[:, 4 * i:4 * i + 4].rearrange("p t n -> p (t n)"), ALU.add), by="d")
        layer_norm(nc, k, t_tm, xn[:])
        turn_image(nc, k, ps, xn, xc)
        copy_blocks(nc, [(k.t_tm[:, b], t_tm[:]), (k.xn_cm[:, b], xc[:])])


def mixture_weights(nc, k):
    with ExitStack() as c:
        feat = c.enter_context(sbuf(nc, "mw_feat", [P, N], F32))
        s = c.enter_context(sbuf(nc, "mw_s", [P, 2, NT], F32))
        ps = c.enter_context(psum(nc, "mw_ps", [P, 8, BANK], F32))
        with stage(nc, "chained") as (block, chained):
            @block.vector
            def _(dve):
                link = linker(dve, chained)
                link(nc.vector.tensor_tensor(feat[:], k.xn_cm[:, 0], k.xn_cm[:, 1], ALU.add))
                for b in range(2, B):
                    link(nc.vector.tensor_tensor(feat[:], feat[:], k.xn_cm[:, b], ALU.add))
                link(nc.vector.tensor_scalar(feat[:], feat[:], 1.0 / B, None, ALU.mult))

        def product(i, bank):
            for t in range(NT):
                o_ = bank[:, t * E1:(t + 1) * E1]
                nc.tensor.matmul(o_, chunk(feat, t, P), k.wr[:], start=True, stop=False)
                last = nc.tensor.matmul(o_, k.ones_row[:], k.rows[0:1, 1, 0:E1], start=False, stop=True)
            return last

        product_pass(nc, ps, 1, product, lambda on_act, i, bank: affine(
            nc, on_act, k.mix[:].rearrange("p t e -> p (t e)"), bank[:, 0:NT * E1]))
        with stage(nc, "chained", "exped") as (block, chained, exped):
            @block.vector
            def _(dve):
                link = linker(dve, chained)
                link(nc.vector.tensor_reduce(s[:, 0], k.mix[:], AX.X, ALU.max))
                link(nc.vector.tensor_tensor(k.mix[:], k.mix[:], s[:, 0].unsqueeze(2).broadcast_to([P, NT, E1]),
                                             ALU.subtract))
                dve.wait_ge(exped, 1)
                link(nc.vector.tensor_reduce(s[:, 1], k.mix[:], AX.X, ALU.add))
                link(nc.vector.reciprocal(s[:, 1], s[:, 1]))
                link(nc.vector.tensor_tensor(k.mix[:], k.mix[:], s[:, 1].unsqueeze(2).broadcast_to([P, NT, E1]),
                                             ALU.mult))

            @block.scalar
            def _(act):
                act.wait_ge(chained, 2)
                nc.scalar.activation(k.mix[:], k.mix[:], ACT.Exp).then_inc(exped, 1)

        turn_tiles(nc, ps, k.ident, [([k.mix[:, t] for t in range(u, u + 4)],
                                      k.mix_t[:, u * P:(u + 4) * P].rearrange("p (k n) -> p k n", n=P)) for u in (0, 4)])


def mixture(nc, k, xc, t_tm, weight, weight_t, experts, bias, hidden, out_parts):
    with ExitStack() as c:
        ps = c.enter_context(psum(nc, "mx_ps", [P, 8, BANK], F32))

        def bias_product(i, bank):
            for t in range(4):
                last = nc.tensor.matmul(bank[:, t * P:(t + 1) * P], chunk(weight_t, 4 * i + t, P), bias, start=True,
                                        stop=True)
            return last

        product_pass(nc, ps, 2, bias_product, lambda on_act, i, bank: nc.vector.tensor_tensor(
            t_tm[:, 4 * i:4 * i + 4].rearrange("p t n -> p (t n)"), bank,
            t_tm[:, 4 * i:4 * i + 4].rearrange("p t n -> p (t n)"), ALU.add), by="d")

        n_h = hidden.n
        block, hidden_ready, hidden_off, out_ready, added = c.enter_context(
            stage(nc, "hidden_ready", "hidden_off", "out_ready", "added"))
        RING = 6

        @block.tensor
        def _(pe):
            for e in range(experts + 1):
                if e < experts:
                    for i in range(n_h):
                        g = e * n_h + i
                        if g >= RING:
                            pe.wait_ge(hidden_off, g - RING + 1)
                        need = hidden.needs(i)
                        if need is not None:
                            pe.wait_ge(hidden_off, e * n_h + need + 1)
                        hidden.product(e, i, ps[:, g % RING]).then_inc(hidden_ready, 1)
                if e >= 1:
                    for u in range(2):
                        o = 2 * (e - 1) + u
                        pe.wait_ge(hidden_off, e * n_h)
                        if o >= 2:
                            pe.wait_ge(added, 4 * (o - 1))
                        for t in range(4):
                            parts = out_parts(e - 1, 4 * u + t)
                            for j, (lhs, rhs) in enumerate(parts):
                                last = nc.tensor.matmul(ps[:, 6 + u, t * P:(t + 1) * P], lhs, rhs, start=(j == 0),
                                                        stop=(j == len(parts) - 1))
                        last.then_inc(out_ready, 1)

        @block.scalar
        def _(act):
            for e in range(experts):
                for i in range(n_h):
                    g = e * n_h + i
                    if i == 0 and e >= 2:
                        act.wait_ge(out_ready, 2 * (e - 1))
                    act.wait_ge(hidden_ready, g + 1)
                    hidden.evacuate(e, i, ps[:, g % RING]).then_inc(hidden_off, 1)

        @block.vector
        def _(dve):
            for e in range(experts):
                for u in range(2):
                    dve.wait_ge(out_ready, 2 * e + u + 1)
                    for t in range(4):
                        tt = 4 * u + t
                        if e >= 1:
                            dve.wait_ge(added, 8 * (e - 1) + tt + 1)
                        nc.vector.scalar_tensor_tensor(t_tm[:, tt], ps[:, 6 + u, t * P:(t + 1) * P],
                                                       weight[:, tt, e:e + 1], t_tm[:, tt], ALU.mult,
                                                       ALU.add).then_inc(added, 1)


class Hidden:

    def __init__(self, n, needs, product, evacuate):
        self.n, self.needs, self.product, self.evacuate = n, needs, product, evacuate


def batch_normed_mixture(nc, k, b):
    with ExitStack() as c:
        t_tm = c.enter_context(sbuf(nc, "bm_t", [P, NT, P], F32))
        xc = c.enter_context(sbuf(nc, "bm_x", [P, N], F32))
        h1 = c.enter_context(sbuf(nc, "bm_h1", [P, N], F32))
        h2 = c.enter_context(sbuf(nc, "bm_h2", [P, 2, N], F32))
        copy_blocks(nc, [(t_tm[:], k.t_tm[:, b]), (xc[:], k.xn_cm[:, b])])

        def product(e, i, bank):
            if i < 2:
                return nc.tensor.matmul(bank, k.m1[:, e], chunk(xc, i), start=True, stop=True)
            return nc.tensor.matmul(bank, k.m2[:, e], chunk(h1, i % 2), start=True, stop=True)

        def evacuate(e, i, bank):
            out = chunk(h1, i) if i < 2 else h2[:, e % 2, (i % 2) * BANK:(i % 2 + 1) * BANK]
            j = i // 2
            return nc.scalar.activation(out, bank, ACT.Relu, bias=k.bn[:, j, 1, e:e + 1], scale=k.bn[:, j, 0, e:e + 1])

        hidden = Hidden(4, lambda i: None if i < 2 else i - 2, product, evacuate)
        mixture(nc, k, xc, t_tm, k.mix, k.mix_t, E1, k.mo_b[:], hidden,
                lambda e, t: [(h2[:, e % 2, t * P:(t + 1) * P], k.mo[:, e])])
        copy_blocks(nc, [(k.t_tm[:, b], t_tm[:])])


def two_attentions(nc, k, b):
    with ExitStack() as c:
        def sb(name, shape):
            return c.enter_context(sbuf(nc, name, shape, F32))

        t_tm, xn, xc = sb("l3_t", [P, NT, P]), sb("l3_xn", [P, NT, P]), sb("l3_xc", [P, N])
        both = sb("l3_both", [P, 2, N])
        copy_blocks(nc, [(t_tm[:], k.t_tm[:, b])])
        layer_norm(nc, k, t_tm, xn[:])
        with ExitStack() as c2:
            ps = c2.enter_context(psum(nc, "l3_ps", [P, 8, BANK], F32))
            turn_image(nc, k, ps, xn, xc)
        def local_part():
            with ExitStack() as c2:
                q = c2.enter_context(sbuf(nc, "l3_q", [P, N], F32))
                pads = c2.enter_context(sbuf(nc, "l3_pads", [P, 2, N + 4], F32))
                with ExitStack() as c3:
                    ps = c3.enter_context(psum(nc, "l3_ps", [P, 8, BANK], F32))
                    with stage(nc, "cleared") as (block, cleared):
                        @block.vector
                        def _(dve):
                            nc.vector.memset(pads[:], 0.0).then_inc(cleared, 1)

                    def evacuate(on_act, i, bank):
                        j = i // 2
                        if j == 0:
                            return affine(nc, on_act, chunk(q, i), bank, 32 ** -0.5, k.qb[:, 3:4])
                        out = pads[:, j - 1, 2 + (i % 2) * BANK:2 + (i % 2 + 1) * BANK]
                        return affine(nc, on_act, out, bank, 1.0, k.cols[:, C_T_IN + j:C_T_IN + j + 1])

                    product_pass(nc, ps, 6, lambda i, bank: nc.tensor.matmul(
                        bank, k.turned[:, k.t_t_in + i // 2, :], chunk(xc, i % 2), start=True, stop=True), evacuate)
                load_stacks(nc, k, 16)

                def window(j):
                    return lambda s, n: pads[:, j, s + n * BANK:s + (n + 1) * BANK]

                local_attention(nc, k, 5, 4, lambda n: chunk(q, n), window(0), window(1), k.place32, k.spread32,
                                k.turned[:, k.t_t_out, :],
                                lambda n, acc: nc.vector.tensor_scalar(chunk(both[:, 1], n), acc,
                                                                       k.cols[:, C_T_OUT:C_T_OUT + 1], None, ALU.add),
                                mask=k.window_mask)

        with ExitStack() as c2:
            o_cm = c2.enter_context(sbuf(nc, "l3_o", [P, N], F32))
            parts = c2.enter_context(sbuf(nc, "l3_parts", [P, 2, 3, N], BF16))
            with ExitStack() as c3:
                qk = c3.enter_context(sbuf(nc, "l3_qk", [P, 2, N], F32))
                ps = c3.enter_context(psum(nc, "l3_ps", [P, 8, BANK], F32))
                dense_queries_keys(nc, k, ps, 16, xc, qk, parts, [k.turned[:, k.t_g_in + i, :] for i in range(2)],
                                   [(16 ** -0.5, k.qb[:, 1:2]), (1.0, k.cols[:, C_G_IN + 1:C_G_IN + 2])])
                dense_values(nc, k, ps, 16, xc, k.turned[:, k.t_g_in + 2, :])
            local_part()
            dense_attention(nc, k, 16, o_cm, k.cols[:, C_G_IN + 2:C_G_IN + 3])
            with ExitStack() as c3:
                ps = c3.enter_context(psum(nc, "l3_ps", [P, 8, BANK], F32))
                product_pass(nc, ps, NC2, lambda i, bank: nc.tensor.matmul(
                    bank, k.turned[:, k.t_g_out, :], chunk(o_cm, i), start=True, stop=True),
                    lambda on_act, i, bank: affine(nc, on_act, chunk(both[:, 0], i), bank, 1.0,
                                                   k.cols[:, C_G_OUT:C_G_OUT + 1]))
        ps = c.enter_context(psum(nc, "l3_ps", [P, 8, BANK], F32))
        hid = sb("l3_hid", [P, 2, N])
        x2 = sb("l3_x2", [P, NT, P])

        def two_layers(inputs, w1, bias1, w2, bias_row, residual):
            def product(i, bank):
                for j, x in enumerate(inputs):
                    last = nc.tensor.matmul(bank, k.turned[:, w1(i // 2, j), :], chunk(x, i % 2), start=(j == 0),
                                            stop=(j == len(inputs) - 1))
                return last

            def evacuate(on_act, i, bank):
                return nc.scalar.activation(chunk(hid[:, i // 2], i % 2), bank, ACT.Silu,
                                            bias=k.cols[:, bias1 + i // 2:bias1 + i // 2 + 1])

            product_pass(nc, ps, 4, product, evacuate, by="a")

            def out_product(i, bank):
                for t in range(4):
                    o_ = bank[:, t * P:(t + 1) * P]
                    for j in range(2):
                        nc.tensor.matmul(o_, chunk(hid[:, j], 4 * i + t, P), k.turned[:, w2 + j, :], start=(j == 0),
                                         stop=False)
                    last = nc.tensor.matmul(o_, k.ones_row[:], k.rows[0:1, bias_row, :], start=False, stop=True)
                return last

            product_pass(nc, ps, 2, out_product, lambda on_act, i, bank: nc.vector.tensor_tensor(
                residual[:, 4 * i:4 * i + 4].rearrange("p t n -> p (t n)"), bank,
                residual[:, 4 * i:4 * i + 4].rearrange("p t n -> p (t n)"), ALU.add), by="d")

        two_layers([both[:, 0], both[:, 1]], lambda half, j: k.t_fus1 + 2 * half + j, C_FUS1, k.t_fus2, 2, xn)
        layer_norm(nc, k, xn, x2[:], k.wide[:, 0], k.wide[:, 1])
        turn_image(nc, k, ps, x2, xc)
        two_layers([xc], lambda half, j: k.t_ffn1 + half, C_FFN1, k.t_ffn2, 3, x2)
        layer_norm(nc, k, x2, xn[:], k.wide[:, 2], k.wide[:, 3])
        with stage(nc, "added") as (block, added):
            @block.vector
            def _(dve):
                nc.vector.tensor_tensor(t_tm[:], t_tm[:], xn[:], ALU.add).then_inc(added, 1)
        layer_norm(nc, k, t_tm, xn[:])
        turn_image(nc, k, ps, xn, xc)
        h = sb("l3_h", [P, NT, GH * GE])

        def gat_product(i, bank):
            for t in range(NT):
                last = nc.tensor.matmul(bank[:, 16 * t:16 * t + 16], chunk(xc, t, P), k.w_gat[:], start=True, stop=True)
            return last

        product_pass(nc, ps, 1, gat_product, lambda on_act, i, bank: affine(
            nc, on_act, h[:].rearrange("p t f -> p (t f)"), bank[:, 0:NT * 16]))
        copy_blocks(nc, [(k.t_tm[:, b], t_tm[:]), (k.xn_cm[:, b], xc[:]), (k.h_tm[:, b], h[:])])


def gelu_mixture(nc, k, b, out):
    with ExitStack() as c:
        t_tm = c.enter_context(sbuf(nc, "gm_t", [P, NT, P], F32))
        xc = c.enter_context(sbuf(nc, "gm_x", [P, N], F32))
        hid = c.enter_context(sbuf(nc, "gm_h", [P, 2, 2, N], F32))
        gates = c.enter_context(sbuf(nc, "gm_g", [P, NT, E2], F32))
        gates_t = c.enter_context(sbuf(nc, "gm_gt", [E2, N], F32))
        copy_blocks(nc, [(t_tm[:], k.t_tm[:, b]), (xc[:], k.xn_cm[:, b]), (gates[:], k.gates[:, b])])
        with ExitStack() as c2:
            ps = c2.enter_context(psum(nc, "gm_ps", [P, 8, BANK], F32))
            turn_tiles(nc, ps, k.ident, [([gates[:, t] for t in range(u, u + 4)],
                                          gates_t[:, u * P:(u + 4) * P].rearrange("p (k n) -> p k n", n=P)) for u in (0, 4)])

        def product(e, i, bank):
            half, n = divmod(i, 2)
            return nc.tensor.matmul(bank, k.x1[:, e, half * P:(half + 1) * P], chunk(xc, n), start=True, stop=True)

        def evacuate(e, i, bank):
            half, n = divmod(i, 2)
            return nc.scalar.activation(chunk(hid[:, e % 2, half], n), bank, ACT.Gelu,
                                        bias=k.cols[:, C_B1 + 2 * e + half:C_B1 + 2 * e + half + 1])

        hidden = Hidden(4, lambda i: None, product, evacuate)
        mixture(nc, k, xc, t_tm, gates, gates_t, E2, k.x2_b[:], hidden,
                lambda e, t: [(hid[:, e % 2, s, t * P:(t + 1) * P], k.x2[:, e, s]) for s in range(2)])
        with ExitStack() as c2:
            ps = c2.enter_context(psum(nc, "gm_ps2", [P, 8, BANK], F32))
            turn_image(nc, k, ps, t_tm, xc)
        with stage(nc, "stored") as (block, stored):
            @block.sync
            def _(sp):
                sp.dma_start(out[b].rearrange("c h w -> c (h w)"), xc[:]).then_inc(stored, 16)
                sp.wait_ge(stored, 16)



ROUNDS = 12
LIST = 8 * ROUNDS
FOLD = 512
REST = 1
BANDS = 4
BAND = MT // BANDS
SLOTS = 32
FEAT = GH + GH * GE
PIECE = 1024
SUB = 128
CLASSES = 8


def code_edges(nc, k, e):
    ends = e.edge_index.rearrange("s (p n) -> s p n", p=P)
    with ExitStack() as c:
        raw = c.enter_context(sbuf(nc, "ce_raw", [P, 2, PIECE], I32))
        a = c.enter_context(sbuf(nc, "ce_a", [P, 2, PIECE], I32))
        f = c.enter_context(sbuf(nc, "ce_f", [P, 3, PIECE], F32))
        with nc.Fori(0, EW // PIECE) as i:
            with stage(nc, "loaded", "chained") as (block, loaded, chained):
                @block.sync
                def _(sp):
                    for s in range(2):
                        sp.dma_start(raw[:, s], ends[s, :, bass.ds(i * PIECE, PIECE)]).then_inc(loaded, 16)

                @block.vector
                def _(dve):
                    link = linker(dve, chained)
                    src, dst = raw[:, 0], raw[:, 1]
                    piece = bass.ds(i * PIECE, PIECE)
                    dve.wait_ge(loaded, 32)
                    link(nc.vector.tensor_scalar(a[:, 0], dst, P - 1, 17, ALU.bitwise_and, ALU.logical_shift_left))
                    link(nc.vector.tensor_scalar(a[:, 1], dst, 7, 12, ALU.logical_shift_right, ALU.logical_shift_left))
                    link(nc.vector.tensor_tensor(a[:, 0], a[:, 0], a[:, 1], ALU.bitwise_or))
                    link(nc.vector.tensor_scalar(a[:, 1], src, float(M - 1), None, ALU.min))
                    link(nc.vector.scalar_tensor_tensor(f[:, 0], a[:, 0], 1.0, a[:, 1], ALU.add, ALU.add))
                    link(nc.vector.tensor_scalar(f[:, 1], dst, float(M), None, ALU.is_lt))
                    link(nc.vector.scalar_tensor_tensor(f[:, 2], src, float(M - 1), f[:, 1], ALU.is_lt, ALU.mult))
                    link(nc.vector.tensor_tensor(e.codes[:, piece], f[:, 0], f[:, 2], ALU.mult))
                    link(nc.vector.tensor_tensor(f[:, 1], f[:, 1], f[:, 2], ALU.subtract))
                    link(nc.vector.scalar_tensor_tensor(e.last[:, piece], dst, 1.0, f[:, 1], ALU.add, ALU.mult))


def fold(nc, link, x, t, width):
    cur, other = x, t
    n = x.shape[1] // 2
    while n >= width:
        low, high = cur[:, 0:n], cur[:, n:2 * n]
        link(nc.vector.tensor_tensor(other[:, 0:n], low, high, ALU.max))
        link(nc.vector.tensor_tensor(x[:, n:2 * n], low, high, ALU.min))
        cur, other = other, cur
        n //= 2
    if cur is x:
        link(nc.vector.tensor_copy(t[:, 0:width], x[:, 0:width]))
    link(nc.vector.memset(x[:, 0:width], 0.0))


def count_last(nc, k, e):
    with ExitStack() as c:
        hot = c.enter_context(sbuf(nc, "cl_hot", [P, 2, 2, 2, 64, SUB // 2], BF16))
        total = c.enter_context(sbuf(nc, "cl_total", [P, P], F32))
        corner = c.enter_context(sbuf(nc, "cl_corner", [P, 64], F32))
        place = c.enter_context(sbuf(nc, "cl_place", [P, 2, P], F32))
        ps = c.enter_context(psum(nc, "cl_ps", [P, BANK], F32))
        ps2 = c.enter_context(psum(nc, "cl_ps2", [P, BANK], F32))
        with stage(nc, "made") as (block, made):
            @block.gpsimd
            def _(pool):
                link = linker(pool, made)
                link(nc.gpsimd.memset(total[:], 0.0))
                link(nc.gpsimd.memset(place[:], 0.0))
                for odd in range(2):
                    for half in range(2):
                        v = place[:, odd, :]
                        link(nc.gpsimd.affine_select(out=v, in_=v, compare_op=ALU.not_equal, fill=1.0,
                                                     base=64 * (odd - half), pattern=[[-1, P]], channel_multiplier=1))
                    v = place[:, odd, 64 * (1 - odd):64 * (2 - odd)]
                    link(nc.gpsimd.memset(v, 0.0))
        folded_last = c.enter_context(sbuf(nc, "cl_folded", [P, EW // 2], F32))
        whole = c.enter_context(sbuf(nc, "cl_whole", [P, 2, FOLD], I32))
        digits = c.enter_context(sbuf(nc, "cl_digits", [P, 2, FOLD], BF16))

        def count_fold(width):
            steps = width // SUB
            with stage(nc, "chained", "hot_ready", "multiplied", "added") as (block, chained, hot_ready, multiplied,
                                                                               added):
                @block.vector
                def _(dve):
                    link = linker(dve, chained)
                    fold(nc, link, e.last[:], folded_last[:], width)
                    low, high = whole[:, 0, 0:width], whole[:, 1, 0:width]
                    link(nc.vector.tensor_scalar(low, folded_last[:, 0:width], -1.0, None, ALU.add))
                    link(nc.vector.tensor_scalar(high, low, 6, None, ALU.logical_shift_right))
                    link(nc.vector.tensor_scalar(low, low, 63, None, ALU.bitwise_and))
                    link(nc.vector.tensor_copy(digits[:, :, 0:width], whole[:, :, 0:width]))
                    for s in range(steps):
                        if s >= 2:
                            dve.wait_ge(multiplied, s - 1)
                        for d in range(2):
                            for v in range(64):
                                nc.vector.tensor_scalar(hot[:, s % 2, d, :, v, :], digits[:, d, s * SUB:(
                                    s + 1) * SUB].rearrange("p (a m) -> p a m", a=2), float(v), None,
                                                        ALU.is_equal).then_inc(hot_ready, 1)
                    dve.wait_ge(multiplied, steps)
                    nc.vector.tensor_tensor(total[:], total[:], ps[:, 0:P], ALU.add).then_inc(added, 1)

                @block.tensor
                def _(pe):
                    for s in range(steps):
                        pe.wait_ge(hot_ready, 128 * (s + 1))
                        for m in range(SUB // 2):
                            low, high = (hot[:, s % 2, d, :, :, m].rearrange("p a v -> p (a v)") for d in range(2))
                            last = nc.tensor.matmul(ps[:, 0:P], low, high, start=(s == 0 and m == 0),
                                                    stop=(s == steps - 1 and m == SUB // 2 - 1))
                        last.then_inc(multiplied, 1)

        count_fold(FOLD)
        count_fold(FOLD // 2)
        sizes = c.enter_context(sbuf(nc, "cl_sizes", [P, 2, SUB], F32))

        def largest_class(link):
            for half in range(2):
                part = e.last[:, half * EW // 2:(half + 1) * EW // 2]
                link(nc.vector.tensor_scalar(folded_last[:], part, 0.5, None, ALU.is_gt))
                link(nc.vector.tensor_reduce(sizes[:, half], folded_last[:].rearrange("p (b w) -> p w b", w=SUB), AX.X,
                                             ALU.add))
            link(nc.vector.tensor_tensor(sizes[:, 0], sizes[:, 0], sizes[:, 1], ALU.add))
            link(nc.vector.tensor_reduce(e.most[:, 0:1], sizes[:, 0], AX.X, ALU.max))

        most = largest(nc, e, largest_class)
        with nc.Fori(0, most) as i:
            count_fold(SUB)
        with stage(nc, "folded", "placed", "copied") as (block, folded, placed, copied):
            @block.tensor
            def _(pe):
                pe.wait_ge(folded, 2)
                for odd in range(2):
                    rhs = corner[:].rearrange("p (t o) -> p o t", o=2)[:, odd, :]
                    last = nc.tensor.matmul(ps2[:, 0:MT], place[:, odd, :], rhs, start=(odd == 0), stop=(odd == 1))
                last.then_inc(placed, 1)

            @block.vector
            def _(dve):
                for half in range(2):
                    r = slice(64 * half, 64 * half + 64)
                    nc.vector.tensor_copy(corner[r, :], total[r, 64 * half:64 * half + 64]).then_inc(folded, 1)
                dve.wait_ge(placed, 1)
                nc.vector.tensor_copy(e.count[:], ps2[:, 0:MT]).then_inc(copied, 1)


def largest(nc, e, measure):
    with stage(nc, "chained", "measured", "reduced", "whole") as (block, chained, measured, reduced, whole):
        @block.vector
        def _(dve):
            measure(linker(dve, chained))
            nc.vector.tensor_copy(e.most[:, 2:3], e.most[:, 0:1]).then_inc(measured, 1)
            dve.wait_ge(reduced, 1)
            nc.vector.tensor_copy(e.most_int[:], e.most[:, 1:2]).then_inc(whole, 1)

        @block.gpsimd
        def _(pool):
            pool.wait_ge(measured, 1)
            nc.gpsimd.partition_all_reduce(e.most[:, 1:2], e.most[:, 2:3], P,
                                           bass.bass_isa.ReduceOp.max).then_inc(reduced, 1)
    value = nc.values_load(e.most_int[0:1, 0:1], min_val=0, max_val=EDGES)
    nc.all_engine_barrier(sem_only=True)
    return value


def count_above(nc, link, candidates, low, scratch, out):
    link(nc.vector.tensor_scalar(scratch, candidates, low, None, ALU.is_gt, ALU.add, accum_out=out))


def take_largest(nc, link, candidates, out, rounds):
    for r in range(rounds):
        o_ = out[:, 8 * r:8 * r + 8]
        link(nc.vector.max(o_, candidates))
        link(nc.vector.match_replace(candidates, o_, candidates, 0.0))


def gather_lists(nc, e, take, lists, candidates, high, spread):
    with stage(nc, "chained", "stored", "loaded") as (block, chained, stored, loaded):
        @block.vector
        def _(dve):
            link = linker(dve, chained)
            take(link)
            dve.wait_ge(loaded, 16 * CLASSES)
            link(nc.vector.scalar_tensor_tensor(candidates, candidates, high, candidates, ALU.is_le, ALU.mult))

        @block.sync
        def _(sp):
            sp.wait_ge(chained, 2 * ROUNDS)
            sp.dma_start(lists, e.list[:]).then_inc(stored, 16)
            sp.wait_ge(stored, 16)
            for c in range(CLASSES):
                sp.dma_start(candidates[16 * c:16 * c + 16, :], spread(lists, c)).then_inc(loaded, 16)


def sort_into_bands(nc, e, candidates):
    with ExitStack() as c:
        found = c.enter_context(sbuf(nc, "sb_found", [P, LIST], F32))
        scratch = c.enter_context(sbuf(nc, "sb_scratch", [P, LIST], F32))

        def measure(link):
            take_largest(nc, link, candidates, found, ROUNDS)
            for g in range(BANDS):
                low, high, o_ = e.band_low[:, g:g + 1], e.band_low[:, g + 1:g + 2], e.banded[:, g]
                link(nc.vector.scalar_tensor_tensor(o_, found[:], low, found[:], ALU.is_gt, ALU.mult))
                link(nc.vector.scalar_tensor_tensor(o_, o_, high, o_, ALU.is_le, ALU.mult))
                count_above(nc, link, o_, 0.5, scratch[:], e.most[:, 4 + g:5 + g])
            link(nc.vector.tensor_reduce(e.most[:, 0:1], e.most[:, 4:4 + BANDS], AX.X, ALU.max))

        return largest(nc, e, measure)


def take_in(nc, k, e):
    with ExitStack() as c:
        def sb(name, shape, dt=F32):
            return c.enter_context(sbuf(nc, name, shape, dt))

        ALL = BANDS * SLOTS
        code, f = sb("ti_code", [P, ALL]), sb("ti_f", [P, 3, ALL])
        whole = sb("ti_int", [P, 3, ALL], I32)
        row = sb("ti_row", [P, ALL, FEAT])
        hot = sb("ti_hot", [P, BAND, SLOTS])
        z, p, y = (sb(f"ti_{n}", [P, GH, BAND, SLOTS]) for n in "zpy")
        n = sb("ti_new", [P, 5, GH, BAND])
        block, chained, indexed, shifted, exped, *gathered = c.enter_context(stage(
            nc, "chained", "indexed", "shifted", "exped", *(f"gathered_{g}" for g in range(BANDS)), pool_dma=True))

        def take_in_band(dve, link, g, tile, row):
            tiles = slice(g * BAND, (g + 1) * BAND)
            wide = [P, BAND, SLOTS]
            link(nc.vector.tensor_tensor(hot[:], e.tiles[:, tiles].unsqueeze(2).broadcast_to(wide),
                                         tile.unsqueeze(1).broadcast_to(wide), ALU.is_equal))
            link(nc.vector.tensor_scalar(hot[:], hot[:], -NEG, NEG, ALU.mult, ALU.add))
            top, shift, a_dst = (x[:, :, tiles] for x in (e.top, e.shift, e.a_dst))
            best, change, total, part, own = (n[:, i] for i in range(5))
            link(nc.vector.tensor_copy(own, a_dst))
            dve.wait_ge(gathered[g], 16 * SLOTS)

            def of_rows(i):
                return row[:, :, i].unsqueeze(1).broadcast_to(wide)

            def flat(x):
                return x.rearrange("p h t -> p (h t)")

            def over_slots(x):
                return flat(x).unsqueeze(2).broadcast_to([P, GH * BAND, SLOTS])

            for h in range(GH):
                link(nc.vector.tensor_tensor(z[:, h], hot[:], of_rows(h), ALU.add))
            z3, p3, y3 = (x[:].rearrange("p h t j -> p (h t) j") for x in (z, p, y))
            link(nc.vector.tensor_reduce(flat(best), z3, AX.X, ALU.max))
            link(nc.vector.tensor_tensor(top, top, best, ALU.max))
            link(nc.vector.tensor_tensor(best, top, own, ALU.add))
            link(nc.vector.scalar_tensor_tensor(best, best, 0.2, best, ALU.mult, ALU.max))
            link(nc.vector.tensor_tensor(change, shift, best, ALU.subtract))
            link(nc.vector.tensor_copy(shift, best))
            link(nc.vector.tensor_tensor(z3, z3, over_slots(own), ALU.add))
            link(nc.vector.scalar_tensor_tensor(z3, z3, 0.2, z3, ALU.mult, ALU.max))
            nc.vector.tensor_tensor(z3, z3, over_slots(best), ALU.subtract).then_inc(shifted, 1)
            dve.wait_ge(exped, 2 * (g + 1))
            link(nc.vector.tensor_reduce(flat(total), p3, AX.X, ALU.add))
            link(nc.vector.tensor_tensor(e.den[:, :, tiles], e.den[:, :, tiles], change, ALU.mult))
            link(nc.vector.tensor_tensor(e.den[:, :, tiles], e.den[:, :, tiles], total, ALU.add))
            for v in range(GE):
                num = e.num[:, v][:, :, tiles]
                for h in range(GH):
                    link(nc.vector.tensor_tensor(y[:, h], p[:, h], of_rows(GH + h * GE + v), ALU.mult))
                link(nc.vector.tensor_reduce(flat(part), y3, AX.X, ALU.add))
                link(nc.vector.tensor_tensor(num, num, change, ALU.mult))
                link(nc.vector.tensor_tensor(num, num, part, ALU.add))

        @block.vector
        def _(dve):
            link = linker(dve, chained)
            for g in range(BANDS):
                take_largest(nc, link, e.banded[:, g], code[:, g * SLOTS:(g + 1) * SLOTS], SLOTS // 8)
            valid, local, tile = (f[:, i] for i in range(3))
            link(nc.vector.tensor_scalar(valid, code[:], e.bounds[:, 2:3], None, ALU.is_gt))
            link(nc.vector.tensor_scalar(local, code[:], e.bounds[:, 2:3], -1.0, ALU.subtract, ALU.add))
            link(nc.vector.tensor_tensor(local, local, valid, ALU.mult))
            link(nc.vector.tensor_copy(whole[:, 0], local))
            nc.vector.tensor_scalar(whole[:, 1], whole[:, 0], M - 1, None, ALU.bitwise_and).then_inc(indexed, 1)
            link(nc.vector.tensor_scalar(whole[:, 2], whole[:, 0], 12, None, ALU.logical_shift_right))
            link(nc.vector.tensor_copy(tile, whole[:, 2]))
            link(nc.vector.scalar_tensor_tensor(tile, tile, 1.0, valid, ALU.add, ALU.mult))
            for g in range(BANDS):
                take_in_band(dve, link, g, tile[:, g * SLOTS:(g + 1) * SLOTS], row[:, g * SLOTS:(g + 1) * SLOTS])

        @block.gpsimd
        def _(pool):
            pool.wait_ge(indexed, 1)
            for g in range(BANDS):
                for j in range(g * SLOTS, (g + 1) * SLOTS):
                    nc.gpsimd.indirect_dma_start(row[:, j, :], None, e.features, bass.IndirectOffsetOnAxis(
                        ap=whole[:, 1, j:j + 1], axis=0)).then_inc(gathered[g], 16)
            for g in range(BANDS):
                pool.wait_ge(gathered[g], 16 * SLOTS)

        @block.scalar
        def _(act):
            for g in range(BANDS):
                act.wait_ge(shifted, g + 1)
                nc.scalar.activation(n[:, 1], n[:, 1], ACT.Exp).then_inc(exped, 1)
                nc.scalar.activation(p[:], z[:], ACT.Exp).then_inc(exped, 1)


def start_sums(nc, k, e):
    with ExitStack() as c:
        def sb(name, shape, dt=F32):
            return c.enter_context(sbuf(nc, name, shape, dt))

        prod = sb("ss_prod", [P, MT, GH * GE])
        rows = sb("ss_rows", [P, MT, FEAT])
        last_row = sb("ss_last", [P, FEAT])
        n = sb("ss_n", [P, 4, GH, MT])
        block, chained, stored, loaded, exped = c.enter_context(stage(nc, "chained", "stored", "loaded", "exped"))
        h3 = k.h_tm[:].rearrange("p b t f -> p (b t) f")
        own, last, e_own, e_last = (n[:, i] for i in range(4))

        @block.vector
        def _(dve):
            link = linker(dve, chained)
            for i in range(2):
                link(nc.vector.tensor_tensor(prod[:], h3, k.gat[:, 3 + i].unsqueeze(1).broadcast_to([P, MT, GH * GE]),
                                             ALU.mult))
                out = (own if i == 0 else e.a_dst[:]).rearrange("p h t -> p t h")
                link(nc.vector.tensor_reduce(out, prod[:].rearrange("p t (h v) -> p t h v", v=GE), AX.X, ALU.add))
            link(nc.vector.tensor_copy(rows[:, :, 0:GH], own.rearrange("p h t -> p t h")))
            link(nc.vector.tensor_copy(rows[:, :, GH:FEAT], h3))
            dve.wait_ge(loaded, 16)
            link(nc.vector.tensor_scalar(last[:, 0], e.count[:], 0.5, NEG, ALU.is_lt, ALU.mult))
            for h in range(GH - 1, -1, -1):
                link(nc.vector.tensor_scalar(last[:, h], last[:, 0], last_row[:, h:h + 1], None, ALU.add))
            link(nc.vector.tensor_tensor(e.top[:], own, last, ALU.max))
            for x, out in ((own, e_own), (last, e_last), (e.top[:], e.shift[:])):
                link(nc.vector.tensor_tensor(out, x, e.a_dst[:], ALU.add))
                link(nc.vector.scalar_tensor_tensor(out, out, 0.2, out, ALU.mult, ALU.max))
            for x in (e_own, e_last):
                link(nc.vector.tensor_tensor(x, x, e.shift[:], ALU.subtract))
            dve.wait_ge(exped, 1)
            link(nc.vector.tensor_tensor(e_last, e_last, e.count[:].unsqueeze(1).broadcast_to([P, GH, MT]), ALU.mult))
            link(nc.vector.tensor_tensor(e.den[:], e_own, e_last, ALU.add))
            for v in range(GE):
                value = h3.rearrange("p t (h v) -> p v h t", v=GE)[:, v]
                link(nc.vector.tensor_tensor(e.num[:, v], e_own, value, ALU.mult))
                for h in range(GH):
                    link(nc.vector.scalar_tensor_tensor(e.num[:, v, h], e_last[:, h],
                                                        last_row[:, GH + h * GE + v:GH + h * GE + v + 1],
                                                        e.num[:, v, h], ALU.mult, ALU.add))

        @block.sync
        def _(sp):
            sp.wait_ge(chained, 6)
            sp.dma_start(e.features.rearrange("(t p) f -> p t f", p=P), rows[:]).then_inc(stored, 16)
            sp.wait_ge(stored, 16)
            sp.dma_start(last_row[:], e.features[M - 1].partition_broadcast(P)).then_inc(loaded, 16)

        @block.scalar
        def _(act):
            act.wait_ge(chained, 6 + 1 + GH + 1 + 6 + 2)
            nc.scalar.activation(n[:, 2:4], n[:, 2:4], ACT.Exp).then_inc(exped, 1)


def choose_experts(nc, k, e):
    with ExitStack() as c:
        def sb(name, shape):
            return c.enter_context(sbuf(nc, name, shape, F32))

        agg, sq = sb("ch_agg", [P, MT, GH * GE]), sb("ch_sq", [P, MT, GH * GE])
        st = sb("ch_st", [P, 6, MT])
        s, rank = sb("ch_s", [P, GE, MT]), sb("ch_rank", [P, GE, MT])
        block, chained, rooted, exped, final = c.enter_context(stage(nc, "chained", "rooted", "exped", "final"))

        @block.vector
        def _(dve):
            link = linker(dve, chained)
            link(nc.vector.tensor_scalar(e.den[:], e.den[:], 1e-16, None, ALU.add))
            link(nc.vector.reciprocal(e.den[:], e.den[:]))
            for v in range(GE):
                out = agg[:].rearrange("p t (h v) -> p v h t", v=GE)[:, v]
                link(nc.vector.tensor_tensor(out, e.num[:, v], e.den[:], ALU.mult))

            def param(i):
                return k.gat[:, i].unsqueeze(1).broadcast_to([P, MT, GH * GE])

            def wide(a):
                return a.unsqueeze(2).broadcast_to([P, MT, GH * GE])

            link(nc.vector.tensor_tensor(agg[:], agg[:], param(0), ALU.add))
            link(nc.vector.tensor_reduce(st[:, 0], agg[:], AX.X, ALU.add))
            link(nc.vector.tensor_scalar(st[:, 0], st[:, 0], 1.0 / 16, None, ALU.mult))
            link(nc.vector.tensor_tensor(agg[:], agg[:], wide(st[:, 0]), ALU.subtract))
            link(nc.vector.tensor_tensor(sq[:], agg[:], agg[:], ALU.mult))
            link(nc.vector.tensor_reduce(st[:, 1], sq[:], AX.X, ALU.add))
            dve.wait_ge(rooted, 1)
            link(nc.vector.reciprocal(st[:, 1], st[:, 1]))
            link(nc.vector.tensor_tensor(agg[:], agg[:], wide(st[:, 1]), ALU.mult))
            link(nc.vector.tensor_tensor(agg[:], agg[:], param(1), ALU.mult))
            link(nc.vector.tensor_tensor(agg[:], agg[:], param(2), ALU.add))
            link(nc.vector.tensor_reduce(s[:].rearrange("p v t -> p t v"), agg[:].rearrange("p t (h v) -> p t v h", v=GE),
                                         AX.X, ALU.add))
            link(nc.vector.tensor_scalar(s[:], s[:], 1.0 / GH, None, ALU.mult))
            for i in range(GE):
                link(nc.vector.memset(rank[:, i], float(GE - 1 - i)))
            for i in range(GE):
                for j in range(i + 1, GE):
                    link(nc.vector.tensor_tensor(st[:, 2], s[:, i], s[:, j], ALU.is_ge))
                    link(nc.vector.tensor_tensor(rank[:, j], rank[:, j], st[:, 2], ALU.add))
                    link(nc.vector.tensor_tensor(rank[:, i], rank[:, i], st[:, 2], ALU.subtract))
            link(nc.vector.tensor_scalar(rank[:], rank[:], 1.5, None, ALU.is_lt))
            link(nc.vector.tensor_reduce(st[:, 3], s[:].rearrange("p v t -> p t v"), AX.X, ALU.max))
            nc.vector.tensor_tensor(s[:], s[:], st[:, 3].unsqueeze(1).broadcast_to([P, GE, MT]), ALU.subtract).then_inc(final, 1)
            dve.wait_ge(exped, 1)
            link(nc.vector.tensor_tensor(s[:], s[:], rank[:], ALU.mult))
            link(nc.vector.tensor_reduce(st[:, 4], s[:].rearrange("p v t -> p t v"), AX.X, ALU.add))
            link(nc.vector.reciprocal(st[:, 4], st[:, 4]))
            link(nc.vector.tensor_tensor(k.gates[:].rearrange("p b t v -> p v (b t)"), s[:],
                                         st[:, 4].unsqueeze(1).broadcast_to([P, GE, MT]), ALU.mult))

        @block.scalar
        def _(act):
            act.wait_ge(chained, 2 + GE + 6)
            nc.scalar.activation(st[:, 1], st[:, 1], ACT.Sqrt, bias=k.eps[:, 0:1], scale=1.0 / 16).then_inc(rooted, 1)
            act.wait_ge(final, 1)
            nc.scalar.activation(s[:], s[:], ACT.Exp).then_inc(exped, 1)


class Edges:
    pass


def route(nc, k, edge_index):
    with ExitStack() as c:
        def sb(name, shape, dt=F32):
            return c.enter_context(sbuf(nc, name, shape, dt))

        e = Edges()
        e.edge_index = edge_index
        e.codes = sb("codes", [P, EW])
        e.count = sb("count", [P, MT])
        e.list = sb("list", [P, LIST])
        e.most, e.most_int = sb("most", [P, 8]), sb("most_int", [P, 1], I32)
        e.bounds = sb("bounds", [P, 4])
        bounds_int = sb("bounds_int", [P, 2], I32)
        e.tiles = sb("tiles", [P, MT])
        e.features = nc.dram_tensor("features", [M, FEAT], F32).ap()
        lists = [nc.dram_tensor(f"lists_{i}", [P, LIST], F32).ap() for i in range(2)]
        with ExitStack() as c2:
            e.last = c2.enter_context(sbuf(nc, "last", [P, EW], F32))
            code_edges(nc, k, e)
            count_last(nc, k, e)
        e.top, e.shift, e.den, e.a_dst = (sb(f"gat_{n}", [P, GH, MT]) for n in ("top", "shift", "den", "a_dst"))
        e.num = sb("gat_num", [P, GE, GH, MT])
        by_class = sb("by_class", [P, CLASSES * LIST])
        by_owner = sb("by_owner", [P, 16 * LIST])
        folded = sb("folded", [P, EW // 2])
        halves = sb("halves", [P, EW // 2])
        scratch = sb("count_scratch", [P, EW])
        e.band_low = sb("band_low", [P, BANDS + 1])
        e.banded = sb("banded", [P, BANDS, LIST])

        with stage(nc, "made", "chained") as (block, made, chained):
            @block.gpsimd
            def _(pool):
                nc.gpsimd.iota(bounds_int[:, 0:1], [[0, 1]], base=0, channel_multiplier=1 << 17).then_inc(made, 1)
                nc.gpsimd.iota(e.tiles[:], [[1, MT]], base=1, channel_multiplier=0,
                               allow_small_or_imprecise_dtypes=True).then_inc(made, 1)

            @block.vector
            def _(dve):
                link = linker(dve, chained)
                dve.wait_ge(made, 2)
                link(nc.vector.tensor_copy(e.bounds[:, 2:3], bounds_int[:, 0:1]))
                link(nc.vector.tensor_scalar(e.bounds[:, 3:4], e.bounds[:, 2:3], float(1 << 17), None, ALU.add))
                for g in range(BANDS + 1):
                    link(nc.vector.tensor_scalar(e.band_low[:, g:g + 1], e.bounds[:, 2:3], float(g * BAND << 12), None,
                                                 ALU.add))
                link(nc.vector.tensor_scalar(bounds_int[:, 1:2], bounds_int[:, 0:1], 21, 21, ALU.logical_shift_right,
                                             ALU.logical_shift_left))
                link(nc.vector.tensor_copy(e.bounds[:, 0:1], bounds_int[:, 1:2]))
                link(nc.vector.tensor_scalar(e.bounds[:, 1:2], e.bounds[:, 0:1], float(1 << 21), None, ALU.add))

        start_sums(nc, k, e)

        def to_class(lists, c):
            return lists.rearrange("(j q) n -> j (q n)", q=CLASSES)

        def to_owners(lists, c):
            return lists[16 * c:16 * c + 16, :].rearrange("j n -> (j n)").partition_broadcast(16)

        with stage(nc, "chained") as (block, chained):
            @block.vector
            def _(dve):
                link = linker(dve, chained)
                for i in range(2):
                    fold(nc, link, e.codes[:], halves[:], FOLD)
                    link(nc.vector.tensor_copy(folded[:, i * FOLD:(i + 1) * FOLD], halves[:, 0:FOLD]))
        candidates = folded[:, 0:2 * FOLD]

        def lists_needed(link):
            count_above(nc, link, candidates, 0.5, scratch[:, 0:2 * FOLD], e.most[:, 4:5])
            count_above(nc, link, e.codes[:], 0.5, scratch[:], e.most[:, 5:6])
            link(nc.vector.tensor_scalar(e.most[:, 5:6], e.most[:, 5:6], float((ROUNDS - REST) // REST), None, ALU.mult))
            link(nc.vector.tensor_reduce(e.most[:, 0:1], e.most[:, 4:6], AX.X, ALU.max))

        def take_from_codes(link):
            cut = 8 * (ROUNDS - REST)
            take_largest(nc, link, candidates, e.list[:, 0:cut], ROUNDS - REST)
            take_largest(nc, link, e.codes[:], e.list[:, cut:LIST], REST)

        def take_from(x):
            return lambda link: take_largest(nc, link, x, e.list[:], ROUNDS)

        def above(x, low):
            return lambda link: count_above(nc, link, x, low, scratch[:, 0:x.shape[1]], e.most[:, 0:1])

        most = largest(nc, e, lists_needed)
        with nc.Fori(0, most, 8 * (ROUNDS - REST)):
            gather_lists(nc, e, take_from_codes, lists[0], by_class[:], e.bounds[:, 1:2], to_class)
            most_a = largest(nc, e, above(by_class[:], e.bounds[:, 0:1]))
            with nc.Fori(0, most_a, LIST):
                gather_lists(nc, e, take_from(by_class[:]), lists[1], by_owner[:], e.bounds[:, 3:4], to_owners)
                most_b = largest(nc, e, above(by_owner[:], e.bounds[:, 2:3]))
                with nc.Fori(0, most_b, LIST):
                    most_c = sort_into_bands(nc, e, by_owner[:])
                    with nc.Fori(0, most_c, SLOTS):
                        take_in(nc, k, e)
        choose_experts(nc, k, e)



class Kept:
    pass


def build(nc, w, out):
    with ExitStack() as c:
        def sb(name, shape, dt=F32):
            return c.enter_context(sbuf(nc, name, shape, dt))

        k = Kept()
        k.xn_cm = sb("xn_cm", [P, B, N])
        k.x_cm = k.xn_cm
        k.t_tm = sb("t_tm", [P, B, NT, P])
        k.h_tm, k.gates = sb("h_tm", [P, B, NT, GH * GE]), sb("gates", [P, B, NT, E2])
        k.ident, k.mean16, k.mean4, k.block32 = (sb(n, [P, P]) for n in ("ident", "mean16", "mean4", "block32"))
        k.place16, k.place32 = sb("place16", [P, 25 * 8]), sb("place32", [P, 9 * 4])
        k.spread16, k.spread32 = sb("spread16", [120, SPREAD * P], BF16), sb("spread32", [60, SPREAD * P], BF16)
        k.ones_row, k.eps, k.window_mask = sb("ones_row", [1, P]), sb("eps", [P, 2]), sb("window_mask", [P, NT, 5])
        k.turned = sb("turned", [P, 25, P])
        k.t_g_in, k.t_g_out, k.t_t_in, k.t_t_out, k.t_fus1, k.t_fus2, k.t_ffn1, k.t_ffn2, k.t_q2 = (
            5, 8, 9, 12, 13, 17, 19, 21, 23)
        k.cols, k.qb, k.bn = sb("cols", [P, P]), sb("qb", [P, 4]), sb("bn", [P, 2, 2, E1])
        k.ident_b = sb("ident_b", [P, P], BF16)
        k.parts_dram = nc.dram_tensor("parts_dram", [2, 3, P, N], BF16).ap()
        k.parted = c.enter_context(nc.semaphore("parted"))
        k.stacked = [c.enter_context(nc.semaphore(f"stacked_{g}")) for g in range(2)]
        k.w_kv, k.w_o2 = sb("w_kv", [P, 4 * P]), sb("w_o2", [P, 2, P])
        k.m1, k.m2, k.mo = (sb(n, [P, E1, P]) for n in ("m1", "m2", "mo"))
        k.mo_b, k.wr, k.mix, k.mix_t = sb("mo_b", [E1, P]), sb("wr", [P, E1]), sb("mix", [P, NT, E1]), sb("mix_t", [E1, N])
        k.w_gat, k.gat = sb("w_gat", [P, GH * GE]), sb("gat", [P, 5, GH * GE])
        k.x1, k.x2, k.x2_b = sb("x1", [P, E2, 2 * P]), sb("x2", [P, E2, 2, P]), sb("x2_b", [E2, P])
        k.rows, k.wide = sb("rows", [1, 4, P]), sb("wide", [P, 4, P])

        make_constants(nc, k)
        load_weights(nc, k, w)
        first_layers(nc, k)
        with nc.Fori(0, B) as b:
            linear_attention(nc, k, b)
        mixture_weights(nc, k)
        with nc.Fori(0, B) as b:
            batch_normed_mixture(nc, k, b)
        with dense_buffers(nc, k, 16), nc.Fori(0, B) as b:
            two_attentions(nc, k, b)
        route(nc, k, w["L3_ffn_edge_index"])
        with nc.Fori(0, B) as b:
            gelu_mixture(nc, k, b, out)



NAMES = """x L0_conv_gn_gamma L0_conv_gn_beta L0_conv_qkv_w L0_conv_qkv_b L0_conv_proj_w L0_conv_proj_b L1_conv_w_out
L1_conv_b_out L2_attn_w_qkv L2_attn_w_out L2_attn_b_out L2_ffn_Wr L2_ffn_br L2_ffn_W1 L2_ffn_b1 L2_ffn_g1 L2_ffn_be1
L2_ffn_m1 L2_ffn_v1 L2_ffn_W2 L2_ffn_b2 L2_ffn_g2 L2_ffn_be2 L2_ffn_m2 L2_ffn_v2 L2_ffn_Wo L2_ffn_bo L3_attn_g_in_w
L3_attn_g_in_b L3_attn_g_out_w L3_attn_g_out_b L3_attn_t_in_w L3_attn_t_in_b L3_attn_t_out_w L3_attn_t_out_b
L3_attn_fus_w1 L3_attn_fus_b1 L3_attn_fus_w2 L3_attn_fus_b2 L3_attn_ffn_w1 L3_attn_ffn_b1 L3_attn_ffn_w2
L3_attn_ffn_b2 L3_attn_gn_g L3_attn_gn_b L3_attn_fn_g L3_attn_fn_b L3_ffn_W_gat L3_ffn_att_src L3_ffn_att_dst
L3_ffn_b_gat L3_ffn_ln_gamma L3_ffn_ln_beta L3_ffn_W1 L3_ffn_b1 L3_ffn_W2 L3_ffn_b2 L3_ffn_edge_index""".split()


def kernel(**inputs):
    import numpy as np
    import concourse.bacc as bacc
    from concourse.bass_utils import run_bass_kernel_spmd

    nc = bacc.Bacc("TRN2", target_bir_lowering=False, num_devices=1)
    arrays = {name: np.ascontiguousarray(inputs[name]) for name in NAMES}
    w = {name: nc.dram_tensor(name, a.shape, mybir.dt.from_np(a.dtype), kind="ExternalInput").ap()
         for name, a in arrays.items()}
    out = nc.dram_tensor("out", [B, P, IMG, IMG], F32, kind="ExternalOutput").ap()
    build(nc, w, out)
    return run_bass_kernel_spmd(nc, [arrays], core_ids=[0]).results[0]["out"]
```

```python
import itertools
from contextlib import ExitStack, contextmanager

import concourse.bass as bass
from concourse import mybir

F32 = mybir.dt.float32
BF16 = mybir.dt.bfloat16
I32 = mybir.dt.int32
ALU = mybir.AluOpType
ACT = mybir.ActivationFunctionType
AX = mybir.AxisListType

P = 128
B, IMG = 4, 32
N = IMG * IMG
NT = N // P
M = B * N
MT = M // P
BANK = 512
NC2 = N // BANK
ROW = 32
E1, E2 = 8, 4
GH, GE = 4, 4
EDGES = 524288
EW = EDGES // P
NEG = -1.0e30


SERIAL = itertools.count()


LAST_STAGE = ExitStack()


@contextmanager
def stage(nc, *names, pool_dma=False):
    with ExitStack() as c:
        sems = [c.enter_context(nc.semaphore(f"{n}_{next(SERIAL)}")) for n in names]
        LAST_STAGE.close()
        with nc.Block() as block:
            yield (block, *sems)
        nums = sorted(s.num for s in sems)
        cuts = [i for i in range(1, len(nums)) if nums[i] != nums[i - 1] + 1]
        for i, j in zip([0] + cuts, cuts + [len(nums)]):
            if nums and pool_dma:
                nc.gpsimd.dma_reset(range(nums[i], nums[j - 1] + 1))
            if nums:
                nc.gpsimd.sem_clear(range(nums[i], nums[j - 1] + 1))
        LAST_STAGE.push(c.pop_all())


@contextmanager
def loop(nc, *bounds):
    with nc.Fori(*bounds) as i:
        yield i
        nc.all_engine_barrier(sem_only=True)
    nc.all_engine_barrier(sem_only=True)


def sbuf(nc, name, shape, dt):
    return nc.sbuf_tensor(f"{name}_{next(SERIAL)}", shape, dt)


def psum(nc, name, shape, dt):
    return nc.psum_tensor(f"{name}_{next(SERIAL)}", shape, dt)


def linker(engine, done):
    count = [0]

    def link(instruction):
        count[0] += 1
        instruction.then_inc(done, 1)
        engine.wait_ge(done, count[0])

    return link


def affine(nc, on_act, out, in_, scale=1.0, bias=0.0, func=ACT.Identity):
    if on_act:
        return nc.scalar.activation(out, in_, func, bias=bias, scale=scale)
    return nc.vector.tensor_scalar(out, in_, scale, bias, ALU.mult, ALU.add)


def product_pass(nc, ps, n, product, evacuate, by="ad"):
    ring = ps.shape[1]
    with stage(nc, "product_ready", "off_by_act", "off_by_dve") as (block, ready, by_act, by_dve):
        done = {"a": by_act, "d": by_dve}
        share = {e: [i for i in range(n) if by[i % len(by)] == e] for e in "ad"}

        @block.tensor
        def _(pe):
            for i in range(n):
                if i >= ring:
                    e = by[(i - ring) % len(by)]
                    pe.wait_ge(done[e], share[e].index(i - ring) + 1)
                product(i, ps[:, i % ring]).then_inc(ready, 1)

        @block.scalar
        def _(act):
            for i in share["a"]:
                act.wait_ge(ready, i + 1)
                evacuate(True, i, ps[:, i % ring]).then_inc(by_act, 1)

        @block.vector
        def _(dve):
            for i in share["d"]:
                dve.wait_ge(ready, i + 1)
                evacuate(False, i, ps[:, i % ring]).then_inc(by_dve, 1)


def turn_tiles(nc, ps, ident, pairs, combine=None):
    def product(i, bank):
        for k, tile in enumerate(pairs[i][0]):
            last = nc.tensor.transpose(bank[0:tile.shape[1], k * P:(k + 1) * P], tile, ident[:])
        return last

    def evacuate(on_act, i, bank):
        tiles, out = pairs[i]
        in_ = bank[0:out.shape[0], 0:len(tiles) * P].rearrange("p (k n) -> p k n", n=P)
        if combine is not None:
            return combine(on_act, i, out, in_)
        if on_act:
            return nc.scalar.copy(out, in_)
        return nc.vector.tensor_copy(out, in_)

    product_pass(nc, ps, len(pairs), product, evacuate)



def make_constants(nc, k, link):
    def select(out, base, pattern, fill, compare):
        link(nc.gpsimd.affine_select(out=out, in_=out, compare_op=compare, fill=fill, base=base,
                                     pattern=pattern, channel_multiplier=1))

    def same_group(t, size, value):
        link(nc.gpsimd.memset(t[:], value))
        n = P // size
        if t.shape[1] == n:
            low, high, view = [[-size, n]], [[size, n]], t[:]
        else:
            low, high = [[-size, n], [0, size]], [[size, n], [0, size]]
            view = t[:].rearrange("p (n s) -> p n s", s=size)
        select(view, 0, low, 0.0, ALU.is_ge)
        link(nc.gpsimd.affine_select(out=view, in_=view, compare_op=ALU.is_ge, fill=0.0,
                                     base=size - 1, pattern=high, channel_multiplier=-1))

    link(nc.gpsimd.memset(k.ident[:], 0.0))
    select(k.ident[:], 0, [[-1, P]], 1.0, ALU.not_equal)
    link(nc.gpsimd.tensor_copy(k.ident_b[:], k.ident[:]))
    same_group(k.mean16, 16, 1.0 / 16)
    same_group(k.mean4, 4, 1.0 / 4)
    same_group(k.block32, 32, 1.0 / N)
    for t, d, shifts in ((k.place16, 16, 13), (k.place32, 32, 5)):
        link(nc.gpsimd.memset(t[:], 0.0))
        H = P // d
        same_group(t[:, (shifts - 1) * H:shifts * H], d, 1.0)
    for t, d in ((k.spread16, 16), (k.spread32, 32)):
        n = SPREAD * P // d
        link(nc.gpsimd.memset(t[:], 0.0))
        for part in range(3):
            select(t[:].rearrange("p (r d) -> p r d", d=d), -part * n, [[-1, n], [0, d]], 1.0, ALU.not_equal)
    link(nc.gpsimd.memset(k.ones_row[:], 1.0))
    link(nc.gpsimd.memset(k.eps[:, 0:1], 1e-5))
    link(nc.gpsimd.memset(k.eps[:, 1:2], 1e-3))
    link(nc.gpsimd.memset(k.window_mask[:], 0.0))
    for t, w in ((0, 0), (0, 1), (NT - 1, 3), (NT - 1, 4)):
        v = k.window_mask[:, t, w:w + 1]
        if t == 0:
            select(v, w - 2, [[0, 1]], NEG, ALU.is_ge)
        else:
            link(nc.gpsimd.affine_select(out=v, in_=v, compare_op=ALU.is_ge, fill=NEG,
                                         base=P - 1 - (w - 2), pattern=[[0, 1]],
                                         channel_multiplier=-1))


C_GN_G, C_GN_B, C_QKV_B, C_PROJ_B, C_L1_B = 0, 1, 2, 5, 6
C_MOE = 7
C_G_IN = C_MOE + 80
C_G_OUT, C_T_IN, C_T_OUT, C_FUS1, C_FFN1, C_B1 = C_G_IN + 3, C_G_IN + 4, C_G_IN + 7, C_G_IN + 8, C_G_IN + 10, C_G_IN + 12
C_ROWS = C_B1 + 2 * E2


def load_weights(nc, k, w):
    with ExitStack() as c:
        table = c.enter_context(sbuf(nc, "table", [P, P], F32))
        raw = c.enter_context(sbuf(nc, "raw", [P, 27, P], F32))
        centre = c.enter_context(sbuf(nc, "centre", [P, 16], F32))
        ps = c.enter_context(psum(nc, "ps_w", [P, 8, BANK], F32))

        rows = [(C_GN_G, w["L0_conv_gn_gamma"]), (C_GN_B, w["L0_conv_gn_beta"]), (C_QKV_B, w["L0_conv_qkv_b"]),
                (C_PROJ_B, w["L0_conv_proj_b"]), (C_L1_B, w["L1_conv_b_out"])]
        rows += [(C_MOE + E1 * i, w[f"L2_ffn_{n}"]) for i, n in enumerate("b1 g1 be1 m1 v1 b2 g2 be2 m2 v2".split())]
        rows += [(C_G_IN, w["L3_attn_g_in_b"]), (C_G_OUT, w["L3_attn_g_out_b"]),
                 (C_T_IN, w["L3_attn_t_in_b"]), (C_T_OUT, w["L3_attn_t_out_b"]), (C_FUS1, w["L3_attn_fus_b1"]),
                 (C_FFN1, w["L3_attn_ffn_b1"]), (C_B1, w["L3_ffn_b1"])]

        def as_rows(a):
            if len(a.shape) == 1:
                return a.rearrange("(r n) -> r n", n=P)
            return a.rearrange("e (r n) -> (e r) n", n=P) if a.shape[1] > P else a

        sources = []
        for name in ("L0_conv_qkv_w", "L0_conv_proj_w", "L1_conv_w_out", "L3_attn_g_in_w", "L3_attn_g_out_w",
                     "L3_attn_t_in_w", "L3_attn_t_out_w", "L3_attn_fus_w1", "L3_attn_fus_w2", "L3_attn_ffn_w1",
                     "L3_attn_ffn_w2"):
            a = w[name]
            sources.append(a)
        sources.append(w["L2_attn_w_qkv"][:, 0:2 * P])
        n_tiles = [a.shape[0] * a.shape[1] // (P * P) for a in sources]

        straight = [(k.w_kv[:], w["L2_attn_w_qkv"][:, 2 * P:6 * P]),
                    (k.w_o2[:], w["L2_attn_w_out"].rearrange("(g e) o -> e g o", g=2)),
                    (k.m1[:], w["L2_ffn_W1"].rearrange("e d h -> d e h")),
                    (k.m2[:], w["L2_ffn_W2"].rearrange("e d h -> d e h")),
                    (k.mo[:], w["L2_ffn_Wo"].rearrange("e d h -> d e h")),
                    (k.mo_b[:], w["L2_ffn_bo"]), (k.wr[:], w["L2_ffn_Wr"]),
                    (k.w_gat[:], w["L3_ffn_W_gat"]),
                    (k.x1[:], w["L3_ffn_W1"].rearrange("e d h -> d e h")),
                    (k.x2[:], w["L3_ffn_W2"].rearrange("e (s h) d -> h e s d", h=P)),
                    (k.x2_b[:], w["L3_ffn_b2"])]
        straight += [(k.rows[0:1, i, 0:n], w[name].rearrange("(a n) -> a n", a=1)) for i, (name, n) in enumerate(
            (("L2_attn_b_out", P), ("L2_ffn_br", E1), ("L3_attn_fus_b2", P), ("L3_attn_ffn_b2", P)))]
        straight += [(k.wide[:, i, :], w[name].partition_broadcast(P)) for i, name in enumerate(
            ("L3_attn_gn_g", "L3_attn_gn_b", "L3_attn_fn_g", "L3_attn_fn_b"))]
        straight += [(k.gat[:, i, :], w[name].partition_broadcast(P)) for i, name in enumerate(
            ("L3_ffn_b_gat", "L3_ffn_ln_gamma", "L3_ffn_ln_beta"))]
        straight += [(k.gat[:, 3 + i, :], w[name].rearrange("h e -> (h e)").partition_broadcast(P))
                     for i, name in enumerate(("L3_ffn_att_src", "L3_ffn_att_dst"))]
        straight += [(k.x_cm[:], w["x"].rearrange("b c h w -> c b (h w)"))]

        with stage(nc, "cleared", "loaded", "made") as (block, cleared, loaded, made):
            n_row_loads = len(rows)

            @block.gpsimd
            def _(pool):
                nc.gpsimd.memset(table[:], 0.0).then_inc(cleared, 1)
                make_constants(nc, k, linker(pool, made))

            @block.sync
            def _(sp):
                for out, in_ in straight:
                    sp.dma_start(out, in_).then_inc(loaded, 16)
                sp.wait_ge(loaded, 16 * (len(straight) + len(sources) + n_row_loads))

            @block.scalar
            def _(act):
                for i, source in enumerate(sources):
                    first = sum(n_tiles[:i])
                    act.dma_start(raw[:, first:first + n_tiles[i], :].rearrange(
                        "p (r q) n -> p r q n", q=source.shape[1] // P), source.rearrange(
                        "(r p) (q n) -> p r q n", p=P, n=P)).then_inc(loaded, 16)
                act.wait_ge(cleared, 1)
                for r, a in rows:
                    v = as_rows(a)
                    act.dma_start(table[r:r + v.shape[0], :], v).then_inc(loaded, 16)

        tiles = [raw[:, i, :] for i in range(sum(n_tiles))]
        flat = []
        for i in range(0, len(tiles), 4):
            flat.append((tiles[i:i + 4], k.turned[:, i:min(i + 4, len(tiles)), :]))
        flat.append(([table[:]], k.cols[:].unsqueeze(1)))
        turn_tiles(nc, ps, k.ident, flat)

        with stage(nc, "scaled", "done") as (block, scaled, done):
            @block.scalar
            def _(act):
                for j in range(2):
                    v = C_MOE + E1 * (4 + 5 * j)
                    nc.scalar.activation(k.bn[:, j, 0, :], k.cols[:, v:v + E1], ACT.Sqrt,
                                         bias=k.eps[:, 1:2]).then_inc(scaled, 1)

            @block.vector
            def _(dve):
                link = linker(dve, done)
                w_kv = k.w_kv[:].rearrange("p (g d) -> p g d", d=32)
                link(nc.vector.tensor_reduce(centre[:], w_kv, AX.X, ALU.add))
                link(nc.vector.tensor_scalar(centre[:], centre[:], 1.0 / 32, None, ALU.mult))
                link(nc.vector.tensor_tensor(w_kv, w_kv, centre[:].unsqueeze(2).broadcast_to([P, 16, 32]), ALU.subtract))
                link(nc.vector.tensor_scalar(k.qb[:, 0:1], k.cols[:, C_QKV_B:C_QKV_B + 1], 32 ** -0.5, None, ALU.mult))
                link(nc.vector.tensor_scalar(k.qb[:, 1:2], k.cols[:, C_G_IN:C_G_IN + 1], 16 ** -0.5, None, ALU.mult))
                link(nc.vector.tensor_scalar(k.qb[:, 3:4], k.cols[:, C_T_IN:C_T_IN + 1], 32 ** -0.5, None, ALU.mult))
                dve.wait_ge(scaled, 2)
                for j in range(2):
                    b_, g_, be_, m_ = (k.cols[:, C_MOE + E1 * (i + 5 * j):C_MOE + E1 * (i + 5 * j + 1)] for i in range(4))
                    link(nc.vector.reciprocal(k.bn[:, j, 0, :], k.bn[:, j, 0, :]))
                    link(nc.vector.tensor_tensor(k.bn[:, j, 0, :], k.bn[:, j, 0, :], g_, ALU.mult))
                    link(nc.vector.tensor_tensor(k.bn[:, j, 1, :], b_, m_, ALU.subtract))
                    link(nc.vector.tensor_tensor(k.bn[:, j, 1, :], k.bn[:, j, 1, :], k.bn[:, j, 0, :], ALU.mult))
                    link(nc.vector.tensor_tensor(k.bn[:, j, 1, :], k.bn[:, j, 1, :], be_, ALU.add))



def group_norm(nc, k, x, out, mean_matrix, gamma, beta):
    with ExitStack() as c:
        stats = c.enter_context(sbuf(nc, "gn_stats", [P, NC2, 6], F32))
        s = c.enter_context(sbuf(nc, "gn_s", [P, 8], F32))
        ps = c.enter_context(psum(nc, "gn_ps", [P, BANK], F32))
        block, chained, ready, averaged, rooted = c.enter_context(stage(nc, "chained", "moments", "averaged", "rooted"))

        @block.vector
        def _(dve):
            link = linker(dve, chained)
            for i in range(NC2):
                link(nc.vector.bn_stats(stats[:, i, :], x[:, i * BANK:(i + 1) * BANK]))
            link(nc.vector.bn_aggr(s[:, 0:2], stats[:].rearrange("p a b -> p (a b)")))
            nc.vector.scalar_tensor_tensor(s[:, 1:2], s[:, 0:1], s[:, 0:1], s[:, 1:2], ALU.mult, ALU.add).then_inc(ready, 1)
            dve.wait_ge(averaged, 1)
            link(nc.vector.tensor_copy(s[:, 2:4], ps[:, 0:2]))
            link(nc.vector.tensor_tensor(s[:, 4:5], s[:, 2:3], s[:, 2:3], ALU.mult))
            nc.vector.tensor_tensor(s[:, 5:6], s[:, 3:4], s[:, 4:5], ALU.subtract).then_inc(ready, 1)
            dve.wait_ge(rooted, 1)
            link(nc.vector.reciprocal(s[:, 6:7], s[:, 6:7]))
            if gamma is not None:
                link(nc.vector.tensor_tensor(s[:, 6:7], s[:, 6:7], gamma, ALU.mult))
            link(nc.vector.tensor_tensor(s[:, 7:8], s[:, 2:3], s[:, 6:7], ALU.mult))
            if beta is not None:
                link(nc.vector.tensor_tensor(s[:, 7:8], beta, s[:, 7:8], ALU.subtract))
            else:
                link(nc.vector.tensor_scalar(s[:, 7:8], s[:, 7:8], -1.0, None, ALU.mult))
            in_ = x.rearrange("p (h w) -> p h w", w=IMG) if len(out.shape) == 3 else x
            link(nc.vector.tensor_scalar(out, in_, s[:, 6:7], s[:, 7:8], ALU.mult, ALU.add))

        @block.tensor
        def _(pe):
            pe.wait_ge(ready, 1)
            nc.tensor.matmul(ps[:, 0:2], mean_matrix[:], s[:, 0:2], start=True, stop=True).then_inc(averaged, 1)

        @block.scalar
        def _(act):
            act.wait_ge(ready, 2)
            nc.scalar.activation(s[:, 6:7], s[:, 5:6], ACT.Sqrt, bias=k.eps[:, 0:1]).then_inc(rooted, 1)


def layer_norm(nc, k, x, out, gamma=None, beta=None, ps=None, turned=None):
    with ExitStack() as c:
        stats = c.enter_context(sbuf(nc, "ln_stats", [P, NT, 6], F32))
        s = c.enter_context(sbuf(nc, "ln_s", [P, NT, 2], F32))
        block, chained, collected, ready, rooted, normed, half_ready, turned_ready, off = c.enter_context(stage(
            nc, "chained", "collected", "variance", "rooted", "normed", "half_ready", "turned_ready", "off"))
        HALF = NT // 2

        @block.vector
        def _(dve):
            link = linker(dve, chained)
            for t in range(NT):
                nc.vector.bn_stats(stats[:, t, :], x[:, t, :]).then_inc(collected, 1)
            for t in range(NT):
                dve.wait_ge(collected, t + 1)
                nc.vector.bn_aggr(s[:, t, :], stats[:, t, :]).then_inc(ready, 1)
            dve.wait_ge(rooted, 1)
            link(nc.vector.reciprocal(s[:, :, 1], s[:, :, 1]))
            for t in range(NT):
                nc.vector.tensor_scalar(out[:, t, :], x[:, t, :], s[:, t, 0:1], s[:, t, 1:2], ALU.subtract,
                                        ALU.mult).then_inc(normed, 1)
            if gamma is not None:
                for u in range(2):
                    dve.wait_ge(normed, HALF * (u + 1))
                    half = out[:, HALF * u:HALF * (u + 1)]
                    link(nc.vector.tensor_tensor(half, half, gamma.unsqueeze(1).broadcast_to([P, HALF, P]), ALU.mult))
                    nc.vector.tensor_tensor(half, half, beta.unsqueeze(1).broadcast_to([P, HALF, P]),
                                            ALU.add).then_inc(half_ready, 1)
            if turned is not None:
                dve.wait_ge(turned_ready, 2)
                nc.vector.tensor_copy(chunk(turned, 1), ps[:, 1]).then_inc(off, 1)

        @block.scalar
        def _(act):
            act.wait_ge(ready, NT)
            nc.scalar.activation(s[:, :, 1], s[:, :, 1], ACT.Sqrt, bias=k.eps[:, 0:1]).then_inc(rooted, 1)
            if turned is not None:
                act.wait_ge(turned_ready, 1)
                nc.scalar.copy(chunk(turned, 0), ps[:, 0]).then_inc(off, 1)

        if turned is not None:
            @block.tensor
            def _(pe):
                for u in range(2):
                    if gamma is not None:
                        pe.wait_ge(half_ready, u + 1)
                    for t in range(HALF):
                        if gamma is None:
                            pe.wait_ge(normed, HALF * u + t + 1)
                        last = nc.tensor.transpose(ps[:, u, t * P:(t + 1) * P], out[:, HALF * u + t, :], k.ident[:])
                    last.then_inc(turned_ready, 1)


STACKS = {16: [((0, 0, 0, 1, 1, 2), (0, 1, 2, 0, 1, 0))],
          32: [((0, 0, 1), (0, 1, 0)), ((0, 1, 2), (2, 1, 0))]}
STACK = 96
S_STEPS = (2, 2, 1, 1, 1, 1, 0, 0)


def split_and_values(nc, k, ps, hd, qk, parts, x, w_values):
    share = 32 // hd
    with stage(nc, "rounded", "rest_ready", "split", "values_ready", "off") as (
            block, rounded, rest_ready, split, values_ready, off):
        @block.tensor
        def _(pe):
            for i in range(2):
                for t in range(4):
                    last = nc.tensor.matmul(ps[:, i, t * P:(t + 1) * P], chunk(x, 4 * i + t, P), w_values, start=True,
                                            stop=True)
                last.then_inc(values_ready, 1)

        def values_off(on_act, i):
            for j in range(share):
                heads = k.v_ext[:, 4 * i:4 * i + 4].rearrange("p t (g j) d -> p t g j d", j=share)[
                    :, :, :, j, j * hd:(j + 1) * hd]
                affine(nc, on_act, heads, ps[:, i].rearrange("p (t g j d) -> p t g j d", t=4, j=share, d=hd)[
                    :, :, :, j]).then_inc(off, 1)

        @block.scalar
        def _(act):
            for part in range(2):
                for j in range(2):
                    if part == 1:
                        act.wait_ge(rest_ready, j + 1)
                    nc.scalar.copy(parts[:, j, part], qk[:, j]).then_inc(rounded, 1)
            act.wait_ge(values_ready, 1)
            values_off(True, 0)

        @block.vector
        def _(dve):
            for j in range(2):
                dve.wait_ge(rounded, j + 1)
                nc.vector.tensor_tensor(qk[:, j], qk[:, j], parts[:, j, 0], ALU.subtract).then_inc(rest_ready, 1)
            for j in range(2):
                dve.wait_ge(rounded, 2 + j + 1)
                nc.vector.tensor_tensor(parts[:, j, 2], qk[:, j], parts[:, j, 1], ALU.subtract).then_inc(split, 1)
            dve.wait_ge(values_ready, 2)
            values_off(False, 1)

        @block.sync
        def _(sp):
            for j in range(2):
                sp.wait_ge(split, j + 1)
                sp.dma_start(k.parts_dram[j].rearrange("s p n -> p s n"), parts[:, j]).then_inc(k.parted, 16)


def start_stacks(queue, k, hd, j):
    queue.wait_ge(k.parted, 32)
    for slot, blocks in enumerate(STACKS[hd]):
        for r, part in enumerate(blocks[j]):
            slots = k.stacks[r * hd:(r + 1) * hd, j].rearrange(
                "p (h s) n -> p h s n", s=len(STACKS[hd]))[:, 0:P // hd, slot, :]
            source = k.parts_dram[j, part].rearrange("(h r) n -> r h n", r=hd)
            queue.dma_start(slots, source).then_inc(k.stacked[j], 16)


def load_stacks(nc, k, hd):
    with stage(nc) as (block,):
        @block.sync
        def _(sp):
            start_stacks(sp, k, hd, 0)

        @block.scalar
        def _(act):
            start_stacks(act, k, hd, 1)


def dense_attention(nc, k, hd, o_cm, bias, w_out, finish):
    heads = P // hd
    per = len(STACKS[hd])
    share = 32 // hd
    groups = heads // share
    items, at_step = [], {}

    def schedule(step, new):
        at_step[step] = list(range(len(items), len(items) + len(new)))
        items.extend(new)

    def tiles(h, lo, hi):
        return [("s", h, t, n) for t in range(lo, hi) for n in range(NC2)]

    rows_of = {}
    schedule("first", tiles(0, 0, NT))
    rows_of[0] = list(range(len(items), len(items) + NC2))
    items += [("r", 0, n) for n in range(NC2)]
    for h in range(heads):
        lo = 0
        for m in range(NT):
            hi = lo + S_STEPS[m]
            schedule((h, m), tiles(h + 1, lo, hi) if h + 1 < heads else [])
            lo = hi
            if m == NT - 1 and h + 1 < heads:
                rows_of[h + 1] = list(range(len(items), len(items) + NC2))
                items += [("r", h + 1, n) for n in range(NC2)]
    order = {"s": {}, "r": {}}
    for i, item in enumerate(items):
        order[item[0]][i] = len(order[item[0]])
    RING = 2
    with ExitStack() as c:
        ring = c.enter_context(psum(nc, "att_ring", [P, RING, BANK], F32))
        ST = c.enter_context(psum(nc, "att_ST", [P, 2, N], F32))
        O = c.enter_context(psum(nc, "att_O", [64, NC2, BANK], F32))
        probs = c.enter_context(sbuf(nc, "att_probs", [P, 3, N], F32))
        half_max = c.enter_context(sbuf(nc, "att_half_max", [P, 2, NT, NC2], F32))
        shift = c.enter_context(sbuf(nc, "att_shift", [P, 2, NT], F32))
        shift_parts = c.enter_context(sbuf(nc, "att_shift_parts", [P, 2, NT, 3], BF16))
        den = c.enter_context(sbuf(nc, "att_den", [P, N], F32))
        (block, ring_ready, reduced, rows_off, chained, parts_ready, st_ready, probs_ready, mixed_ready,
         off_by_act, off_by_dve, normed, biased, projected, finished) = c.enter_context(stage(nc, "ring_ready", "reduced", "rows_off", "chained", "parts_ready", "st_ready",
                                         "probs_ready", "mixed_ready", "off_by_act", "off_by_dve", "normed",
                                         "biased", "projected", "finished"))

        def rows_of_group(x, g):
            return x[32 * g:32 * g + 32, :].rearrange("p (n m) -> p n m", m=BANK)

        @block.tensor
        def _(pe):
            def bank_free(i):
                if i >= RING:
                    kind = items[i - RING][0]
                    pe.wait_ge(reduced if kind == "s" else rows_off, order[kind][i - RING] + 1)

            def scores(i):
                _, h, t, n = items[i]
                bank_free(i)
                nc.tensor.matmul(ring[:, i % RING], k.stacks[0:STACK, 0, per * h, t * P:(t + 1) * P],
                                 k.stacks[0:STACK, 1, per * h, n * BANK:(n + 1) * BANK], start=True,
                                 stop=True).then_inc(ring_ready, 1)

            def shift_rows(h):
                pe.wait_ge(parts_ready, h + 1)
                for i in rows_of[h]:
                    n = items[i][2]
                    bank_free(i)
                    for t in range(4):
                        last = nc.tensor.matmul(ring[STACK:STACK + 3, i % RING, t * P:(t + 1) * P],
                                                shift_parts[:, h % 2, 4 * n + t, :], k.ident_b[:], start=True,
                                                stop=True, tile_position=(0, STACK))
                    last.then_inc(ring_ready, 1)

            def scores_transposed(h, m):
                s = h * NT + m
                if m == 0:
                    pe.wait_ge(rows_off, NC2 * (h + 1))
                if s >= 2:
                    pe.wait_ge(probs_ready, s - 1)
                for n in range(NC2):
                    for j in range(per):
                        rows = STACK + 3 if j == per - 1 else STACK
                        last = nc.tensor.matmul(ST[:, s % 2, n * BANK:(n + 1) * BANK],
                                                k.stacks[0:rows, 1, per * h + j, m * P:(m + 1) * P],
                                                k.stacks[0:rows, 0, per * h + j, n * BANK:(n + 1) * BANK],
                                                start=(j == 0), stop=(j == per - 1))
                last.then_inc(st_ready, 1)

            def mix(h, m):
                s = h * NT + m
                pe.wait_ge(probs_ready, s + 1)
                g, first, last_step = h // share, h % share == 0 and m == 0, h % share == share - 1 and m == NT - 1
                if first and g >= 1:
                    pe.wait_ge(off_by_act, g)
                    pe.wait_ge(off_by_dve, g)
                for n in range(NC2):
                    last = nc.tensor.matmul(O[:, n], k.v_ext[:, m, h, :], probs[:, s % 3, n * BANK:(n + 1) * BANK],
                                            start=first, stop=last_step)
                last.then_inc(mixed_ready, 1)

            for loaded in k.stacked:
                pe.wait_ge(loaded, 16 * 6)
            for i in at_step["first"]:
                scores(i)
            shift_rows(0)
            for h in range(heads):
                for m in range(NT):
                    for i in at_step[(h, m)]:
                        scores(i)
                    if m == NT - 1 and h + 1 < heads:
                        shift_rows(h + 1)
                    scores_transposed(h, m)
                    if h * NT + m >= 1:
                        mix(*divmod(h * NT + m - 1, NT))
            mix(heads - 1, NT - 1)
            for n in range(NC2):
                pe.wait_ge(biased, n + 1)
                nc.tensor.matmul(ring[:, n], w_out, chunk(o_cm, n), start=True, stop=True).then_inc(projected, 1)

        @block.scalar
        def _(act):
            def rows(h):
                for i in rows_of[h]:
                    n = items[i][2]
                    act.wait_ge(ring_ready, i + 1)
                    nc.scalar.copy(k.stacks[STACK:STACK + 3, 0, per * h + per - 1, n * BANK:(n + 1) * BANK],
                                   ring[STACK:STACK + 3, i % RING, :]).then_inc(rows_off, 1)

            def carry_off(g):
                act.wait_ge(mixed_ready, NT * share * (g + 1))
                nc.scalar.copy(rows_of_group(o_cm, g), O[0:32]).then_inc(off_by_act, 1)

            rows(0)
            for h in range(heads):
                for m in range(NT):
                    s = h * NT + m
                    if m == NT - 1 and h + 1 < heads:
                        rows(h + 1)
                    act.wait_ge(st_ready, s + 1)
                    if s >= 3:
                        act.wait_ge(mixed_ready, s - 2)
                    nc.scalar.activation(probs[:, s % 3, :], ST[:, s % 2, :], ACT.Exp).then_inc(probs_ready, 1)
                    if m == 0 and h % share == 0 and h > 0:
                        carry_off(h // share - 1)
            carry_off(groups - 1)
            for n in range(NC2):
                act.wait_ge(normed, n + 1)
                affine(nc, True, chunk(o_cm, n), chunk(o_cm, n), 1.0, bias).then_inc(biased, 1)

        @block.vector
        def _(dve):
            link = linker(dve, chained)

            def maxima(indices):
                for i in indices:
                    _, h, t, n = items[i]
                    dve.wait_ge(ring_ready, i + 1)
                    nc.vector.tensor_reduce(half_max[:, h % 2, t, n:n + 1], ring[:, i % RING], AX.X, ALU.max,
                                            negate=True).then_inc(reduced, 1)
                    if t == NT - 1 and n == NC2 - 1:
                        parts(h)

            def parts(h):
                a, p_ = shift[:, h % 2], shift_parts[:, h % 2]
                dve.wait_ge(reduced, NC2 * NT * (h + 1))
                link(nc.vector.tensor_tensor(a, half_max[:, h % 2, :, 0], half_max[:, h % 2, :, 1], ALU.min))
                link(nc.vector.tensor_copy(p_[:, :, 0], a))
                link(nc.vector.tensor_tensor(a, a, p_[:, :, 0], ALU.subtract))
                link(nc.vector.tensor_copy(p_[:, :, 1], a))
                nc.vector.tensor_tensor(p_[:, :, 2], a, p_[:, :, 1], ALU.subtract).then_inc(parts_ready, 1)

            def carry_off(g):
                dve.wait_ge(mixed_ready, NT * share * (g + 1))
                nc.vector.tensor_copy(rows_of_group(den, g), O[32:64]).then_inc(off_by_dve, 1)

            maxima(at_step["first"])
            for h in range(heads):
                for m in range(NT):
                    maxima(at_step[(h, m)])
                    if m == 0 and h % share == 0 and h > 0:
                        carry_off(h // share - 1)
            carry_off(groups - 1)
            dve.wait_ge(off_by_dve, groups)
            for n in range(NC2):
                link(nc.vector.reciprocal(chunk(den, n), chunk(den, n)))
                if n == 0:
                    dve.wait_ge(off_by_act, groups)
                nc.vector.tensor_tensor(chunk(o_cm, n), chunk(o_cm, n), chunk(den, n), ALU.mult).then_inc(normed, 1)
            for n in range(NC2):
                dve.wait_ge(projected, n + 1)
                finish(n, ring[:, n]).then_inc(finished, 1)
    for sem in (k.parted, *k.stacked):
        nc.gpsimd.sem_clear(sem)
    nc.all_engine_barrier(sem_only=True)


SPREAD = 5


def local_attention(nc, k, K, H, q, shifted_k, shifted_v, place, spread, w_out, out, mask=None, mirrored=False,
                    next_stacks=None):
    KH = K * H
    first = K // 2 if mirrored else 0
    order = list(range(first, K)) + list(range(first - 1, -1, -1))
    n_a = K - first
    rows_a, rows_b = n_a * H, first * H
    groups = K // SPREAD
    GR = SPREAD * H
    HALF = NT // 2
    SLOTS_OF_PROD = 3 if mirrored else 2
    with ExitStack() as c:
        parts = c.enter_context(sbuf(nc, "loc_parts", [P, NT, groups, 3 * GR], BF16))
        att_t = c.enter_context(sbuf(nc, "loc_att_t", [3 * GR, groups, N], BF16))

        with ExitStack() as c2:
            att = c2.enter_context(sbuf(nc, "loc_att", [P, NT, KH], F32))
            small = c2.enter_context(sbuf(nc, "loc_small", [P, 2, NT, H], F32))
            prod = c2.enter_context(sbuf(nc, "loc_prod", [P, SLOTS_OF_PROD, N], F32))
            in_rows = c2.enter_context(sbuf(nc, "loc_rows", [rows_a, N], F32))
            if mirrored:
                R = IMG + 4
                padded = c2.enter_context(sbuf(nc, "loc_padded", [rows_a, R, R], F32))
                moved = c2.enter_context(sbuf(nc, "loc_moved", [rows_b, IMG, R], F32))
                in_rows_b = c2.enter_context(sbuf(nc, "loc_rows_b", [rows_b, N], F32))
            ps = c2.enter_context(psum(nc, "loc_ps", [P, NC2, BANK], F32))
            turned = c2.enter_context(psum(nc, "loc_turned", [P, NT // 2, 2, BANK // 2], F32))
            (block, product_ready, scored, rows_ready, zeroed, pad_ready, moved_ready, rows_b_ready, turned_ready,
             chained, shifted, exped, weighed, rest_ready, rounded, split) = c2.enter_context(stage(
                nc, "product_ready", "scored", "rows_ready", "zeroed", "pad_ready", "moved_ready", "rows_b_ready",
                "turned_ready", "chained", "shifted", "exped", "weighed", "rest_ready", "rounded", "split"))

            def half(x, u):
                return x[:, HALF * u:HALF * (u + 1)]

            def grouped(u):
                return half(att, u).rearrange("p t (g r) -> p (t g) r", r=GR)

            def part(i, u):
                return half(parts, u)[:, :, :, i * GR:(i + 1) * GR].rearrange("p t g r -> p (t g) r")

            @block.tensor
            def _(pe):
                for j in range(n_a):
                    pe.wait_ge(product_ready, NC2 * (j + 1))
                    for n in range(NC2):
                        last = nc.tensor.matmul(ps[0:rows_a, n], place[:, (n_a - 1 - j) * H:(n_a - 1 - j) * H + rows_a],
                                                prod[:, j % SLOTS_OF_PROD, n * BANK:(n + 1) * BANK], start=(j == 0),
                                                stop=(j == n_a - 1))
                    last.then_inc(scored, 1)
                pe.wait_ge(rows_ready, NC2)
                for t in range(NT):
                    last = nc.tensor.transpose(turned[:, t // 2, t % 2, 0:rows_a], in_rows[:, t * P:(t + 1) * P],
                                               k.ident[0:rows_a, 0:rows_a])
                    if not mirrored:
                        last.then_inc(turned_ready, 1)
                if mirrored:
                    for t in range(NT):
                        if t % HALF == 0:
                            pe.wait_ge(rows_b_ready, t // HALF + 1)
                        nc.tensor.transpose(turned[:, t // 2, t % 2, rows_a:KH], in_rows_b[:, t * P:(t + 1) * P],
                                            k.ident[0:rows_b, 0:rows_b]).then_inc(turned_ready, 1)

            if mirrored:
                @block.gpsimd
                def _(pool):
                    nc.gpsimd.memset(padded[:], 0.0).then_inc(zeroed, 1)

                @block.sync
                def _(sp):
                    flat = padded[:].rearrange("p a b -> p (a b)")
                    flat_moved = moved[:].rearrange("p a b -> p (a b)")
                    size = IMG * R - 4
                    sp.wait_ge(pad_ready, NC2)
                    for j in range(1, n_a):
                        dy, dx = divmod(order[j], 5)
                        start = (4 - dy) * R + 4 - dx
                        sp.dma_start(flat_moved[(j - 1) * H:j * H, 0:size],
                                     flat[j * H:(j + 1) * H, start:start + size]).then_inc(moved_ready, 16)

            @block.vector
            def _(dve):
                for j in range(n_a):
                    if j >= SLOTS_OF_PROD:
                        dve.wait_ge(scored, j - SLOTS_OF_PROD + 1)
                    for n in range(NC2):
                        a, b_ = q(n), shifted_k(order[j], n)
                        o_ = prod[:, j % SLOTS_OF_PROD, n * BANK:(n + 1) * BANK]
                        if len(a.shape) == 3:
                            o_ = o_.rearrange("p (h w) -> p h w", w=IMG)
                        nc.vector.tensor_tensor(o_, a, b_, ALU.mult).then_inc(product_ready, 1)
                if mirrored:
                    dve.wait_ge(zeroed, 1)
                    dve.wait_ge(scored, n_a)
                    lines = IMG // NC2
                    for n in range(NC2):
                        nc.vector.tensor_copy(padded[:, 2 + n * lines:2 + (n + 1) * lines, 2:2 + IMG],
                                              ps[0:rows_a, n].rearrange("p (a b) -> p a b", b=IMG)).then_inc(pad_ready, 1)
                link = linker(dve, chained)

                def heads_last(x):
                    return x.rearrange("p t (s h) -> p t s h", h=H)

                def shifts_last(x):
                    return x.rearrange("p t (s h) -> p t h s", h=H)

                def over_shifts(x):
                    return x.unsqueeze(2).broadcast_to([P, HALF, K, H])

                for u in range(2):
                    dve.wait_ge(turned_ready, HALF * (u + 1))
                    scores = turned[:, u * NT // 4:(u + 1) * NT // 4].rearrange("p b j f -> p (b j) f")[:, :, 0:KH]
                    if mask is not None:
                        link(nc.vector.tensor_tensor(heads_last(half(att, u)), heads_last(scores), half(
                            mask, u).unsqueeze(3).broadcast_to([P, HALF, K, H]), ALU.add))
                        scores = half(att, u)
                    link(nc.vector.tensor_reduce(half(small[:, 0], u), shifts_last(scores), AX.X, ALU.max))
                    nc.vector.tensor_tensor(heads_last(half(att, u)), heads_last(scores), over_shifts(
                        half(small[:, 0], u)), ALU.subtract).then_inc(shifted, 1)
                for u in range(2):
                    dve.wait_ge(exped, u + 1)
                    total = half(small[:, 1], u)
                    link(nc.vector.tensor_reduce(total, shifts_last(half(att, u)), AX.X, ALU.add))
                    link(nc.vector.reciprocal(total, total))
                    nc.vector.tensor_tensor(heads_last(half(att, u)), heads_last(half(att, u)), over_shifts(total),
                                            ALU.mult).then_inc(weighed, 1)
                for u in range(2):
                    dve.wait_ge(rounded, u + 1)
                    nc.vector.tensor_tensor(grouped(u), grouped(u), part(0, u), ALU.subtract).then_inc(rest_ready, 1)
                for u in range(2):
                    dve.wait_ge(rounded, 2 + u + 1)
                    nc.vector.tensor_tensor(part(2, u), grouped(u), part(1, u), ALU.subtract).then_inc(split, 1)

            @block.scalar
            def _(act):
                act.wait_ge(scored, n_a)
                lines = IMG // NC2
                for n in range(NC2):
                    o_ = in_rows[:, n * BANK:(n + 1) * BANK]
                    if mirrored:
                        act.wait_ge(pad_ready, n + 1)
                        nc.scalar.copy(o_.rearrange("p (a b) -> p a b", b=IMG),
                                       padded[:, 2 + n * lines:2 + (n + 1) * lines, 2:2 + IMG]).then_inc(rows_ready, 1)
                    else:
                        nc.scalar.copy(o_, ps[0:rows_a, n]).then_inc(rows_ready, 1)
                if mirrored:
                    act.wait_ge(moved_ready, 16 * (n_a - 1))
                    for n in range(NC2):
                        nc.scalar.copy(in_rows_b[:, n * BANK:(n + 1) * BANK].rearrange("p (a b) -> p a b", b=IMG),
                                       moved[:, n * lines:(n + 1) * lines, 0:IMG]).then_inc(rows_b_ready, 1)
                for u in range(2):
                    act.wait_ge(shifted, u + 1)
                    nc.scalar.activation(half(att, u), half(att, u), ACT.Exp).then_inc(exped, 1)
                for u in range(2):
                    act.wait_ge(weighed, u + 1)
                    nc.scalar.copy(part(0, u), grouped(u)).then_inc(rounded, 1)
                for u in range(2):
                    act.wait_ge(rest_ready, u + 1)
                    nc.scalar.copy(part(1, u), grouped(u)).then_inc(rounded, 1)

        with psum(nc, "loc_ps", [P, 8, 2 * BANK], BF16) as ps:
            turn_tiles(nc, ps, k.ident_b, [([parts[:, t, g] for t in range(NT)],
                                            att_t[:, g].rearrange("p (k n) -> p k n", n=P)) for g in range(groups)])

        with ExitStack() as c2:
            wide = c2.enter_context(psum(nc, "loc_wide", [P, 4, BANK], F32))
            acc = c2.enter_context(psum(nc, "loc_acc", [P, NC2, BANK], F32))
            RING = 8 if mirrored else 4
            LAG = 3
            weighed = c2.enter_context(sbuf(nc, "loc_weighed", [P, RING, BANK], F32))
            partial = c2.enter_context(sbuf(nc, "loc_partial", [P, NC2, BANK], F32))
            block, spread_ready, weighed_ready, summed, added, off = c2.enter_context(
                stage(nc, "spread_ready", "weighed_ready", "summed", "added", "off"))
            steps = [(j, n) for j in range(K) for n in range(NC2)]
            by_pool = [i for i, (j, n) in enumerate(steps) if j % 2 == 1]
            by_pe = [i for i, (j, n) in enumerate(steps) if j % 2 == 0]

            @block.tensor
            def _(pe):
                for i in range(len(steps) + LAG):
                    if i < len(steps):
                        j, n = steps[i]
                        if i >= 4:
                            pe.wait_ge(weighed_ready, i - 3)
                        g, column = divmod(j, SPREAD)
                        nc.tensor.matmul(wide[:, i % 4], spread[:, column * P:(column + 1) * P],
                                         att_t[:, g, n * BANK:(n + 1) * BANK], start=True,
                                         stop=True).then_inc(spread_ready, 1)
                    if i - LAG in by_pe:
                        j, n = steps[i - LAG]
                        pe.wait_ge(weighed_ready, i - LAG + 1)
                        nc.tensor.matmul(acc[:, n], w_out, weighed[:, (i - LAG) % RING], start=(j == 0),
                                         stop=False).then_inc(summed, 1)
                pe.wait_ge(added, len(by_pool))
                for n in range(NC2):
                    nc.tensor.matmul(acc[:, n], w_out, partial[:, n], start=False, stop=True).then_inc(summed, 1)

            if next_stacks is not None:
                @block.sync
                def _(sp):
                    start_stacks(sp, k, next_stacks, 0)

                @block.scalar
                def _(act):
                    start_stacks(act, k, next_stacks, 1)

            @block.gpsimd
            def _(pool):
                for count, i in enumerate(by_pool):
                    j, n = steps[i]
                    pool.wait_ge(weighed_ready, i + 1)
                    if count >= NC2:
                        pool.wait_ge(added, count - NC2 + 1)
                        nc.gpsimd.tensor_tensor(partial[:, n], partial[:, n], weighed[:, i % RING],
                                                ALU.add).then_inc(added, 1)
                    else:
                        nc.gpsimd.tensor_copy(partial[:, n], weighed[:, i % RING]).then_inc(added, 1)

            @block.vector
            def _(dve):
                for i, (j, n) in enumerate(steps):
                    dve.wait_ge(spread_ready, i + 1)
                    if i >= RING:
                        if i - RING in by_pool:
                            dve.wait_ge(added, by_pool.index(i - RING) + 1)
                        else:
                            dve.wait_ge(summed, by_pe.index(i - RING) + 1)
                    v = shifted_v(order[j], n)
                    a, o_ = wide[:, i % 4], weighed[:, i % RING]
                    if len(v.shape) == 3:
                        a, o_ = (y.rearrange("p (h w) -> p h w", w=IMG) for y in (a, o_))
                    nc.vector.tensor_tensor(o_, a, v, ALU.mult).then_inc(weighed_ready, 1)
                for n in range(NC2):
                    dve.wait_ge(summed, len(by_pe) + n + 1)
                    out(n, acc[:, n]).then_inc(off, 1)


def chunk(a, n, size=BANK):
    return a[:, n * size:(n + 1) * size]


def turn_image(nc, k, ps, x, out, combine=None):
    pairs = [([x[:, t, :] if len(x.shape) == 3 else chunk(x, t, P) for t in range(u, u + 4)],
              out[:, u:u + 4, :] if len(out.shape) == 3 else
              chunk(out, u // 4).rearrange("p (k n) -> p k n", n=P)) for u in range(0, NT, 4)]
    turn_tiles(nc, ps, k.ident, pairs, combine)


def copy_blocks(nc, pairs):
    with stage(nc, "by_act", "by_dve") as (block, by_act, by_dve):
        @block.scalar
        def _(act):
            for out, in_ in pairs[1::2]:
                nc.scalar.copy(out, in_).then_inc(by_act, 1)

        @block.vector
        def _(dve):
            for out, in_ in pairs[0::2]:
                nc.vector.tensor_copy(out, in_).then_inc(by_dve, 1)


def dense_operands(nc, k, ps, hd, x, qk, parts, weights, scale_bias):
    product_pass(nc, ps, 4, lambda i, bank: nc.tensor.matmul(bank, weights[i // 2], chunk(x, i % 2), start=True,
                                                             stop=True),
                 lambda on_act, i, bank: affine(nc, on_act, chunk(qk[:, i // 2], i % 2), bank, *scale_bias[i // 2]))
    split_and_values(nc, k, ps, hd, qk, parts, x, weights[2])


@contextmanager
def dense_buffers(nc, k, hd):
    heads, share = P // hd, 32 // hd
    with ExitStack() as c:
        k.stacks = c.enter_context(sbuf(nc, "stacks", [P, 2, 8, N], BF16))
        k.v_ext = c.enter_context(sbuf(nc, "v_ext", [P, NT, heads, 64], F32))
        with stage(nc, "made", "zeroed") as (block, made, zeroed):
            @block.gpsimd
            def _(pool):
                nc.gpsimd.memset(k.stacks[STACK:STACK + 3, 1, 0:3], 1.0).then_inc(made, 1)

            @block.vector
            def _(dve):
                nc.vector.memset(k.stacks[STACK:STACK + 3, 1, 3:8], 1.0).then_inc(made, 1)
                nc.vector.memset(k.v_ext[:], 0.0).then_inc(zeroed, 1)
                dve.wait_ge(zeroed, 1)
                for j in range(share):
                    nc.vector.memset(k.v_ext[:].rearrange("p t (g j) d -> p (t g) j d", j=share)[
                        :, :, j, 32 + j * hd:32 + (j + 1) * hd], 1.0).then_inc(made, 1)
        yield



@contextmanager
def cleared_buffer(nc, name, shape):
    with sbuf(nc, name, shape, F32) as buffer:
        with stage(nc, "cleared") as (block, cleared):
            @block.vector
            def _(dve):
                nc.vector.memset(buffer[:], 0.0).then_inc(cleared, 1)
        yield buffer


LAST_IMAGE = B - 1


def first_layers(nc, k):
    with ExitStack() as c:
        x = c.enter_context(sbuf(nc, "l0_x", [P, N], F32))
        parts = c.enter_context(sbuf(nc, "l0_parts", [P, 2, 3, N], BF16))
        pad = c.enter_context(cleared_buffer(nc, "l1_pad", [P, IMG + 4, IMG + 4]))
        c.enter_context(dense_buffers(nc, k, 32))
        start_attention(nc, k, 0, parts)
        load_stacks(nc, k, 32)
        with loop(nc, 0, B - 1) as b:
            finish_attention(nc, k, b, x)
            start_attention(nc, k, b + 1, parts)
            local_attention_of_image(nc, k, b, x, pad)
        finish_attention(nc, k, LAST_IMAGE, x)
        local_attention_of_image(nc, k, LAST_IMAGE, x, pad)


def start_attention(nc, k, b, parts):
    with ExitStack() as c:
        h = c.enter_context(sbuf(nc, "l0_h", [P, N], F32))
        qk = c.enter_context(sbuf(nc, "l0_qk", [P, 2, N], F32))
        ps = c.enter_context(psum(nc, "l0_ps", [P, 7, BANK], F32))
        group_norm(nc, k, k.x_cm[:, b, :], h[:], k.mean16, k.cols[:, C_GN_G:C_GN_G + 1], k.cols[:, C_GN_B:C_GN_B + 1])
        dense_operands(nc, k, ps, 32, h, qk, parts, [k.turned[:, i, :] for i in range(3)],
                       [(32 ** -0.5, k.qb[:, 0:1]), (1.0, k.cols[:, C_QKV_B + 1:C_QKV_B + 2])])


def finish_attention(nc, k, b, x):
    with ExitStack() as c:
        o_cm = c.enter_context(sbuf(nc, "l0_o", [P, N], F32))
        dense_attention(nc, k, 32, o_cm, k.cols[:, C_QKV_B + 2:C_QKV_B + 3], k.turned[:, 3, :],
                        lambda n, bank: nc.vector.scalar_tensor_tensor(
                            chunk(x, n), bank, k.cols[:, C_PROJ_B:C_PROJ_B + 1],
                            k.x_cm[:, b, n * BANK:(n + 1) * BANK], ALU.add, ALU.add))


def local_attention_of_image(nc, k, b, x, pad):
    with ExitStack() as c:
        def sb(name, shape):
            return c.enter_context(sbuf(nc, name, shape, F32))

        group_norm(nc, k, x[:], pad[:, 2:2 + IMG, 2:2 + IMG], k.mean4, None, None)
        rows = BANK // IMG

        def window(s, n):
            i, j = divmod(s, 5)
            return pad[:, n * rows + i:n * rows + i + rows, j:j + IMG]

        def out(n, acc):
            return nc.vector.scalar_tensor_tensor(chunk(x, n), acc, k.cols[:, C_L1_B:C_L1_B + 1], chunk(x, n),
                                                  ALU.add, ALU.add)

        local_attention(nc, k, 25, 8, lambda n: window(12, n), window, window, k.place16, k.spread16,
                        k.turned[:, 4, :], out, mirrored=True,
                        next_stacks=None if b is LAST_IMAGE else 32)
        with ExitStack() as c2:
            ps = c2.enter_context(psum(nc, "l1_ps", [P, 8, BANK], F32))
            turn_image(nc, k, ps, x, k.t_tm[:, b])


def linear_attention(nc, k, b):
    with ExitStack() as c:
        def sb(name, shape):
            return c.enter_context(sbuf(nc, name, shape, F32))

        G = 16
        t_tm, xn, xc = k.t_tm[:, b], sb("l2_xn", [P, NT, P]), sb("l2_xc", [P, N])
        kv, sq = sb("l2_kv", [P, NT, 4 * P]), sb("l2_sq", [P, NT, 4 * P])
        st = sb("l2_st", [P, NT, G])
        dots, mo, g = sb("l2_dots", [P, 2, P]), sb("l2_mo", [P, 2, P]), sb("l2_g", [P, P])
        ps = c.enter_context(psum(nc, "l2_ps", [P, 8, BANK], F32))
        layer_norm(nc, k, t_tm, xn[:], ps=ps, turned=xc)
        with stage(nc, "kv_ready", "copied", "squared", "chained", "rooted", "normed", "dots_ready", "masked") as (
                block, kv_ready, copied, squared, chained, rooted, normed, dots_ready, masked):
            def heads(x, t):
                return x[:, t].rearrange("p (g d) -> p g d", d=32)

            @block.tensor
            def _(pe):
                for t in range(NT):
                    nc.tensor.matmul(ps[:, t], chunk(xc, t, P), k.w_kv[:], start=True, stop=True).then_inc(kv_ready, 1)
                pe.wait_ge(squared, NT)
                for t in range(NT):
                    pe.wait_ge(normed, t + 1)
                    for i in range(2):
                        last = nc.tensor.matmul(ps[:, i, 0:P], kv[:, t, (2 + i) * P:(3 + i) * P],
                                                kv[:, t, i * P:(i + 1) * P], start=(t == 0), stop=(t == NT - 1))
                last.then_inc(dots_ready, 1)

            @block.scalar
            def _(act):
                for t in range(NT):
                    act.wait_ge(kv_ready, t + 1)
                    nc.scalar.copy(kv[:, t], ps[:, t]).then_inc(copied, 1)
                    nc.scalar.activation(sq[:, t], ps[:, t], ACT.Square).then_inc(squared, 1)
                act.wait_ge(chained, NT)
                nc.scalar.activation(st[:], st[:], ACT.Sqrt, bias=k.eps[:, 0:1], scale=1.0 / 32).then_inc(rooted, 1)

            @block.vector
            def _(dve):
                for t in range(NT):
                    dve.wait_ge(squared, t + 1)
                    nc.vector.tensor_reduce(st[:, t], heads(sq, t), AX.X, ALU.add).then_inc(chained, 1)
                dve.wait_ge(rooted, 1)
                nc.vector.reciprocal(st[:], st[:]).then_inc(chained, 1)
                dve.wait_ge(chained, NT + 1)
                dve.wait_ge(copied, NT)
                for t in range(NT):
                    nc.vector.tensor_tensor(heads(kv, t), heads(kv, t), st[:, t].unsqueeze(2).broadcast_to([P, G, 32]),
                                            ALU.mult).then_inc(normed, 1)
                dve.wait_ge(dots_ready, 1)
                for i in range(2):
                    nc.vector.tensor_tensor(dots[:, i], ps[:, i, 0:P], k.block32[:], ALU.mult).then_inc(masked, 1)

        product_pass(nc, ps, 2, lambda i, bank: nc.tensor.matmul(bank[:, 0:P], dots[:, i], k.w_o2[:, i], start=True,
                                                                 stop=True),
                     lambda on_act, i, bank: affine(nc, on_act, mo[:, i], bank[:, 0:P]))

        def g_product(i, bank):
            for j in range(2):
                last = nc.tensor.matmul(bank[:, 0:P], k.turned[:, k.t_q2 + j, :], mo[:, j], start=(j == 0), stop=(j == 1))
            return last

        product_pass(nc, ps, 1, g_product, lambda on_act, i, bank: affine(nc, on_act, g[:], bank[:, 0:P]))

        def out_product(i, bank):
            for t in range(4):
                o_ = bank[:, t * P:(t + 1) * P]
                nc.tensor.matmul(o_, chunk(xc, 4 * i + t, P), g[:], start=True, stop=False)
                last = nc.tensor.matmul(o_, k.ones_row[:], k.rows[0:1, 0, :], start=False, stop=True)
            return last

        product_pass(nc, ps, 2, out_product, lambda on_act, i, bank: nc.vector.tensor_tensor(
            t_tm[:, 4 * i:4 * i + 4].rearrange("p t n -> p (t n)"), bank,
            t_tm[:, 4 * i:4 * i + 4].rearrange("p t n -> p (t n)"), ALU.add), by="d")
        layer_norm(nc, k, t_tm, xn[:], ps=ps, turned=k.xn_cm[:, b])


def mixture_weights(nc, k):
    with ExitStack() as c:
        feat = c.enter_context(sbuf(nc, "mw_feat", [P, N], F32))
        s = c.enter_context(sbuf(nc, "mw_s", [P, 2, NT], F32))
        ps = c.enter_context(psum(nc, "mw_ps", [P, 8, BANK], F32))
        with stage(nc, "chained") as (block, chained):
            @block.vector
            def _(dve):
                link = linker(dve, chained)
                link(nc.vector.tensor_tensor(feat[:], k.xn_cm[:, 0], k.xn_cm[:, 1], ALU.add))
                for b in range(2, B):
                    link(nc.vector.tensor_tensor(feat[:], feat[:], k.xn_cm[:, b], ALU.add))
                link(nc.vector.tensor_scalar(feat[:], feat[:], 1.0 / B, None, ALU.mult))

        def product(i, bank):
            for t in range(NT):
                o_ = bank[:, t * E1:(t + 1) * E1]
                nc.tensor.matmul(o_, chunk(feat, t, P), k.wr[:], start=True, stop=False)
                last = nc.tensor.matmul(o_, k.ones_row[:], k.rows[0:1, 1, 0:E1], start=False, stop=True)
            return last

        product_pass(nc, ps, 1, product, lambda on_act, i, bank: affine(
            nc, on_act, k.mix[:].rearrange("p t e -> p (t e)"), bank[:, 0:NT * E1]))
        with stage(nc, "chained", "exped") as (block, chained, exped):
            @block.vector
            def _(dve):
                link = linker(dve, chained)
                link(nc.vector.tensor_reduce(s[:, 0], k.mix[:], AX.X, ALU.max))
                link(nc.vector.tensor_tensor(k.mix[:], k.mix[:], s[:, 0].unsqueeze(2).broadcast_to([P, NT, E1]),
                                             ALU.subtract))
                dve.wait_ge(exped, 1)
                link(nc.vector.tensor_reduce(s[:, 1], k.mix[:], AX.X, ALU.add))
                link(nc.vector.reciprocal(s[:, 1], s[:, 1]))
                link(nc.vector.tensor_tensor(k.mix[:], k.mix[:], s[:, 1].unsqueeze(2).broadcast_to([P, NT, E1]),
                                             ALU.mult))

            @block.scalar
            def _(act):
                act.wait_ge(chained, 2)
                nc.scalar.activation(k.mix[:], k.mix[:], ACT.Exp).then_inc(exped, 1)

        turn_tiles(nc, ps, k.ident, [([k.mix[:, t] for t in range(u, u + 4)],
                                      k.mix_t[:, u * P:(u + 4) * P].rearrange("p (k n) -> p k n", n=P)) for u in (0, 4)])


def mixture(nc, k, xc, t_tm, weight, weight_t, experts, bias, hidden, out_parts, beside=None):
    with ExitStack() as c:
        ps = c.enter_context(psum(nc, "mx_ps", [P, 8, BANK], F32))

        def bias_product(i, bank):
            for t in range(4):
                last = nc.tensor.matmul(bank[:, t * P:(t + 1) * P], chunk(weight_t, 4 * i + t, P), bias, start=True,
                                        stop=True)
            return last

        product_pass(nc, ps, 2, bias_product, lambda on_act, i, bank: nc.vector.tensor_tensor(
            t_tm[:, 4 * i:4 * i + 4].rearrange("p t n -> p (t n)"), bank,
            t_tm[:, 4 * i:4 * i + 4].rearrange("p t n -> p (t n)"), ALU.add), by="d")

        n_h = hidden.n
        block, hidden_ready, hidden_off, out_ready, added, loaded, coded = c.enter_context(
            stage(nc, "hidden_ready", "hidden_off", "out_ready", "added", "loaded", "coded"))
        RING = 6

        @block.tensor
        def _(pe):
            for e in range(experts + 1):
                if e < experts:
                    for i in range(n_h):
                        g = e * n_h + i
                        if g >= RING:
                            pe.wait_ge(hidden_off, g - RING + 1)
                        need = hidden.needs(i)
                        if need is not None:
                            pe.wait_ge(hidden_off, e * n_h + need + 1)
                        hidden.product(e, i, ps[:, g % RING]).then_inc(hidden_ready, 1)
                if e >= 1:
                    for u in range(2):
                        o = 2 * (e - 1) + u
                        pe.wait_ge(hidden_off, e * n_h)
                        if o >= 2:
                            pe.wait_ge(added, 4 * (o - 1))
                        for t in range(4):
                            parts = out_parts(e - 1, 4 * u + t)
                            for j, (lhs, rhs) in enumerate(parts):
                                last = nc.tensor.matmul(ps[:, 6 + u, t * P:(t + 1) * P], lhs, rhs, start=(j == 0),
                                                        stop=(j == len(parts) - 1))
                        last.then_inc(out_ready, 1)

        @block.scalar
        def _(act):
            for e in range(experts):
                for i in range(n_h):
                    g = e * n_h + i
                    if i == 0 and e >= 2:
                        act.wait_ge(out_ready, 2 * (e - 1))
                    act.wait_ge(hidden_ready, g + 1)
                    hidden.evacuate(e, i, ps[:, g % RING]).then_inc(hidden_off, 1)

        if beside is not None:
            @block.sync
            def _(sp):
                beside.load(sp, loaded)

        @block.vector
        def _(dve):
            link = linker(dve, coded)
            for e in range(experts):
                if beside is not None:
                    beside.step(dve, link, loaded, e)
                for u in range(2):
                    dve.wait_ge(out_ready, 2 * e + u + 1)
                    for t in range(4):
                        tt = 4 * u + t
                        if e >= 1:
                            dve.wait_ge(added, 8 * (e - 1) + tt + 1)
                        nc.vector.scalar_tensor_tensor(t_tm[:, tt], ps[:, 6 + u, t * P:(t + 1) * P],
                                                       weight[:, tt, e:e + 1], t_tm[:, tt], ALU.mult,
                                                       ALU.add).then_inc(added, 1)


class Hidden:

    def __init__(self, n, needs, product, evacuate):
        self.n, self.needs, self.product, self.evacuate = n, needs, product, evacuate


def batch_normed_mixture(nc, k, b, edge_index):
    with ExitStack() as c:
        t_tm, xc = k.t_tm[:, b], k.xn_cm[:, b]
        h1 = c.enter_context(sbuf(nc, "bm_h1", [P, N], F32))
        h2 = c.enter_context(sbuf(nc, "bm_h2", [P, 2, N], F32))

        def product(e, i, bank):
            if i < 2:
                return nc.tensor.matmul(bank, k.m1[:, e], chunk(xc, i), start=True, stop=True)
            return nc.tensor.matmul(bank, k.m2[:, e], chunk(h1, i % 2), start=True, stop=True)

        def evacuate(e, i, bank):
            out = chunk(h1, i) if i < 2 else h2[:, e % 2, (i % 2) * BANK:(i % 2 + 1) * BANK]
            j = i // 2
            return nc.scalar.activation(out, bank, ACT.Relu, bias=k.bn[:, j, 1, e:e + 1], scale=k.bn[:, j, 0, e:e + 1])

        hidden = Hidden(4, lambda i: None if i < 2 else i - 2, product, evacuate)
        mixture(nc, k, xc, t_tm, k.mix, k.mix_t, E1, k.mo_b[:], hidden,
                lambda e, t: [(h2[:, e % 2, t * P:(t + 1) * P], k.mo[:, e])],
                beside=EdgeCoding(nc, k, c, edge_index, b))


def two_attentions(nc, k, b, pads):
    with ExitStack() as c:
        def sb(name, shape):
            return c.enter_context(sbuf(nc, name, shape, F32))

        t_tm, xn, xc = k.t_tm[:, b], sb("l3_xn", [P, NT, P]), sb("l3_xc", [P, N])
        both = sb("l3_both", [P, 2, N])
        with psum(nc, "l3_ps", [P, 8, BANK], F32) as ps:
            layer_norm(nc, k, t_tm, xn[:], ps=ps, turned=xc)
        def local_part():
            with ExitStack() as c2:
                q = c2.enter_context(sbuf(nc, "l3_q", [P, N], F32))
                with ExitStack() as c3:
                    ps = c3.enter_context(psum(nc, "l3_ps", [P, 8, BANK], F32))
                    def evacuate(on_act, i, bank):
                        j = i // 2
                        if j == 0:
                            return affine(nc, on_act, chunk(q, i), bank, 32 ** -0.5, k.qb[:, 3:4])
                        out = pads[:, j - 1, 2 + (i % 2) * BANK:2 + (i % 2 + 1) * BANK]
                        return affine(nc, on_act, out, bank, 1.0, k.cols[:, C_T_IN + j:C_T_IN + j + 1])

                    product_pass(nc, ps, 6, lambda i, bank: nc.tensor.matmul(
                        bank, k.turned[:, k.t_t_in + i // 2, :], chunk(xc, i % 2), start=True, stop=True), evacuate)
                load_stacks(nc, k, 16)

                def window(j):
                    return lambda s, n: pads[:, j, s + n * BANK:s + (n + 1) * BANK]

                local_attention(nc, k, 5, 4, lambda n: chunk(q, n), window(0), window(1), k.place32, k.spread32,
                                k.turned[:, k.t_t_out, :],
                                lambda n, acc: nc.vector.tensor_scalar(chunk(both[:, 1], n), acc,
                                                                       k.cols[:, C_T_OUT:C_T_OUT + 1], None, ALU.add),
                                mask=k.window_mask)

        with ExitStack() as c2:
            o_cm = both[:, 0]
            parts = c2.enter_context(sbuf(nc, "l3_parts", [P, 2, 3, N], BF16))
            with ExitStack() as c3:
                qk = c3.enter_context(sbuf(nc, "l3_qk", [P, 2, N], F32))
                ps = c3.enter_context(psum(nc, "l3_ps", [P, 8, BANK], F32))
                dense_operands(nc, k, ps, 16, xc, qk, parts, [k.turned[:, k.t_g_in + i, :] for i in range(3)],
                               [(16 ** -0.5, k.qb[:, 1:2]), (1.0, k.cols[:, C_G_IN + 1:C_G_IN + 2])])
            local_part()
            dense_attention(nc, k, 16, o_cm, k.cols[:, C_G_IN + 2:C_G_IN + 3], k.turned[:, k.t_g_out, :],
                            lambda n, bank: affine(nc, False, chunk(both[:, 0], n), bank, 1.0,
                                                   k.cols[:, C_G_OUT:C_G_OUT + 1]))
        ps = c.enter_context(psum(nc, "l3_ps", [P, 8, BANK], F32))
        hid = sb("l3_hid", [P, 2, N])
        x2 = sb("l3_x2", [P, NT, P])

        def two_layers(inputs, w1, bias1, w2, bias_row, residual):
            def product(i, bank):
                for j, x in enumerate(inputs):
                    last = nc.tensor.matmul(bank, k.turned[:, w1(i // 2, j), :], chunk(x, i % 2), start=(j == 0),
                                            stop=(j == len(inputs) - 1))
                return last

            def evacuate(on_act, i, bank):
                return nc.scalar.activation(chunk(hid[:, i // 2], i % 2), bank, ACT.Silu,
                                            bias=k.cols[:, bias1 + i // 2:bias1 + i // 2 + 1])

            product_pass(nc, ps, 4, product, evacuate, by="a")

            def out_product(i, bank):
                for t in range(4):
                    o_ = bank[:, t * P:(t + 1) * P]
                    for j in range(2):
                        nc.tensor.matmul(o_, chunk(hid[:, j], 4 * i + t, P), k.turned[:, w2 + j, :], start=(j == 0),
                                         stop=False)
                    last = nc.tensor.matmul(o_, k.ones_row[:], k.rows[0:1, bias_row, :], start=False, stop=True)
                return last

            product_pass(nc, ps, 2, out_product, lambda on_act, i, bank: nc.vector.tensor_tensor(
                residual[:, 4 * i:4 * i + 4].rearrange("p t n -> p (t n)"), bank,
                residual[:, 4 * i:4 * i + 4].rearrange("p t n -> p (t n)"), ALU.add), by="d")

        two_layers([both[:, 0], both[:, 1]], lambda half, j: k.t_fus1 + 2 * half + j, C_FUS1, k.t_fus2, 2, xn)
        layer_norm(nc, k, xn, x2[:], k.wide[:, 0], k.wide[:, 1], ps=ps, turned=xc)
        two_layers([xc], lambda half, j: k.t_ffn1 + half, C_FFN1, k.t_ffn2, 3, x2)
        layer_norm(nc, k, x2, xn[:], k.wide[:, 2], k.wide[:, 3])
        with stage(nc, "added") as (block, added):
            @block.vector
            def _(dve):
                nc.vector.tensor_tensor(t_tm, t_tm, xn[:], ALU.add).then_inc(added, 1)
        layer_norm(nc, k, t_tm, xn[:], ps=ps, turned=xc)
        h = sb("l3_h", [P, NT, GH * GE])

        def gat_product(i, bank):
            for t in range(NT):
                last = nc.tensor.matmul(bank[:, 16 * t:16 * t + 16], chunk(xc, t, P), k.w_gat[:], start=True, stop=True)
            return last

        product_pass(nc, ps, 1, gat_product, lambda on_act, i, bank: affine(
            nc, on_act, h[:].rearrange("p t f -> p (t f)"), bank[:, 0:NT * 16]))
        copy_blocks(nc, [(k.xn_cm[:, b], xc[:]), (k.h_tm[:, b], h[:])])


def gelu_mixture(nc, k, b, out):
    with ExitStack() as c:
        t_tm = c.enter_context(sbuf(nc, "gm_t", [P, NT, P], F32))
        xc = k.xn_cm[:, b]
        hid = c.enter_context(sbuf(nc, "gm_h", [P, 2, 2, N], F32))
        gates = c.enter_context(sbuf(nc, "gm_g", [P, NT, E2], F32))
        gates_t = c.enter_context(sbuf(nc, "gm_gt", [E2, N], F32))
        copy_blocks(nc, [(t_tm[:], k.t_tm[:, b]), (gates[:], k.gates[:, b])])
        with ExitStack() as c2:
            ps = c2.enter_context(psum(nc, "gm_ps", [P, 8, BANK], F32))
            turn_tiles(nc, ps, k.ident, [([gates[:, t] for t in range(u, u + 4)],
                                          gates_t[:, u * P:(u + 4) * P].rearrange("p (k n) -> p k n", n=P)) for u in (0, 4)])

        def product(e, i, bank):
            half, n = divmod(i, 2)
            return nc.tensor.matmul(bank, k.x1[:, e, half * P:(half + 1) * P], chunk(xc, n), start=True, stop=True)

        def evacuate(e, i, bank):
            half, n = divmod(i, 2)
            return nc.scalar.activation(chunk(hid[:, e % 2, half], n), bank, ACT.Gelu,
                                        bias=k.cols[:, C_B1 + 2 * e + half:C_B1 + 2 * e + half + 1])

        hidden = Hidden(4, lambda i: None, product, evacuate)
        mixture(nc, k, xc, t_tm, gates, gates_t, E2, k.x2_b[:], hidden,
                lambda e, t: [(hid[:, e % 2, s, t * P:(t + 1) * P], k.x2[:, e, s]) for s in range(2)])
        with ExitStack() as c2:
            ps = c2.enter_context(psum(nc, "gm_ps2", [P, 8, BANK], F32))
            turn_image(nc, k, ps, t_tm, xc)
        with stage(nc) as (block,):
            @block.sync
            def _(sp):
                sp.dma_start(out[b].rearrange("c h w -> c (h w)"), xc).then_inc(k.stored, 16)



ROUNDS = 12
LIST = 8 * ROUNDS
FOLD = 512
REST = 1
BANDS = 4
BAND = MT // BANDS
SLOTS = 32
FEAT = GH + GH * GE
PIECE = EW // B
SUB = 128
SMALL = 16
CLASSES = 8


class EdgeCoding:

    def __init__(self, nc, k, c, edge_index, i):
        self.nc = nc
        self.ends = edge_index.rearrange("s (p n) -> s p n", p=P)[:, :, bass.ds(i * PIECE, PIECE)]
        self.out = k.edges[:, bass.ds(i * PIECE, PIECE)]
        self.raw = c.enter_context(sbuf(nc, "ce_raw", [P, 2, PIECE], I32))
        self.a = c.enter_context(sbuf(nc, "ce_a", [P, 2, PIECE], I32))
        self.f = c.enter_context(sbuf(nc, "ce_f", [P, 3, PIECE], F32))

    def load(self, sp, loaded):
        for s in range(2):
            sp.dma_start(self.raw[:, s], self.ends[s]).then_inc(loaded, 16)

    def step(self, dve, link, loaded, step):
        nc, a, f, src, dst = self.nc, self.a, self.f, self.raw[:, 0], self.raw[:, 1]
        if step == 0:
            dve.wait_ge(loaded, 32)
            link(nc.vector.tensor_scalar(a[:, 0], dst, P - 1, 17, ALU.bitwise_and, ALU.logical_shift_left))
            link(nc.vector.tensor_scalar(a[:, 1], dst, 7, 12, ALU.logical_shift_right, ALU.logical_shift_left))
        elif step == 1:
            link(nc.vector.tensor_tensor(a[:, 0], a[:, 0], a[:, 1], ALU.bitwise_or))
            link(nc.vector.tensor_scalar(a[:, 1], src, float(M - 1), None, ALU.min))
        elif step == 2:
            link(nc.vector.scalar_tensor_tensor(f[:, 0], a[:, 0], 1.0, a[:, 1], ALU.add, ALU.add))
            link(nc.vector.tensor_scalar(f[:, 1], dst, float(M), None, ALU.is_lt))
        elif step == 3:
            link(nc.vector.scalar_tensor_tensor(f[:, 2], src, float(M - 1), f[:, 1], ALU.is_lt, ALU.mult))
            link(nc.vector.tensor_tensor(f[:, 0], f[:, 0], f[:, 2], ALU.mult))
        elif step == 4:
            link(nc.vector.tensor_tensor(f[:, 1], f[:, 1], f[:, 2], ALU.subtract))
            link(nc.vector.scalar_tensor_tensor(f[:, 1], dst, 1.0, f[:, 1], ALU.add, ALU.mult))
        elif step == 5:
            link(nc.vector.tensor_tensor(self.out, f[:, 0], f[:, 1], ALU.subtract))


def part_edges(nc, k, e):
    with stage(nc, "parted") as (block, parted):
        @block.vector
        def _(dve):
            nc.vector.tensor_scalar(e.last[:], k.edges[:], -1.0, 0.0, ALU.mult, ALU.max).then_inc(parted, 1)
            dve.wait_ge(parted, 1)
            nc.vector.tensor_scalar(e.codes[:], k.edges[:], 0.0, None, ALU.max).then_inc(parted, 1)


def fold(nc, link, x, t, width):
    cur, other = x, t
    n = x.shape[1] // 2
    while n >= width:
        low, high = cur[:, 0:n], cur[:, n:2 * n]
        link(nc.vector.tensor_tensor(other[:, 0:n], low, high, ALU.max))
        link(nc.vector.tensor_tensor(x[:, n:2 * n], low, high, ALU.min))
        cur, other = other, cur
        n //= 2
    if cur is x:
        link(nc.vector.tensor_copy(t[:, 0:width], x[:, 0:width]))
    link(nc.vector.memset(x[:, 0:width], 0.0))


def count_last(nc, k, e):
    with ExitStack() as c:
        hot = c.enter_context(sbuf(nc, "cl_hot", [P, 2, 2, 2, 64, SUB // 2], BF16))
        total = c.enter_context(sbuf(nc, "cl_total", [P, P], F32))
        corner = c.enter_context(sbuf(nc, "cl_corner", [P, 64], F32))
        place = c.enter_context(sbuf(nc, "cl_place", [P, 2, P], F32))
        ps = c.enter_context(psum(nc, "cl_ps", [P, BANK], F32))
        ps2 = c.enter_context(psum(nc, "cl_ps2", [P, BANK], F32))
        with stage(nc, "made") as (block, made):
            @block.gpsimd
            def _(pool):
                link = linker(pool, made)
                link(nc.gpsimd.memset(total[:], 0.0))
                link(nc.gpsimd.memset(place[:], 0.0))
                for odd in range(2):
                    for half in range(2):
                        v = place[:, odd, :]
                        link(nc.gpsimd.affine_select(out=v, in_=v, compare_op=ALU.not_equal, fill=1.0,
                                                     base=64 * (odd - half), pattern=[[-1, P]], channel_multiplier=1))
                    v = place[:, odd, 64 * (1 - odd):64 * (2 - odd)]
                    link(nc.gpsimd.memset(v, 0.0))
        columns = c.enter_context(sbuf(nc, "cl_columns", [P, EW // 2], F32))
        whole = c.enter_context(sbuf(nc, "cl_whole", [P, 2, FOLD], I32))
        digits = c.enter_context(sbuf(nc, "cl_digits", [P, 2, FOLD], BF16))

        def count_fold(width):
            count(width, lambda link: fold(nc, link, e.last[:], columns[:], width))

        def count(width, fill):
            size = min(width, SUB)
            steps = width // size
            with stage(nc, "chained", "hot_ready", "multiplied", "added") as (block, chained, hot_ready, multiplied,
                                                                               added):
                @block.vector
                def _(dve):
                    link = linker(dve, chained)
                    fill(link)
                    low, high = whole[:, 0, 0:width], whole[:, 1, 0:width]
                    link(nc.vector.tensor_scalar(low, columns[:, 0:width], -1.0, None, ALU.add))
                    link(nc.vector.tensor_scalar(high, low, 6, None, ALU.logical_shift_right))
                    link(nc.vector.tensor_scalar(low, low, 63, None, ALU.bitwise_and))
                    link(nc.vector.tensor_copy(digits[:, :, 0:width], whole[:, :, 0:width]))
                    for s in range(steps):
                        if s >= 2:
                            dve.wait_ge(multiplied, s - 1)
                        here = digits[:, :, s * size:(s + 1) * size].rearrange("p d (a m) -> p d a m", a=2)
                        for v in range(64):
                            nc.vector.tensor_scalar(hot[:, s % 2, :, :, v, 0:size // 2], here, float(v), None,
                                                    ALU.is_equal).then_inc(hot_ready, 1)
                    dve.wait_ge(multiplied, steps)
                    nc.vector.tensor_tensor(total[:], total[:], ps[:, 0:P], ALU.add).then_inc(added, 1)

                @block.tensor
                def _(pe):
                    for s in range(steps):
                        pe.wait_ge(hot_ready, 64 * (s + 1))
                        for m in range(size // 2):
                            low, high = (hot[:, s % 2, d, :, :, m].rearrange("p a v -> p (a v)") for d in range(2))
                            last = nc.tensor.matmul(ps[:, 0:P], low, high, start=(s == 0 and m == 0),
                                                    stop=(s == steps - 1 and m == size // 2 - 1))
                        last.then_inc(multiplied, 1)

        count_fold(FOLD)
        count_fold(FOLD // 2)
        count_fold(SUB)

        def left(link):
            for half in range(2):
                count_above(nc, link, e.last[:, half * EW // 2:(half + 1) * EW // 2], 0.5, columns[:],
                            e.most[:, 4 + half:5 + half])
            link(nc.vector.tensor_tensor(e.most[:, 0:1], e.most[:, 4:5], e.most[:, 5:6], ALU.add))

        most = largest(nc, e, left)
        with loop(nc, 0, most, SMALL):
            count(SMALL, lambda link: take_largest(nc, link, e.last[:], columns[:, 0:SMALL], SMALL // 8))
        with stage(nc, "folded", "placed", "copied") as (block, folded, placed, copied):
            @block.tensor
            def _(pe):
                pe.wait_ge(folded, 2)
                for odd in range(2):
                    rhs = corner[:].rearrange("p (t o) -> p o t", o=2)[:, odd, :]
                    last = nc.tensor.matmul(ps2[:, 0:MT], place[:, odd, :], rhs, start=(odd == 0), stop=(odd == 1))
                last.then_inc(placed, 1)

            @block.vector
            def _(dve):
                for half in range(2):
                    r = slice(64 * half, 64 * half + 64)
                    nc.vector.tensor_copy(corner[r, :], total[r, 64 * half:64 * half + 64]).then_inc(folded, 1)
                dve.wait_ge(placed, 1)
                nc.vector.tensor_copy(e.count[:], ps2[:, 0:MT]).then_inc(copied, 1)


def largest(nc, e, measure):
    with stage(nc, "chained", "measured", "reduced", "whole") as (block, chained, measured, reduced, whole):
        @block.vector
        def _(dve):
            measure(linker(dve, chained))
            nc.vector.tensor_copy(e.most[:, 2:3], e.most[:, 0:1]).then_inc(measured, 1)
            dve.wait_ge(reduced, 1)
            nc.vector.tensor_copy(e.most_int[:], e.most[:, 1:2]).then_inc(whole, 1)

        @block.gpsimd
        def _(pool):
            pool.wait_ge(measured, 1)
            nc.gpsimd.partition_all_reduce(e.most[:, 1:2], e.most[:, 2:3], P,
                                           bass.bass_isa.ReduceOp.max).then_inc(reduced, 1)
    value = nc.values_load(e.most_int[0:1, 0:1], min_val=0, max_val=EDGES)
    nc.all_engine_barrier(sem_only=True)
    return value


def count_above(nc, link, candidates, low, scratch, out):
    link(nc.vector.tensor_scalar(scratch, candidates, low, None, ALU.is_gt, ALU.add, accum_out=out))


def take_largest(nc, link, candidates, out, rounds):
    for r in range(rounds):
        o_ = out[:, 8 * r:8 * r + 8]
        link(nc.vector.max(o_, candidates))
        link(nc.vector.match_replace(candidates, o_, candidates, 0.0))


def gather_lists(nc, e, take, lists, candidates, high, spread):
    with stage(nc, "chained", "stored", "loaded") as (block, chained, stored, loaded):
        @block.vector
        def _(dve):
            link = linker(dve, chained)
            take(link)
            dve.wait_ge(loaded, 16 * CLASSES)
            link(nc.vector.scalar_tensor_tensor(candidates, candidates, high, candidates, ALU.is_le, ALU.mult))

        @block.sync
        def _(sp):
            sp.wait_ge(chained, 2 * ROUNDS)
            sp.dma_start(lists, e.list[:]).then_inc(stored, 16)
            sp.wait_ge(stored, 16)
            for c in range(CLASSES):
                sp.dma_start(candidates[16 * c:16 * c + 16, :], spread(lists, c)).then_inc(loaded, 16)


def sort_into_bands(nc, e, candidates):
    with ExitStack() as c:
        found = c.enter_context(sbuf(nc, "sb_found", [P, LIST], F32))
        scratch = c.enter_context(sbuf(nc, "sb_scratch", [P, LIST], F32))

        def measure(link):
            take_largest(nc, link, candidates, found, ROUNDS)
            for g in range(BANDS):
                low, high, o_ = e.band_low[:, g:g + 1], e.band_low[:, g + 1:g + 2], e.banded[:, g]
                link(nc.vector.scalar_tensor_tensor(o_, found[:], low, found[:], ALU.is_gt, ALU.mult))
                link(nc.vector.scalar_tensor_tensor(o_, o_, high, o_, ALU.is_le, ALU.mult))
                count_above(nc, link, o_, 0.5, scratch[:], e.most[:, 4 + g:5 + g])
            link(nc.vector.tensor_reduce(e.most[:, 0:1], e.most[:, 4:4 + BANDS], AX.X, ALU.max))

        return largest(nc, e, measure)


def take_in(nc, k, e):
    with ExitStack() as c:
        def sb(name, shape, dt=F32):
            return c.enter_context(sbuf(nc, name, shape, dt))

        ALL = BANDS * SLOTS
        code, f = sb("ti_code", [P, ALL]), sb("ti_f", [P, 3, ALL])
        whole = sb("ti_int", [P, 3, ALL], I32)
        row = sb("ti_row", [P, ALL, FEAT])
        hot = sb("ti_hot", [P, BAND, SLOTS])
        z, p, y = (sb(f"ti_{n}", [P, GH, BAND, SLOTS]) for n in "zpy")
        n = sb("ti_new", [P, 5, GH, BAND])
        block, chained, indexed, shifted, exped, *gathered = c.enter_context(stage(
            nc, "chained", "indexed", "shifted", "exped", *(f"gathered_{g}" for g in range(BANDS)), pool_dma=True))

        def take_in_band(dve, link, g, tile, row):
            tiles = slice(g * BAND, (g + 1) * BAND)
            wide = [P, BAND, SLOTS]
            link(nc.vector.tensor_tensor(hot[:], e.tiles[:, tiles].unsqueeze(2).broadcast_to(wide),
                                         tile.unsqueeze(1).broadcast_to(wide), ALU.is_equal))
            link(nc.vector.tensor_scalar(hot[:], hot[:], -NEG, NEG, ALU.mult, ALU.add))
            top, shift, a_dst = (x[:, :, tiles] for x in (e.top, e.shift, e.a_dst))
            best, change, total, part, own = (n[:, i] for i in range(5))
            link(nc.vector.tensor_copy(own, a_dst))
            dve.wait_ge(gathered[g], 16 * SLOTS)

            def of_rows(i):
                return row[:, :, i].unsqueeze(1).broadcast_to(wide)

            def flat(x):
                return x.rearrange("p h t -> p (h t)")

            def over_slots(x):
                return flat(x).unsqueeze(2).broadcast_to([P, GH * BAND, SLOTS])

            for h in range(GH):
                link(nc.vector.tensor_tensor(z[:, h], hot[:], of_rows(h), ALU.add))
            z3, p3, y3 = (x[:].rearrange("p h t j -> p (h t) j") for x in (z, p, y))
            link(nc.vector.tensor_reduce(flat(best), z3, AX.X, ALU.max))
            link(nc.vector.tensor_tensor(top, top, best, ALU.max))
            link(nc.vector.tensor_tensor(best, top, own, ALU.add))
            link(nc.vector.scalar_tensor_tensor(best, best, 0.2, best, ALU.mult, ALU.max))
            link(nc.vector.tensor_tensor(change, shift, best, ALU.subtract))
            link(nc.vector.tensor_copy(shift, best))
            link(nc.vector.tensor_tensor(z3, z3, over_slots(own), ALU.add))
            link(nc.vector.scalar_tensor_tensor(z3, z3, 0.2, z3, ALU.mult, ALU.max))
            nc.vector.tensor_tensor(z3, z3, over_slots(best), ALU.subtract).then_inc(shifted, 1)
            dve.wait_ge(exped, 2 * (g + 1))
            link(nc.vector.tensor_reduce(flat(total), p3, AX.X, ALU.add))
            link(nc.vector.tensor_tensor(e.den[:, :, tiles], e.den[:, :, tiles], change, ALU.mult))
            link(nc.vector.tensor_tensor(e.den[:, :, tiles], e.den[:, :, tiles], total, ALU.add))
            for v in range(GE):
                num = e.num[:, v][:, :, tiles]
                for h in range(GH):
                    link(nc.vector.tensor_tensor(y[:, h], p[:, h], of_rows(GH + h * GE + v), ALU.mult))
                link(nc.vector.tensor_reduce(flat(part), y3, AX.X, ALU.add))
                link(nc.vector.tensor_tensor(num, num, change, ALU.mult))
                link(nc.vector.tensor_tensor(num, num, part, ALU.add))

        @block.vector
        def _(dve):
            link = linker(dve, chained)
            valid, local, tile = (f[:, i] for i in range(3))
            for g in range(BANDS):
                band = slice(g * SLOTS, (g + 1) * SLOTS)
                take_largest(nc, link, e.banded[:, g], code[:, band], SLOTS // 8)
                link(nc.vector.tensor_scalar(valid[:, band], code[:, band], e.bounds[:, 2:3], None, ALU.is_gt))
                link(nc.vector.tensor_scalar(local[:, band], code[:, band], e.bounds[:, 2:3], -1.0, ALU.subtract,
                                             ALU.add))
                link(nc.vector.tensor_tensor(local[:, band], local[:, band], valid[:, band], ALU.mult))
                link(nc.vector.tensor_copy(whole[:, 0, band], local[:, band]))
                nc.vector.tensor_scalar(whole[:, 1, band], whole[:, 0, band], M - 1, None,
                                        ALU.bitwise_and).then_inc(indexed, 1)
            link(nc.vector.tensor_scalar(whole[:, 2], whole[:, 0], 12, None, ALU.logical_shift_right))
            link(nc.vector.tensor_copy(tile, whole[:, 2]))
            link(nc.vector.scalar_tensor_tensor(tile, tile, 1.0, valid, ALU.add, ALU.mult))
            for g in range(BANDS):
                take_in_band(dve, link, g, tile[:, g * SLOTS:(g + 1) * SLOTS], row[:, g * SLOTS:(g + 1) * SLOTS])

        @block.gpsimd
        def _(pool):
            for g in range(BANDS):
                pool.wait_ge(indexed, g + 1)
                for j in range(g * SLOTS, (g + 1) * SLOTS):
                    nc.gpsimd.indirect_dma_start(row[:, j, :], None, e.features, bass.IndirectOffsetOnAxis(
                        ap=whole[:, 1, j:j + 1], axis=0)).then_inc(gathered[g], 16)
            for g in range(BANDS):
                pool.wait_ge(gathered[g], 16 * SLOTS)

        @block.scalar
        def _(act):
            for g in range(BANDS):
                act.wait_ge(shifted, g + 1)
                nc.scalar.activation(n[:, 1], n[:, 1], ACT.Exp).then_inc(exped, 1)
                nc.scalar.activation(p[:], z[:], ACT.Exp).then_inc(exped, 1)


def start_sums(nc, k, e):
    with ExitStack() as c:
        def sb(name, shape, dt=F32):
            return c.enter_context(sbuf(nc, name, shape, dt))

        prod = sb("ss_prod", [P, MT, GH * GE])
        rows = sb("ss_rows", [P, MT, FEAT])
        last_row = sb("ss_last", [P, FEAT])
        n = sb("ss_n", [P, 4, GH, MT])
        block, chained, stored, loaded, exped = c.enter_context(stage(nc, "chained", "stored", "loaded", "exped"))
        h3 = k.h_tm[:].rearrange("p b t f -> p (b t) f")
        own, last, e_own, e_last = (n[:, i] for i in range(4))

        @block.vector
        def _(dve):
            link = linker(dve, chained)
            for i in range(2):
                link(nc.vector.tensor_tensor(prod[:], h3, k.gat[:, 3 + i].unsqueeze(1).broadcast_to([P, MT, GH * GE]),
                                             ALU.mult))
                out = (own if i == 0 else e.a_dst[:]).rearrange("p h t -> p t h")
                link(nc.vector.tensor_reduce(out, prod[:].rearrange("p t (h v) -> p t h v", v=GE), AX.X, ALU.add))
            link(nc.vector.tensor_copy(rows[:, :, 0:GH], own.rearrange("p h t -> p t h")))
            link(nc.vector.tensor_copy(rows[:, :, GH:FEAT], h3))
            dve.wait_ge(loaded, 16)
            link(nc.vector.tensor_scalar(last[:, 0], e.count[:], 0.5, NEG, ALU.is_lt, ALU.mult))
            for h in range(GH - 1, -1, -1):
                link(nc.vector.tensor_scalar(last[:, h], last[:, 0], last_row[:, h:h + 1], None, ALU.add))
            link(nc.vector.tensor_tensor(e.top[:], own, last, ALU.max))
            for x, out in ((own, e_own), (last, e_last), (e.top[:], e.shift[:])):
                link(nc.vector.tensor_tensor(out, x, e.a_dst[:], ALU.add))
                link(nc.vector.scalar_tensor_tensor(out, out, 0.2, out, ALU.mult, ALU.max))
            for x in (e_own, e_last):
                link(nc.vector.tensor_tensor(x, x, e.shift[:], ALU.subtract))
            dve.wait_ge(exped, 1)
            link(nc.vector.tensor_tensor(e_last, e_last, e.count[:].unsqueeze(1).broadcast_to([P, GH, MT]), ALU.mult))
            link(nc.vector.tensor_tensor(e.den[:], e_own, e_last, ALU.add))
            for v in range(GE):
                value = h3.rearrange("p t (h v) -> p v h t", v=GE)[:, v]
                link(nc.vector.tensor_tensor(e.num[:, v], e_own, value, ALU.mult))
                for h in range(GH):
                    link(nc.vector.scalar_tensor_tensor(e.num[:, v, h], e_last[:, h],
                                                        last_row[:, GH + h * GE + v:GH + h * GE + v + 1],
                                                        e.num[:, v, h], ALU.mult, ALU.add))

        @block.sync
        def _(sp):
            sp.wait_ge(chained, 6)
            sp.dma_start(e.features.rearrange("(t p) f -> p t f", p=P), rows[:]).then_inc(stored, 16)
            sp.wait_ge(stored, 16)
            sp.dma_start(last_row[:], e.features[M - 1].partition_broadcast(P)).then_inc(loaded, 16)

        @block.scalar
        def _(act):
            act.wait_ge(chained, 6 + 1 + GH + 1 + 6 + 2)
            nc.scalar.activation(n[:, 2:4], n[:, 2:4], ACT.Exp).then_inc(exped, 1)


def choose_experts(nc, k, e):
    with ExitStack() as c:
        def sb(name, shape):
            return c.enter_context(sbuf(nc, name, shape, F32))

        agg, sq = sb("ch_agg", [P, MT, GH * GE]), sb("ch_sq", [P, MT, GH * GE])
        st = sb("ch_st", [P, 6, MT])
        s, rank = sb("ch_s", [P, GE, MT]), sb("ch_rank", [P, GE, MT])
        block, chained, rooted, exped, final = c.enter_context(stage(nc, "chained", "rooted", "exped", "final"))

        @block.vector
        def _(dve):
            link = linker(dve, chained)
            link(nc.vector.tensor_scalar(e.den[:], e.den[:], 1e-16, None, ALU.add))
            link(nc.vector.reciprocal(e.den[:], e.den[:]))
            for v in range(GE):
                out = agg[:].rearrange("p t (h v) -> p v h t", v=GE)[:, v]
                link(nc.vector.tensor_tensor(out, e.num[:, v], e.den[:], ALU.mult))

            def param(i):
                return k.gat[:, i].unsqueeze(1).broadcast_to([P, MT, GH * GE])

            def wide(a):
                return a.unsqueeze(2).broadcast_to([P, MT, GH * GE])

            link(nc.vector.tensor_tensor(agg[:], agg[:], param(0), ALU.add))
            link(nc.vector.tensor_reduce(st[:, 0], agg[:], AX.X, ALU.add))
            link(nc.vector.tensor_scalar(st[:, 0], st[:, 0], 1.0 / 16, None, ALU.mult))
            link(nc.vector.tensor_tensor(agg[:], agg[:], wide(st[:, 0]), ALU.subtract))
            link(nc.vector.tensor_tensor(sq[:], agg[:], agg[:], ALU.mult))
            link(nc.vector.tensor_reduce(st[:, 1], sq[:], AX.X, ALU.add))
            dve.wait_ge(rooted, 1)
            link(nc.vector.reciprocal(st[:, 1], st[:, 1]))
            link(nc.vector.tensor_tensor(agg[:], agg[:], wide(st[:, 1]), ALU.mult))
            link(nc.vector.tensor_tensor(agg[:], agg[:], param(1), ALU.mult))
            link(nc.vector.tensor_tensor(agg[:], agg[:], param(2), ALU.add))
            link(nc.vector.tensor_reduce(s[:].rearrange("p v t -> p t v"), agg[:].rearrange("p t (h v) -> p t v h", v=GE),
                                         AX.X, ALU.add))
            link(nc.vector.tensor_scalar(s[:], s[:], 1.0 / GH, None, ALU.mult))
            for i in range(GE):
                link(nc.vector.memset(rank[:, i], float(GE - 1 - i)))
            for i in range(GE):
                for j in range(i + 1, GE):
                    link(nc.vector.tensor_tensor(st[:, 2], s[:, i], s[:, j], ALU.is_ge))
                    link(nc.vector.tensor_tensor(rank[:, j], rank[:, j], st[:, 2], ALU.add))
                    link(nc.vector.tensor_tensor(rank[:, i], rank[:, i], st[:, 2], ALU.subtract))
            link(nc.vector.tensor_scalar(rank[:], rank[:], 1.5, None, ALU.is_lt))
            link(nc.vector.tensor_reduce(st[:, 3], s[:].rearrange("p v t -> p t v"), AX.X, ALU.max))
            nc.vector.tensor_tensor(s[:], s[:], st[:, 3].unsqueeze(1).broadcast_to([P, GE, MT]), ALU.subtract).then_inc(final, 1)
            dve.wait_ge(exped, 1)
            link(nc.vector.tensor_tensor(s[:], s[:], rank[:], ALU.mult))
            link(nc.vector.tensor_reduce(st[:, 4], s[:].rearrange("p v t -> p t v"), AX.X, ALU.add))
            link(nc.vector.reciprocal(st[:, 4], st[:, 4]))
            link(nc.vector.tensor_tensor(k.gates[:].rearrange("p b t v -> p v (b t)"), s[:],
                                         st[:, 4].unsqueeze(1).broadcast_to([P, GE, MT]), ALU.mult))

        @block.scalar
        def _(act):
            act.wait_ge(chained, 2 + GE + 6)
            nc.scalar.activation(st[:, 1], st[:, 1], ACT.Sqrt, bias=k.eps[:, 0:1], scale=1.0 / 16).then_inc(rooted, 1)
            act.wait_ge(final, 1)
            nc.scalar.activation(s[:], s[:], ACT.Exp).then_inc(exped, 1)


class Edges:
    pass


def route(nc, k):
    with ExitStack() as c:
        def sb(name, shape, dt=F32):
            return c.enter_context(sbuf(nc, name, shape, dt))

        e = Edges()
        e.codes = k.edges
        e.count = sb("count", [P, MT])
        e.list = sb("list", [P, LIST])
        e.most, e.most_int = sb("most", [P, 8]), sb("most_int", [P, 1], I32)
        e.bounds = sb("bounds", [P, 4])
        bounds_int = sb("bounds_int", [P, 2], I32)
        e.tiles = sb("tiles", [P, MT])
        e.features = nc.dram_tensor("features", [M, FEAT], F32).ap()
        lists = [nc.dram_tensor(f"lists_{i}", [P, LIST], F32).ap() for i in range(2)]
        with ExitStack() as c2:
            e.last = c2.enter_context(sbuf(nc, "last", [P, EW], F32))
            part_edges(nc, k, e)
            count_last(nc, k, e)
        e.top, e.shift, e.den, e.a_dst = (sb(f"gat_{n}", [P, GH, MT]) for n in ("top", "shift", "den", "a_dst"))
        e.num = sb("gat_num", [P, GE, GH, MT])
        by_class = sb("by_class", [P, CLASSES * LIST])
        by_owner = sb("by_owner", [P, 16 * LIST])
        folded = sb("folded", [P, EW // 2])
        halves = sb("halves", [P, EW // 2])
        scratch = sb("count_scratch", [P, EW])
        e.band_low = sb("band_low", [P, BANDS + 1])
        e.banded = sb("banded", [P, BANDS, LIST])

        with stage(nc, "made", "chained") as (block, made, chained):
            @block.gpsimd
            def _(pool):
                nc.gpsimd.iota(bounds_int[:, 0:1], [[0, 1]], base=0, channel_multiplier=1 << 17).then_inc(made, 1)
                nc.gpsimd.iota(e.tiles[:], [[1, MT]], base=1, channel_multiplier=0,
                               allow_small_or_imprecise_dtypes=True).then_inc(made, 1)

            @block.vector
            def _(dve):
                link = linker(dve, chained)
                dve.wait_ge(made, 2)
                link(nc.vector.tensor_copy(e.bounds[:, 2:3], bounds_int[:, 0:1]))
                link(nc.vector.tensor_scalar(e.bounds[:, 3:4], e.bounds[:, 2:3], float(1 << 17), None, ALU.add))
                for g in range(BANDS + 1):
                    link(nc.vector.tensor_scalar(e.band_low[:, g:g + 1], e.bounds[:, 2:3], float(g * BAND << 12), None,
                                                 ALU.add))
                link(nc.vector.tensor_scalar(bounds_int[:, 1:2], bounds_int[:, 0:1], 21, 21, ALU.logical_shift_right,
                                             ALU.logical_shift_left))
                link(nc.vector.tensor_copy(e.bounds[:, 0:1], bounds_int[:, 1:2]))
                link(nc.vector.tensor_scalar(e.bounds[:, 1:2], e.bounds[:, 0:1], float(1 << 21), None, ALU.add))

        start_sums(nc, k, e)

        def to_class(lists, c):
            return lists.rearrange("(j q) n -> j (q n)", q=CLASSES)

        def to_owners(lists, c):
            return lists[16 * c:16 * c + 16, :].rearrange("j n -> (j n)").partition_broadcast(16)

        with stage(nc, "chained") as (block, chained):
            @block.vector
            def _(dve):
                link = linker(dve, chained)
                for start, width in ((0, FOLD), (FOLD, FOLD // 2)):
                    fold(nc, link, e.codes[:], halves[:], width)
                    link(nc.vector.tensor_copy(folded[:, start:start + width], halves[:, 0:width]))
        candidates = folded[:, 0:FOLD + FOLD // 2]

        def lists_needed(link):
            count_above(nc, link, candidates, 0.5, scratch[:, 0:candidates.shape[1]], e.most[:, 4:5])
            count_above(nc, link, e.codes[:], 0.5, scratch[:], e.most[:, 5:6])
            link(nc.vector.tensor_scalar(e.most[:, 5:6], e.most[:, 5:6], float((ROUNDS - REST) // REST), None, ALU.mult))
            link(nc.vector.tensor_reduce(e.most[:, 0:1], e.most[:, 4:6], AX.X, ALU.max))

        def take_from_codes(link):
            cut = 8 * (ROUNDS - REST)
            take_largest(nc, link, candidates, e.list[:, 0:cut], ROUNDS - REST)
            take_largest(nc, link, e.codes[:], e.list[:, cut:LIST], REST)

        def take_from(x):
            return lambda link: take_largest(nc, link, x, e.list[:], ROUNDS)

        def above(x, low):
            return lambda link: count_above(nc, link, x, low, scratch[:, 0:x.shape[1]], e.most[:, 0:1])

        most = largest(nc, e, lists_needed)
        with loop(nc, 0, most, 8 * (ROUNDS - REST)):
            gather_lists(nc, e, take_from_codes, lists[0], by_class[:], e.bounds[:, 1:2], to_class)
            most_a = largest(nc, e, above(by_class[:], e.bounds[:, 0:1]))
            with loop(nc, 0, most_a, LIST):
                gather_lists(nc, e, take_from(by_class[:]), lists[1], by_owner[:], e.bounds[:, 3:4], to_owners)
                most_b = largest(nc, e, above(by_owner[:], e.bounds[:, 2:3]))
                with loop(nc, 0, most_b, LIST):
                    most_c = sort_into_bands(nc, e, by_owner[:])
                    with loop(nc, 0, most_c, SLOTS):
                        take_in(nc, k, e)
        choose_experts(nc, k, e)



def wait_for_output(nc, k):
    with stage(nc) as (block,):
        @block.sync
        def _(sp):
            sp.wait_ge(k.stored, 16 * B)


class Kept:
    pass


def build(nc, w, out):
    with ExitStack() as c:
        def sb(name, shape, dt=F32):
            return c.enter_context(sbuf(nc, name, shape, dt))

        k = Kept()
        k.xn_cm = sb("xn_cm", [P, B, N])
        k.x_cm = k.xn_cm
        k.t_tm = sb("t_tm", [P, B, NT, P])
        k.h_tm, k.gates = sb("h_tm", [P, B, NT, GH * GE]), sb("gates", [P, B, NT, E2])
        k.ident, k.mean16, k.mean4, k.block32 = (sb(n, [P, P]) for n in ("ident", "mean16", "mean4", "block32"))
        k.place16, k.place32 = sb("place16", [P, 25 * 8]), sb("place32", [P, 9 * 4])
        k.spread16, k.spread32 = sb("spread16", [120, SPREAD * P], BF16), sb("spread32", [60, SPREAD * P], BF16)
        k.ones_row, k.eps, k.window_mask = sb("ones_row", [1, P]), sb("eps", [P, 2]), sb("window_mask", [P, NT, 5])
        k.turned = sb("turned", [P, 25, P])
        k.t_g_in, k.t_g_out, k.t_t_in, k.t_t_out, k.t_fus1, k.t_fus2, k.t_ffn1, k.t_ffn2, k.t_q2 = (
            5, 8, 9, 12, 13, 17, 19, 21, 23)
        k.cols, k.qb, k.bn = sb("cols", [P, P]), sb("qb", [P, 4]), sb("bn", [P, 2, 2, E1])
        k.ident_b = sb("ident_b", [P, P], BF16)
        k.parts_dram = nc.dram_tensor("parts_dram", [2, 3, P, N], BF16).ap()
        k.stored = c.enter_context(nc.semaphore("stored"))
        k.parted = c.enter_context(nc.semaphore("parted"))
        k.stacked = [c.enter_context(nc.semaphore(f"stacked_{g}")) for g in range(2)]
        k.w_kv, k.w_o2 = sb("w_kv", [P, 4 * P]), sb("w_o2", [P, 2, P])
        k.m1, k.m2, k.mo = (sb(n, [P, E1, P]) for n in ("m1", "m2", "mo"))
        k.mo_b, k.wr, k.mix, k.mix_t = sb("mo_b", [E1, P]), sb("wr", [P, E1]), sb("mix", [P, NT, E1]), sb("mix_t", [E1, N])
        k.w_gat, k.gat = sb("w_gat", [P, GH * GE]), sb("gat", [P, 5, GH * GE])
        k.x1, k.x2, k.x2_b = sb("x1", [P, E2, 2 * P]), sb("x2", [P, E2, 2, P]), sb("x2_b", [E2, P])
        k.rows, k.wide = sb("rows", [1, 4, P]), sb("wide", [P, 4, P])

        load_weights(nc, k, w)
        first_layers(nc, k)
        k.edges = sb("edges", [P, EW])
        with loop(nc, 0, B) as b:
            linear_attention(nc, k, b)
        mixture_weights(nc, k)
        with loop(nc, 0, B) as b:
            batch_normed_mixture(nc, k, b, w["L3_ffn_edge_index"])
        with dense_buffers(nc, k, 16), cleared_buffer(nc, "l3_pads", [P, 2, N + 4]) as pads, loop(nc, 0, B) as b:
            two_attentions(nc, k, b, pads)
        route(nc, k)
        with loop(nc, 0, B) as b:
            gelu_mixture(nc, k, b, out)
        wait_for_output(nc, k)
        LAST_STAGE.close()



NAMES = """x L0_conv_gn_gamma L0_conv_gn_beta L0_conv_qkv_w L0_conv_qkv_b L0_conv_proj_w L0_conv_proj_b L1_conv_w_out
L1_conv_b_out L2_attn_w_qkv L2_attn_w_out L2_attn_b_out L2_ffn_Wr L2_ffn_br L2_ffn_W1 L2_ffn_b1 L2_ffn_g1 L2_ffn_be1
L2_ffn_m1 L2_ffn_v1 L2_ffn_W2 L2_ffn_b2 L2_ffn_g2 L2_ffn_be2 L2_ffn_m2 L2_ffn_v2 L2_ffn_Wo L2_ffn_bo L3_attn_g_in_w
L3_attn_g_in_b L3_attn_g_out_w L3_attn_g_out_b L3_attn_t_in_w L3_attn_t_in_b L3_attn_t_out_w L3_attn_t_out_b
L3_attn_fus_w1 L3_attn_fus_b1 L3_attn_fus_w2 L3_attn_fus_b2 L3_attn_ffn_w1 L3_attn_ffn_b1 L3_attn_ffn_w2
L3_attn_ffn_b2 L3_attn_gn_g L3_attn_gn_b L3_attn_fn_g L3_attn_fn_b L3_ffn_W_gat L3_ffn_att_src L3_ffn_att_dst
L3_ffn_b_gat L3_ffn_ln_gamma L3_ffn_ln_beta L3_ffn_W1 L3_ffn_b1 L3_ffn_W2 L3_ffn_b2 L3_ffn_edge_index""".split()


def kernel(**inputs):
    import numpy as np
    import concourse.bacc as bacc
    from concourse.bass_utils import run_bass_kernel_spmd

    nc = bacc.Bacc("TRN2", target_bir_lowering=False, num_devices=1)
    arrays = {name: np.ascontiguousarray(inputs[name]) for name in NAMES}
    w = {name: nc.dram_tensor(name, a.shape, mybir.dt.from_np(a.dtype), kind="ExternalInput").ap()
         for name, a in arrays.items()}
    out = nc.dram_tensor("out", [B, P, IMG, IMG], F32, kind="ExternalOutput").ap()
    build(nc, w, out)
    return run_bass_kernel_spmd(nc, [arrays], core_ids=[0]).results[0]["out"]
```
